# Optimizing a Trainium2 kernel written in Bass

```python
import numpy as np
import jax
import jax.numpy as jnp

def _softmax(x, axis=-1):
    return jax.nn.softmax(x, axis=axis)

def _gelu(x):
    return jax.nn.gelu(x, approximate=True)

def _silu(x):
    return jax.nn.silu(x)

def _sigmoid(x):
    return jax.nn.sigmoid(x)

def _layernorm(x, axis=-1, eps=1e-05):
    m = jnp.mean(x, axis=axis, keepdims=True)
    v = jnp.var(x, axis=axis, keepdims=True)
    return (x - m) / jnp.sqrt(v + eps)

def _scatter_add(tgt, idx, src, axis=0):
    return tgt.at[idx].add(src)

def _segment_sum(src, seg, n):
    return jax.ops.segment_sum(src, seg, n)
kernel_name = 'mk_perceiver_d1_seqx_r8_b6b185'

def setup_inputs(seed: int=0):
    np.random.seed(seed)
    _w = jnp.asarray

    def _rec_inputs():
        import jax
        import jax.numpy as jnp
        _rk = jax.random.key(seed)
        x = -0.0005146 + 1 * jax.random.normal(jax.random.fold_in(_rk, 1), (16, 32, 512), jnp.float32)
        _lenS = 32 - jax.random.randint(jax.random.fold_in(_rk, 7), (16,), 0, max(1, 32 // 4) + 1, jnp.int32)
        _lenS2 = 512 - jax.random.randint(jax.random.fold_in(_rk, 8), (16,), 0, max(1, 512 // 4) + 1, jnp.int32)
        _ctx_4096P = jax.random.normal(jax.random.fold_in(_rk, 11), (16, 16, 512), jnp.float32)
        _ctx_4096c = jax.random.dirichlet(jax.random.fold_in(_rk, 511), 0.3 * jnp.ones((16,), jnp.float32), (16, 512))
        _ctx_4096t = jnp.einsum('bsk,bkd->bsd', _ctx_4096c, _ctx_4096P)
        _ctx_4096t = _ctx_4096t * jax.lax.rsqrt(jnp.mean(jnp.square(_ctx_4096t)) + 1e-12) * 0.953939
        ctx_4096 = -0.0142356 + 1.00583 * (_ctx_4096t + 0.3 * jax.random.normal(jax.random.fold_in(_rk, 611), (16, 512, 512), jnp.float32))
        return (x, ctx_4096)
    x, ctx_4096 = _rec_inputs()

    def _L0_xattn_setup():
        import jax, jax.numpy as jnp
        import numpy as np
        K = 10
        NUM_BITS = 10
        M_METHODS = 4

        def _quantize(coords, num_bits=NUM_BITS):
            cmin = coords.min(axis=1, keepdims=True)
            cmax = coords.max(axis=1, keepdims=True)
            scale = (2 ** num_bits - 1) / (cmax - cmin + 1e-06)
            q = jnp.floor((coords - cmin) * scale)
            return jnp.clip(q, 0, 2 ** num_bits - 1).astype(jnp.int32)

        def _morton_key(q):
            x, y, z = (q[..., 0], q[..., 1], q[..., 2])
            key = jnp.zeros(x.shape, dtype=jnp.int32)
            for b in range(NUM_BITS):
                key = key | (x >> b & 1) << 3 * b + 2 | (y >> b & 1) << 3 * b + 1 | (z >> b & 1) << 3 * b
            return key

        def _hilbert_key(q, num_bits=NUM_BITS):
            n = 3
            X = [q[..., i] for i in range(n)]
            M = 1 << num_bits - 1
            Q = M
            while Q > 1:
                P = Q - 1
                for i in range(n):
                    cond = X[i] & Q > 0
                    t = (X[0] ^ X[i]) & P
                    new_X0 = jnp.where(cond, X[0] ^ P, X[0] ^ t)
                    if i != 0:
                        X[i] = jnp.where(cond, X[i], X[i] ^ t)
                    X[0] = new_X0
                Q >>= 1
            for i in range(1, n):
                X[i] = X[i] ^ X[i - 1]
            t = jnp.zeros_like(X[0])
            Q = M
            while Q > 1:
                t = jnp.where(X[n - 1] & Q > 0, t ^ Q - 1, t)
                Q >>= 1
            X = [xi ^ t for xi in X]
            key = jnp.zeros(X[0].shape, dtype=jnp.int32)
            for b in range(num_bits - 1, -1, -1):
                for i in range(n):
                    key = key << 1 | X[i] >> b & 1
            return key

        def _sorted_indices(coords_bn3):
            q = _quantize(coords_bn3)
            qt = q[..., jnp.array([1, 0, 2])]
            keys = [_morton_key(q), _morton_key(qt), _hilbert_key(q), _hilbert_key(qt)]
            return [jnp.argsort(kk, axis=1) for kk in keys]

        def _window_inds(sorted_idx, k=K):
            B, N = sorted_idx.shape
            i = jnp.arange(N)
            start = jnp.maximum(0, i - k // 2)
            end = jnp.minimum(N, i + k // 2 + 1)
            pos = jnp.minimum(start[:, None] + jnp.arange(k)[None, :], (end - 1)[:, None])
            return jnp.take(sorted_idx, pos, axis=1)

        def _get_graph_features(feats, inds_list, perm, W_lin, b_lin, k=K):
            B, N, C = feats.shape
            center = feats[:, :, None, :]
            gather = jax.vmap(lambda f, idx: f[idx])
            per_method = []
            for inds in inds_list:
                neigh = gather(feats, inds)
                gf = jnp.concatenate([jnp.broadcast_to(center, (B, N, k, C)), neigh - center], axis=-1)
                per_method.append(gf)
            allf = jnp.stack(per_method, axis=-1)
            allf = allf[..., perm]
            total = 2 * C * M_METHODS
            x = allf.reshape(B * N, k, total)
            x16 = x.astype(jnp.float16).astype(jnp.float32)
            headdim = min(32, total)
            nheads = total // headdim
            qh = x16.reshape(B * N, k, nheads, headdim)
            scores = jnp.einsum('bihd,bjhd->bhij', qh, qh) / np.float32(np.sqrt(headdim))
            attn = jax.nn.softmax(scores, axis=-1)
            out = jnp.einsum('bhij,bjhd->bihd', attn, qh).reshape(B * N, k, total)
            fused = out @ W_lin.T + b_lin
            return fused.reshape(B, N, k, 64)

        def _instance_norm(x, axes):
            mu = x.mean(axis=axes, keepdims=True)
            var = x.var(axis=axes, keepdims=True)
            return (x - mu) / jnp.sqrt(var + 1e-05)

        def _lrelu(x):
            return jnp.where(x > 0, x, 0.2 * x)
        key = jax.random.key(seed)
        ks = jax.random.split(key, 8)
        B, N, C = (2, 512, 32)
        tot = M_METHODS * 2 * C
        s = 0.02
        return {'coords': jax.random.normal(ks[0], (B, 3, N), jnp.float32), 'feats': jax.random.normal(ks[1], (B, C, N), jnp.float32), 'W_lin1': jax.random.normal(ks[2], (64, tot), jnp.float32) * s, 'b_lin1': jnp.zeros((64,), jnp.float32), 'W_lin2': jax.random.normal(ks[3], (64, tot), jnp.float32) * s, 'b_lin2': jnp.zeros((64,), jnp.float32), 'W_conv1': jax.random.normal(ks[4], (C, 2 * C), jnp.float32) * s, 'W_conv2': jax.random.normal(ks[5], (2 * C, 2 * C), jnp.float32) * s, 'W_conv3': jax.random.normal(ks[6], (C, 4 * C), jnp.float32) * s}
    _L0_xattn_all = _L0_xattn_setup()
    _L0_xattn_in = {k: v for k, v in _L0_xattn_all.items() if k in ('W_lin1', 'b_lin1', 'W_lin2', 'b_lin2', 'W_conv1', 'W_conv2', 'W_conv3')}
    del _L0_xattn_all

    def _L0_attn_setup():
        import jax, jax.numpy as jnp
        import numpy as np
        H_M, P_M, G_M, N_M, K_CONV, CHUNK = (128, 64, 8, 128, 4, 128)
        D_MODEL = 512
        D_INNER = H_M * P_M
        CONV_DIM = D_INNER + 2 * G_M * N_M
        PROJ_DIM = D_INNER + CONV_DIM + H_M
        EPS = 1e-05

        def segsum(x):
            l = x.shape[-1]
            xe = jnp.broadcast_to(x[..., None], x.shape + (l,))
            m1 = jnp.tril(jnp.ones((l, l), dtype=bool), -1)
            s = jnp.cumsum(jnp.where(m1, xe, 0.0), axis=-2)
            m2 = jnp.tril(jnp.ones((l, l), dtype=bool), 0)
            return jnp.where(m2, s, -jnp.inf)

        def causal_conv(x, w, bconv):
            k = w.shape[1]
            s = x.shape[1]
            xp = jnp.pad(x, ((0, 0), (k - 1, 0), (0, 0)))
            y = sum((xp[:, i:i + s, :] * w[:, i] for i in range(k)))
            return y + bconv
        key = jax.random.key(seed)
        ks = jax.random.split(key, 8)
        B_, S = (1, 256)
        sc = 0.02
        return {'x': jax.random.normal(ks[0], (B_, S, D_MODEL), dtype=jnp.float32), 'norm_w': jnp.ones((D_MODEL,), dtype=jnp.float32), 'in_proj_w': jax.random.normal(ks[1], (PROJ_DIM, D_MODEL), dtype=jnp.float32) * sc, 'conv_w': jax.random.normal(ks[2], (CONV_DIM, K_CONV), dtype=jnp.float32) * 0.2, 'conv_b': jnp.zeros((CONV_DIM,), dtype=jnp.float32), 'dt_bias': jax.random.uniform(ks[3], (H_M,), dtype=jnp.float32) * 0.1, 'A_log': jnp.log(1.0 + 15.0 * jax.random.uniform(ks[4], (H_M,), dtype=jnp.float32)), 'Dp': jnp.ones((H_M,), dtype=jnp.float32), 'gnorm_w': jnp.ones((D_INNER,), dtype=jnp.float32), 'out_proj_w': jax.random.normal(ks[5], (D_MODEL, D_INNER), dtype=jnp.float32) * sc}
    _L0_attn_all = _L0_attn_setup()
    _L0_attn_in = {k: v for k, v in _L0_attn_all.items() if k in ('norm_w', 'in_proj_w', 'conv_w', 'conv_b', 'dt_bias', 'A_log', 'Dp', 'gnorm_w', 'out_proj_w')}
    del _L0_attn_all

    def _L0_ffn_setup():
        import jax, jax.numpy as jnp
        import numpy as np
        LORA_SCALING = 1.0 / 2.0

        def _qlora_linear(x, wq, A, B):
            w = jnp.tile(wq, (1, 4))
            base = x @ w.T
            lora = x @ A.T @ B.T
            return base + lora * LORA_SCALING
        key = jax.random.key(seed)
        ks = jax.random.split(key, 10)
        d, h, r = (512, 1376, 2)
        return {'x': jax.random.normal(ks[0], (16, 1, d), dtype=jnp.float32), 'w1q': jax.random.normal(ks[1], (h, d // 4), dtype=jnp.float32) * 0.02, 'a1': jax.random.normal(ks[2], (r, d), dtype=jnp.float32) * 0.02, 'b1': jax.random.normal(ks[3], (h, r), dtype=jnp.float32) * 0.02, 'w3q': jax.random.normal(ks[4], (h, d // 4), dtype=jnp.float32) * 0.02, 'a3': jax.random.normal(ks[5], (r, d), dtype=jnp.float32) * 0.02, 'b3': jax.random.normal(ks[6], (h, r), dtype=jnp.float32) * 0.02, 'w2q': jax.random.normal(ks[7], (d, h // 4), dtype=jnp.float32) * 0.02, 'a2': jax.random.normal(ks[8], (r, h), dtype=jnp.float32) * 0.02, 'b2': jax.random.normal(ks[9], (d, r), dtype=jnp.float32) * 0.02}
    _L0_ffn_all = _L0_ffn_setup()
    _L0_ffn_in = {k: v for k, v in _L0_ffn_all.items() if k in ('w1q', 'a1', 'b1', 'w3q', 'a3', 'b3', 'w2q', 'a2', 'b2')}
    del _L0_ffn_all
    return {'x': x, 'ctx_4096': ctx_4096, 'L0_xattn_W_lin1': _L0_xattn_in['W_lin1'], 'L0_xattn_b_lin1': _L0_xattn_in['b_lin1'], 'L0_xattn_W_lin2': _L0_xattn_in['W_lin2'], 'L0_xattn_b_lin2': _L0_xattn_in['b_lin2'], 'L0_xattn_W_conv1': _L0_xattn_in['W_conv1'], 'L0_xattn_W_conv2': _L0_xattn_in['W_conv2'], 'L0_xattn_W_conv3': _L0_xattn_in['W_conv3'], 'L0_attn_norm_w': _L0_attn_in['norm_w'], 'L0_attn_in_proj_w': _L0_attn_in['in_proj_w'], 'L0_attn_conv_w': _L0_attn_in['conv_w'], 'L0_attn_conv_b': _L0_attn_in['conv_b'], 'L0_attn_dt_bias': _L0_attn_in['dt_bias'], 'L0_attn_A_log': _L0_attn_in['A_log'], 'L0_attn_Dp': _L0_attn_in['Dp'], 'L0_attn_gnorm_w': _L0_attn_in['gnorm_w'], 'L0_attn_out_proj_w': _L0_attn_in['out_proj_w'], 'L0_ffn_w1q': _L0_ffn_in['w1q'], 'L0_ffn_a1': _L0_ffn_in['a1'], 'L0_ffn_b1': _L0_ffn_in['b1'], 'L0_ffn_w3q': _L0_ffn_in['w3q'], 'L0_ffn_a3': _L0_ffn_in['a3'], 'L0_ffn_b3': _L0_ffn_in['b3'], 'L0_ffn_w2q': _L0_ffn_in['w2q'], 'L0_ffn_a2': _L0_ffn_in['a2'], 'L0_ffn_b2': _L0_ffn_in['b2']}

def reference(x, ctx_4096, L0_xattn_W_lin1, L0_xattn_b_lin1, L0_xattn_W_lin2, L0_xattn_b_lin2, L0_xattn_W_conv1, L0_xattn_W_conv2, L0_xattn_W_conv3, L0_attn_norm_w, L0_attn_in_proj_w, L0_attn_conv_w, L0_attn_conv_b, L0_attn_dt_bias, L0_attn_A_log, L0_attn_Dp, L0_attn_gnorm_w, L0_attn_out_proj_w, L0_ffn_w1q, L0_ffn_a1, L0_ffn_b1, L0_ffn_w3q, L0_ffn_a3, L0_ffn_b3, L0_ffn_w2q, L0_ffn_a2, L0_ffn_b2):
    import jax
    import jax.numpy as jnp

    def _L0_xattn_ref(coords, feats, W_lin1, b_lin1, W_lin2, b_lin2, W_conv1, W_conv2, W_conv3):
        import jax, jax.numpy as jnp
        import numpy as np
        K = 10
        NUM_BITS = 10
        M_METHODS = 4

        def _quantize(coords, num_bits=NUM_BITS):
            cmin = coords.min(axis=1, keepdims=True)
            cmax = coords.max(axis=1, keepdims=True)
            scale = (2 ** num_bits - 1) / (cmax - cmin + 1e-06)
            q = jnp.floor((coords - cmin) * scale)
            return jnp.clip(q, 0, 2 ** num_bits - 1).astype(jnp.int32)

        def _morton_key(q):
            x, y, z = (q[..., 0], q[..., 1], q[..., 2])
            key = jnp.zeros(x.shape, dtype=jnp.int32)
            for b in range(NUM_BITS):
                key = key | (x >> b & 1) << 3 * b + 2 | (y >> b & 1) << 3 * b + 1 | (z >> b & 1) << 3 * b
            return key

        def _hilbert_key(q, num_bits=NUM_BITS):
            n = 3
            X = [q[..., i] for i in range(n)]
            M = 1 << num_bits - 1
            Q = M
            while Q > 1:
                P = Q - 1
                for i in range(n):
                    cond = X[i] & Q > 0
                    t = (X[0] ^ X[i]) & P
                    new_X0 = jnp.where(cond, X[0] ^ P, X[0] ^ t)
                    if i != 0:
                        X[i] = jnp.where(cond, X[i], X[i] ^ t)
                    X[0] = new_X0
                Q >>= 1
            for i in range(1, n):
                X[i] = X[i] ^ X[i - 1]
            t = jnp.zeros_like(X[0])
            Q = M
            while Q > 1:
                t = jnp.where(X[n - 1] & Q > 0, t ^ Q - 1, t)
                Q >>= 1
            X = [xi ^ t for xi in X]
            key = jnp.zeros(X[0].shape, dtype=jnp.int32)
            for b in range(num_bits - 1, -1, -1):
                for i in range(n):
                    key = key << 1 | X[i] >> b & 1
            return key

        def _sorted_indices(coords_bn3):
            q = _quantize(coords_bn3)
            qt = q[..., jnp.array([1, 0, 2])]
            keys = [_morton_key(q), _morton_key(qt), _hilbert_key(q), _hilbert_key(qt)]
            return [jnp.argsort(kk, axis=1) for kk in keys]

        def _window_inds(sorted_idx, k=K):
            B, N = sorted_idx.shape
            i = jnp.arange(N)
            start = jnp.maximum(0, i - k // 2)
            end = jnp.minimum(N, i + k // 2 + 1)
            pos = jnp.minimum(start[:, None] + jnp.arange(k)[None, :], (end - 1)[:, None])
            return jnp.take(sorted_idx, pos, axis=1)

        def _get_graph_features(feats, inds_list, perm, W_lin, b_lin, k=K):
            B, N, C = feats.shape
            center = feats[:, :, None, :]
            gather = jax.vmap(lambda f, idx: f[idx])
            per_method = []
            for inds in inds_list:
                neigh = gather(feats, inds)
                gf = jnp.concatenate([jnp.broadcast_to(center, (B, N, k, C)), neigh - center], axis=-1)
                per_method.append(gf)
            allf = jnp.stack(per_method, axis=-1)
            allf = allf[..., perm]
            total = 2 * C * M_METHODS
            x = allf.reshape(B * N, k, total)
            x16 = x.astype(jnp.float16).astype(jnp.float32)
            headdim = min(32, total)
            nheads = total // headdim
            qh = x16.reshape(B * N, k, nheads, headdim)
            scores = jnp.einsum('bihd,bjhd->bhij', qh, qh) / np.float32(np.sqrt(headdim))
            attn = jax.nn.softmax(scores, axis=-1)
            out = jnp.einsum('bhij,bjhd->bihd', attn, qh).reshape(B * N, k, total)
            fused = out @ W_lin.T + b_lin
            return fused.reshape(B, N, k, 64)

        def _instance_norm(x, axes):
            mu = x.mean(axis=axes, keepdims=True)
            var = x.var(axis=axes, keepdims=True)
            return (x - mu) / jnp.sqrt(var + 1e-05)

        def _lrelu(x):
            return jnp.where(x > 0, x, 0.2 * x)
        inds_sorted = _sorted_indices(coords.transpose(0, 2, 1))
        inds_list = [_window_inds(s) for s in inds_sorted]
        perm1 = jnp.array([2, 0, 3, 1])
        perm2 = jnp.array([1, 3, 0, 2])
        f0 = feats.transpose(0, 2, 1)
        g1 = _get_graph_features(f0, inds_list, perm1, W_lin1, b_lin1)
        h1 = jnp.einsum('oc,bnkc->bonk', W_conv1, g1)
        h1 = _lrelu(_instance_norm(h1, (2, 3)))
        feats1 = h1.max(axis=-1)
        g2 = _get_graph_features(feats1.transpose(0, 2, 1), inds_list, perm2, W_lin2, b_lin2)
        h2 = jnp.einsum('oc,bnkc->bonk', W_conv2, g2)
        h2 = _lrelu(_instance_norm(h2, (2, 3)))
        feats2 = h2.max(axis=-1)
        f3 = jnp.concatenate([feats, feats1, feats2], axis=1)
        h3 = jnp.einsum('oc,bcn->bon', W_conv3, f3)
        return _lrelu(_instance_norm(h3, (2,)))

    def _L0_attn_ref(x, norm_w, in_proj_w, conv_w, conv_b, dt_bias, A_log, Dp, gnorm_w, out_proj_w):
        import jax, jax.numpy as jnp
        import numpy as np
        H_M, P_M, G_M, N_M, K_CONV, CHUNK = (128, 64, 8, 128, 4, 128)
        D_MODEL = 512
        D_INNER = H_M * P_M
        CONV_DIM = D_INNER + 2 * G_M * N_M
        PROJ_DIM = D_INNER + CONV_DIM + H_M
        EPS = 1e-05

        def segsum(x):
            l = x.shape[-1]
            xe = jnp.broadcast_to(x[..., None], x.shape + (l,))
            m1 = jnp.tril(jnp.ones((l, l), dtype=bool), -1)
            s = jnp.cumsum(jnp.where(m1, xe, 0.0), axis=-2)
            m2 = jnp.tril(jnp.ones((l, l), dtype=bool), 0)
            return jnp.where(m2, s, -jnp.inf)

        def causal_conv(x, w, bconv):
            k = w.shape[1]
            s = x.shape[1]
            xp = jnp.pad(x, ((0, 0), (k - 1, 0), (0, 0)))
            y = sum((xp[:, i:i + s, :] * w[:, i] for i in range(k)))
            return y + bconv
        b, s, _ = x.shape
        residual = x
        h = x * jax.lax.rsqrt(jnp.mean(x * x, axis=-1, keepdims=True) + EPS) * norm_w
        proj = jnp.einsum('bsd,od->bso', h, in_proj_w)
        gate = proj[..., :D_INNER]
        hBC = proj[..., D_INNER:D_INNER + CONV_DIM]
        dt = proj[..., D_INNER + CONV_DIM:]
        hBC = jax.nn.silu(causal_conv(hBC, conv_w, conv_b))
        hid = hBC[..., :D_INNER].reshape(b, s, H_M, P_M)
        B = hBC[..., D_INNER:D_INNER + G_M * N_M].reshape(b, s, G_M, N_M)
        C = hBC[..., D_INNER + G_M * N_M:].reshape(b, s, G_M, N_M)
        dt = jax.nn.softplus(dt + dt_bias)
        A = -jnp.exp(A_log)
        pad = -s % CHUNK
        D_res = Dp[None, None, :, None] * hid
        hid_dt = hid * dt[..., None]
        A_full = A[None, None, :] * dt

        def padseq(t):
            return jnp.pad(t, [(0, 0), (0, pad)] + [(0, 0)] * (t.ndim - 2))
        hid_dt, A_full, Bp, Cp = (padseq(hid_dt), padseq(A_full), padseq(B), padseq(C))
        S = s + pad
        c, l = (S // CHUNK, CHUNK)
        hc = hid_dt.reshape(b, c, l, H_M, P_M)
        Ac = A_full.reshape(b, c, l, H_M).transpose(0, 3, 1, 2)
        rep = H_M // G_M
        Bh = jnp.repeat(Bp.reshape(b, c, l, G_M, N_M), rep, axis=3)
        Ch = jnp.repeat(Cp.reshape(b, c, l, G_M, N_M), rep, axis=3)
        A_cs = jnp.cumsum(Ac, axis=-1)
        L = jnp.exp(segsum(Ac))
        M = jnp.einsum('bcihn,bcjhn->bcijh', Ch, Bh) * jnp.transpose(L, (0, 2, 3, 4, 1))
        Y_diag = jnp.einsum('bcijh,bcjhp->bcihp', M, hc)
        decay_states = jnp.exp(A_cs[..., -1:] - A_cs)
        states = jnp.einsum('bclhn,bhcl,bclhp->bchpn', Bh, decay_states, hc)
        A_last = jnp.pad(A_cs[..., -1], ((0, 0), (0, 0), (1, 0)))
        decay_chunk = jnp.exp(segsum(A_last))
        states_cat = jnp.concatenate([jnp.zeros_like(states[:, :1]), states], axis=1)
        prev_states = jnp.einsum('bhij,bjhpn->bihpn', decay_chunk, states_cat)[:, :-1]
        Y_off = jnp.einsum('bclhn,bchpn,bhcl->bclhp', Ch, prev_states, jnp.exp(A_cs))
        y = (Y_diag + Y_off).reshape(b, S, H_M, P_M)[:, :s] + D_res
        y = y.reshape(b, s, D_INNER)
        yg = y * jax.nn.silu(gate)
        gsz = D_INNER // G_M
        ygr = yg.reshape(b, s, G_M, gsz)
        ygr = ygr * jax.lax.rsqrt(jnp.mean(ygr * ygr, axis=-1, keepdims=True) + EPS)
        y = ygr.reshape(b, s, D_INNER) * gnorm_w
        out = jnp.einsum('bsd,od->bso', y, out_proj_w)
        return residual + out

    def _L0_ffn_ref(x, w1q, a1, b1, w3q, a3, b3, w2q, a2, b2):
        import jax, jax.numpy as jnp
        import numpy as np
        LORA_SCALING = 1.0 / 2.0

        def _qlora_linear(x, wq, A, B):
            w = jnp.tile(wq, (1, 4))
            base = x @ w.T
            lora = x @ A.T @ B.T
            return base + lora * LORA_SCALING
        gate = jax.nn.silu(_qlora_linear(x, w1q, a1, b1))
        up = _qlora_linear(x, w3q, a3, b3)
        return _qlora_linear(gate * up, w2q, a2, b2)
    x = x + _L0_xattn_ref(ctx_4096, _layernorm(x, axis=-1), L0_xattn_W_lin1, L0_xattn_b_lin1, L0_xattn_W_lin2, L0_xattn_b_lin2, L0_xattn_W_conv1, L0_xattn_W_conv2, L0_xattn_W_conv3)
    x = x + _L0_attn_ref(_layernorm(x, axis=-1), L0_attn_norm_w, L0_attn_in_proj_w, L0_attn_conv_w, L0_attn_conv_b, L0_attn_dt_bias, L0_attn_A_log, L0_attn_Dp, L0_attn_gnorm_w, L0_attn_out_proj_w)
    x = x + _L0_ffn_ref(_layernorm(x, axis=-1), L0_ffn_w1q, L0_ffn_a1, L0_ffn_b1, L0_ffn_w3q, L0_ffn_a3, L0_ffn_b3, L0_ffn_w2q, L0_ffn_a2, L0_ffn_b2)
    return x

_drawn_inputs = setup_inputs


def setup_inputs(seed=0):
    import zlib

    import numpy as np

    out = dict(_drawn_inputs(seed))
    spreads = {'L0_xattn_b_lin1': (0.0, 0.8),
     'L0_xattn_b_lin2': (0.0, 0.8),
     'L0_attn_norm_w': (1.0, 0.2),
     'L0_attn_conv_b': (0.0, 0.1),
     'L0_attn_Dp': (1.0, 0.2),
     'L0_attn_gnorm_w': (1.0, 0.2)}
    factors = {'L0_attn_dt_bias': 8.0,
     'L0_attn_A_log': 8.0,
     'L0_ffn_a1': 8.0,
     'L0_ffn_b1': 8.0,
     'L0_ffn_a3': 8.0,
     'L0_ffn_b3': 8.0,
     'L0_ffn_a2': 8.0,
     'L0_ffn_b2': 8.0}
    for name, (base, spread) in spreads.items():
        noise = np.random.default_rng([zlib.crc32(name.encode()), seed]).standard_normal(out[name].shape)
        drawn = base * np.exp(spread * noise) if base else spread * noise
        out[name] = jnp.asarray(drawn.astype(out[name].dtype))
    for name, factor in factors.items():
        out[name] = (out[name] * factor).astype(out[name].dtype)
    return out
```

```python
from contextlib import ExitStack

import concourse.bass as bass
from concourse import mybir

F32 = mybir.dt.float32
F16 = mybir.dt.float16
I32 = mybir.dt.int32
ALU = mybir.AluOpType
ACT = mybir.ActivationFunctionType
X = mybir.AxisListType.X

B, S, D = 16, 32, 512
N = D
C = S
NT = N // 128
M = 4
K = 10
HALF = K // 2
BITS = 10
LEAD = HALF
PTS = 3
SUBS = 15
GROUPS = 12
GP = PTS * SUBS
PADN = GP * GROUPS
NSUB = (N - LEAD) // PTS + 2
GC = 32 * SUBS
EXT = LEAD * K + N + HALF - 1
EPS = 1e-5
SLOPE = 0.2
HEADS, HD, GR, NST, TAPS = 128, 64, 8, 128, 4
INNER = HEADS * HD
TOK = B * S
TT = TOK // 128
DT = D // 128
CT_ = INNER // 128
TPG = CT_ // GR
FFH = 1376
FQ = FFH // 4
FR = 4
FP = FQ // FR



def clear(nc, semaphores):
    with nc.Block() as block:
        @block.sync
        def _(sp):
            for s in semaphores:
                sp.sem_clear(s)


def chain(eng, sem):
    count = [0]

    def link(ins):
        count[0] += 1
        ins.then_inc(sem, 1)
        eng.wait_ge(sem, count[0])
        return ins

    return link


def norm_and_keys(nc, io, scratch):
    with ExitStack() as ctx:
        def sb(name, shape, dt=F32):
            return ctx.enter_context(nc.sbuf_tensor(name, shape, dt))

        used = []

        def sem(name):
            used.append(ctx.enter_context(nc.semaphore(name)))
            return used[-1]

        lat = sb("lat", [128, 4, D])
        latn = sb("latn", [128, 4, D])
        bst = sb("bst", [128, 4, 6])
        mv = sb("mv", [128, 4, 2])
        sd = sb("sd", [128, 4])
        rstd = sb("rstd", [128, 4])
        rtmp = sb("rtmp", [128, 4])
        co = sb("co", [48, N])
        cv = sb("cv", [48, N])
        ci = sb("ci", [48, N], I32)
        cf = sb("cf", [48, N])
        cg = sb("cg", [48, N])
        sc = sb("sc", [48, 24])
        sci = sb("sci", [48, 4], I32)
        P64 = B * N // 128
        A = sb("A", [128, 4, 3, P64], I32)
        A2 = sb("A2", [128, 4, 3, P64], I32)
        qin = sb("qin", [128, 3, P64], I32)
        u = sb("u", [128, 6, 2, P64], I32)
        key = sb("key", [128, 4, P64], I32)
        kp = sb("kp", [128, 4, P64], I32)
        hi = sb("hi", [128, 4, P64])
        lo = sb("lo", [128, 4, P64])
        idx = sb("idx", [128, P64])

        lat_in = sem("lat_in")
        co_in = sem("co_in")
        idx_in = sem("idx_in")
        q_out = sem("q_out")
        q_in = sem("q_in")
        q_ready = sem("q_ready")
        var_ready = sem("var_ready")
        sd_ready = sem("sd_ready")
        latn_ready = sem("latn_ready")
        keys_ready = sem("keys_ready")
        stored = sem("stored")
        v_chain = sem("v_chain_keys")
        ctx.callback(clear, nc, used)
        block = ctx.enter_context(nc.Block())

        @block.sync
        def _(sp):
            sp.dma_start(co[:, :], io["coords"]).then_inc(co_in, 16)
            sp.dma_start(idx[:, :], io["idx"]).then_inc(idx_in, 16)
            sp.dma_start(lat[:, :, :], io["x"].rearrange("(t p) d -> p t d", p=128)).then_inc(lat_in, 16)
            sp.wait_ge(q_ready, 1)
            sp.dma_start(scratch["q"], ci[:, :]).then_inc(q_out, 16)
            sp.wait_ge(q_out, 16)
            sp.dma_start(qin[:, :, :], scratch["q"].rearrange("(k b) n -> k (b n)", k=3)
                         .rearrange("k (p i) -> p k i", p=128)).then_inc(q_in, 16)
            sp.wait_ge(latn_ready, 1)
            sp.dma_start(scratch["f0"].rearrange("(t p) d -> p t d", p=128), latn[:, :, :]).then_inc(stored, 16)
            sp.wait_ge(keys_ready, 1)
            sp.dma_start(scratch["hi"].rearrange("m b n -> m (b n)").rearrange("m (p i) -> p m i", p=128),
                         hi[:, :, :]).then_inc(stored, 16)
            sp.dma_start(scratch["lo"].rearrange("m b n -> m (b n)").rearrange("m (p i) -> p m i", p=128),
                         lo[:, :, :]).then_inc(stored, 16)
            sp.wait_ge(stored, 48)

        @block.scalar
        def _(act):
            act.wait_ge(var_ready, 1)
            nc.scalar.activation(sd[:, :], mv[:, :, 1], ACT.Sqrt).then_inc(sd_ready, 1)

        @block.vector
        def _(dve):
            link = chain(dve, v_chain)
            v = nc.vector
            dve.wait_ge(co_in, 16)
            cmin, cmax, d, r, s, e = (sc[:, i:i + 1] for i in range(6))
            dh, dl, sh, sl, t0, t1 = (sc[:, i:i + 1] for i in range(6, 12))
            link(v.tensor_reduce(cmin, co[:, :], X, ALU.min))
            link(v.tensor_reduce(cmax, co[:, :], X, ALU.max))
            link(v.tensor_tensor(d, cmax, cmin, ALU.subtract))
            link(v.tensor_scalar(d, d, 1e-6, None, ALU.add))
            link(v.reciprocal(r, d))
            link(v.tensor_scalar(s, r, 1023.0, None, ALU.mult))
            for whole, high, low in ((d, dh, dl), (s, sh, sl)):
                link(v.tensor_scalar(high.bitcast(I32), whole.bitcast(I32), -4096, None, ALU.bitwise_and))
                link(v.tensor_tensor(low, whole, high, ALU.subtract))
            link(v.tensor_tensor(t0, sh, dh, ALU.mult))
            link(v.tensor_scalar(e, t0, -1.0, 1023.0, ALU.mult, ALU.add))
            for a, b in ((sh, dl), (sl, dh), (sl, dl)):
                link(v.tensor_tensor(t1, a, b, ALU.mult))
                link(v.tensor_tensor(e, e, t1, ALU.subtract))
            link(v.tensor_tensor(t1, e, r, ALU.mult))
            link(v.tensor_tensor(s, s, t1, ALU.add))
            link(v.tensor_scalar(cv[:, :], co[:, :], cmin, s, ALU.subtract, ALU.mult))
            link(v.tensor_copy(ci[:, :], cv[:, :]))
            link(v.tensor_copy(cf[:, :], ci[:, :]))
            link(v.tensor_tensor(cg[:, :], cf[:, :], cv[:, :], ALU.is_gt))
            link(v.tensor_tensor(cf[:, :], cf[:, :], cg[:, :], ALU.subtract))
            link(v.tensor_scalar(cf[:, :], cf[:, :], 0.0, float(2 ** BITS - 1), ALU.max, ALU.min))
            v.tensor_copy(ci[:, :], cf[:, :]).then_inc(q_ready, 1)

            dve.wait_ge(lat_in, 16)
            for t in range(4):
                link(v.bn_stats(bst[:, t, :], lat[:, t, :]))
            for t in range(4):
                link(v.bn_aggr(mv[:, t, :], bst[:, t, :]))
            v.tensor_scalar(mv[:, :, 1], mv[:, :, 1], EPS, None, ALU.add).then_inc(var_ready, 1)
            dve.wait_ge(sd_ready, 1)
            inverse_root(v, link, rstd[:, :], mv[:, :, 1], sd[:, :], rtmp[:, :])
            for t in range(4):
                last = v.tensor_scalar(latn[:, t, :], lat[:, t, :], mv[:, t, 0:1], rstd[:, t:t + 1],
                                       ALU.subtract, ALU.mult)
                if t < 3:
                    link(last)
            last.then_inc(latn_ready, 1)

            dve.wait_ge(q_in, 16)
            for m in range(4):
                for k in range(3):
                    link(v.tensor_copy(A[:, m, k, :], qin[:, (k if m % 2 == 0 or k == 2 else 1 - k), :]))
            ax = [A[:, 2:4, k, :] for k in range(3)]
            neg, pos, t, w = (u[:, i, :, :] for i in range(4))
            for bit in range(BITS - 1, 0, -1):
                low = 2 ** bit - 1
                link(v.tensor_scalar(pos, ax[0], 31 - bit, 31, ALU.logical_shift_left, ALU.arith_shift_right))
                link(v.scalar_tensor_tensor(ax[0], pos, low, ax[0], ALU.bitwise_and, ALU.bitwise_xor))
                for i in (1, 2):
                    link(v.tensor_scalar(pos, ax[i], 31 - bit, 31, ALU.logical_shift_left, ALU.arith_shift_right))
                    link(v.tensor_scalar(neg, pos, -1, None, ALU.bitwise_xor))
                    link(v.tensor_tensor(t, ax[0], ax[i], ALU.bitwise_xor))
                    link(v.scalar_tensor_tensor(w, t, low, neg, ALU.bitwise_and, ALU.bitwise_and))
                    link(v.tensor_tensor(ax[i], ax[i], w, ALU.bitwise_xor))
                    link(v.scalar_tensor_tensor(t, pos, low, w, ALU.bitwise_and, ALU.bitwise_xor))
                    link(v.tensor_tensor(ax[0], ax[0], t, ALU.bitwise_xor))
            link(v.tensor_tensor(ax[1], ax[1], ax[0], ALU.bitwise_xor))
            link(v.tensor_tensor(ax[2], ax[2], ax[1], ALU.bitwise_xor))
            for bit in range(BITS - 1, 0, -1):
                link(v.tensor_scalar(pos, ax[2], 31 - bit, 31, ALU.logical_shift_left, ALU.arith_shift_right))
                if bit == BITS - 1:
                    link(v.tensor_scalar(t, pos, 2 ** bit - 1, None, ALU.bitwise_and))
                else:
                    link(v.scalar_tensor_tensor(t, pos, 2 ** bit - 1, t, ALU.bitwise_and, ALU.bitwise_xor))
            for k in range(3):
                link(v.tensor_tensor(ax[k], ax[k], t, ALU.bitwise_xor))
            flat = A[:, :, :, :].rearrange("p m k i -> p (m k i)")
            flat2 = A2[:, :, :, :].rearrange("p m k i -> p (m k i)")
            for shift, mask in ((16, 0x030000FF), (8, 0x0300F00F), (4, 0x030C30C3), (2, 0x09249249)):
                link(v.scalar_tensor_tensor(flat2, flat, shift, flat, ALU.logical_shift_left, ALU.bitwise_or))
                link(v.tensor_scalar(flat, flat2, mask, None, ALU.bitwise_and))
            link(v.scalar_tensor_tensor(key[:, :, :], A[:, :, 0, :], 2, A[:, :, 2, :],
                                        ALU.logical_shift_left, ALU.bitwise_or))
            link(v.scalar_tensor_tensor(kp[:, :, :], A[:, :, 1, :], 1, key[:, :, :],
                                        ALU.logical_shift_left, ALU.bitwise_or))
            link(v.tensor_scalar(key[:, :, :], kp[:, :, :], 12, None, ALU.logical_shift_right))
            link(v.tensor_copy(hi[:, :, :], key[:, :, :]))
            link(v.tensor_scalar(hi[:, :, :], hi[:, :, :], 4096.0, None, ALU.mult))
            link(v.tensor_scalar(key[:, :, :], kp[:, :, :], 4095, None, ALU.bitwise_and))
            link(v.tensor_copy(lo[:, :, :], key[:, :, :]))
            dve.wait_ge(idx_in, 16)
            v.tensor_tensor(lo[:, :, :], lo[:, :, :], idx[:, :].unsqueeze(1).to_broadcast([128, 4, P64]),
                            ALU.add).then_inc(keys_ready, 1)


def ranks(nc, io, scratch, rank):
    with ExitStack() as ctx:
        def sb(name, shape, dt=F32):
            return ctx.enter_context(nc.sbuf_tensor(name, shape, dt))

        used = []

        def sem(name):
            used.append(ctx.enter_context(nc.semaphore(name)))
            return used[-1]

        ident = sb("ident_r", [64, 64])
        hrow = sb("hrow", [64, N])
        lrow = sb("lrow", [64, N])
        hcol = sb("hcol", [128, NT, M * B])
        lcol = sb("lcol", [128, NT, M * B])
        hall = sb("hall", [128, 2, M, N])
        lall = sb("lall", [128, 2, M, N])
        diff = sb("diff", [128, 4, N])
        sign = sb("sign", [128, 4, N])
        tally = sb("tally", [128, M * B, NT])
        tp = ctx.enter_context(nc.psum_tensor("tp_r", [128, 2, 512], F32))

        rows_in = sem("rows_in")
        turned = sem("turned")
        cols_ready = sem("cols_ready")
        all_in = [sem("all_in0"), sem("all_in1")]
        diff_ready = sem("diff_ready")
        tallied = sem("tallied")
        ctx.callback(clear, nc, used)
        block = ctx.enter_context(nc.Block())

        @block.sync
        def _(sp):
            sp.dma_start(ident[:, :], io["ident"][0:64, 0:64]).then_inc(rows_in, 16)
            sp.dma_start(hrow[:, :], scratch["hi"].rearrange("m b n -> (m b) n")).then_inc(rows_in, 16)
            sp.dma_start(lrow[:, :], scratch["lo"].rearrange("m b n -> (m b) n")).then_inc(rows_in, 16)
            with sp.Fori(0, B // 2) as i:
                for k in range(2):
                    sp.wait_ge(diff_ready, i * (2 * M * NT) + (k + 1) * M * NT)
                    for dst, src in ((hall, "hi"), (lall, "lo")):
                        sp.dma_start(dst[:, k, :, :],
                                     scratch[src][:, bass.ds(2 * i + k, 1), :].rearrange("m b n -> (m b) n")
                                     .partition_broadcast(128)).then_inc(all_in[k], 16)

        @block.tensor
        def _(pe):
            pe.wait_ge(rows_in, 48)
            for t in range(NT):
                nc.tensor.transpose(tp[:, 0, t * 64:t * 64 + 64], hrow[:, t * 128:(t + 1) * 128], ident[:, :])
                last = nc.tensor.transpose(tp[:, 1, t * 64:t * 64 + 64], lrow[:, t * 128:(t + 1) * 128], ident[:, :])
            last.then_inc(turned, 1)

        @block.vector
        def _(dve):
            v = nc.vector
            dve.wait_ge(turned, 1)
            v.tensor_copy(hcol[:, :, :], tp[:, 0, 0:NT * 64].rearrange("p (t r) -> p t r", t=NT)).then_inc(cols_ready, 1)
            v.tensor_scalar(lcol[:, :, :], tp[:, 1, 0:NT * 64].rearrange("p (t r) -> p t r", t=NT), -1.0, None,
                            ALU.mult).then_inc(cols_ready, 1)
            dve.wait_ge(cols_ready, 2)
            dve.sem_inc(diff_ready, 2 * M * NT)
            with dve.Fori(0, B // 2) as i:
                for k in range(2):
                    b = 2 * i + k
                    dve.wait_ge(all_in[k], 32 * i + 32)
                    for m in range(M):
                        for t in range(NT):
                            j = m * NT + t
                            dve.wait_ge(tallied, b * (M * NT) + (j + 1))
                            ins = v.scalar_tensor_tensor(
                                diff[:, j % 4, :], hall[:, k, m, :], hcol[:, t, bass.ds(b + m * B, 1)],
                                lall[:, k, m, :], ALU.subtract, ALU.add)
                            ins.then_inc(diff_ready, 1)
            dve.wait_ge(tallied, B * M * NT + 4)
            v.tensor_scalar(rank[:, :, :], tally[:, :, :], -0.5, (N - 1) / 2.0, ALU.mult, ALU.add)\
                .then_inc(cols_ready, 1)

        @block.scalar
        def _(act):
            act.wait_ge(cols_ready, 2)
            act.sem_inc(tallied, 4)
            with act.Fori(0, B) as b:
                for m in range(M):
                    for t in range(NT):
                        j = m * NT + t
                        act.wait_ge(diff_ready, b * (M * NT) + (2 * M * NT + j + 1))
                        act.wait_ge(tallied, b * (M * NT) + (j + 1))
                        ins = nc.scalar.activation(sign[:, j % 4, :], diff[:, j % 4, :], ACT.Sign,
                                                   bias=lcol[:, t, bass.ds(b + m * B, 1)],
                                                   accum_out=tally[:, bass.ds(b + m * B, 1), t])
                        ins.then_inc(tallied, 1)


def inverse_root(v, link, out, var, root, tmp):
    link(v.reciprocal(out, root))
    link(v.tensor_tensor(tmp, out, out, ALU.mult))
    link(v.tensor_tensor(tmp, tmp, var, ALU.mult))
    link(v.tensor_scalar(tmp, tmp, -0.5, 1.5, ALU.mult, ALU.add))
    return link(v.tensor_tensor(out, out, tmp, ALU.mult))


def split16(v, link, high, low, whole):
    link(v.tensor_copy(high, whole))
    return link(v.tensor_tensor(low, whole, high, ALU.subtract))


def fold_weights(nc, io, layer, O, W):
    with ExitStack() as ctx:
        def sb(name, shape, dt=F32):
            return ctx.enter_context(nc.sbuf_tensor(name + layer, shape, dt))

        used = []

        def sem(name):
            used.append(ctx.enter_context(nc.semaphore(name + "_fw" + layer)))
            return used[-1]

        ident = sb("ident_w", [128, 128])
        lin = sb("lin", [64, 256])
        convT = sb("convT", [64, O])
        blin = sb("blin", [64, 1])
        eff = sb("eff", [O, 256])
        inv = sb("inv", [O, 1])
        pw = ctx.enter_context(nc.psum_tensor("pw" + layer, [128, 4, 512], F32))
        w_in = sem("w_in")
        folded = sem("folded")
        scaled = sem("scaled")
        turned = sem("w_turned")
        v_chain = sem("v_chain_w")
        ctx.callback(clear, nc, used)
        block = ctx.enter_context(nc.Block())

        @block.sync
        def _(sp):
            sp.dma_start(ident[:, :], io["ident"]).then_inc(w_in, 16)
            sp.dma_start(lin[:, :], io["lin" + layer]).then_inc(w_in, 16)
            sp.dma_start(convT[:, :], io["convT" + layer]).then_inc(w_in, 16)
            sp.dma_start(blin[:, :], io["blin" + layer]).then_inc(w_in, 16)

        @block.tensor
        def _(pe):
            pe.wait_ge(w_in, 64)
            nc.tensor.matmul(pw[0:O, 0, 0:256], convT[:, :], lin[:, :], start=True, stop=True)
            nc.tensor.matmul(pw[0:O, 1, 0:1], convT[:, :], blin[:, :], start=True, stop=True).then_inc(folded, 1)
            pe.wait_ge(scaled, 1)
            nc.tensor.transpose(pw[:, 2, 0:O], eff[:, 0:128], ident[0:O, 0:O])
            nc.tensor.transpose(pw[:, 3, 0:O], eff[:, 128:256], ident[0:O, 0:O]).then_inc(turned, 1)

        @block.vector
        def _(dve):
            v = nc.vector
            link = chain(dve, v_chain)
            dve.wait_ge(folded, 1)
            link(v.tensor_copy(W["bias"][0:O, :], pw[0:O, 1, 0:1]))
            link(v.tensor_reduce(W["amax"][0:O, :], pw[0:O, 0, 0:256], X, ALU.max, apply_absolute_value=True))
            link(v.tensor_scalar(W["amax"][0:O, :], W["amax"][0:O, :], 1e-30, None, ALU.max))
            link(v.reciprocal(inv[:, :], W["amax"][0:O, :]))
            v.tensor_scalar(eff[:, :], pw[0:O, 0, 0:256], inv[:, :], None, ALU.mult).then_inc(scaled, 1)
            dve.wait_ge(turned, 1)
            split16(v, link, W["center_hi"][:, 0:O], W["center_lo"][:, 0:O], pw[:, 2, 0:O])
            split16(v, link, W["neigh_hi"][:, 0:O], W["neigh_lo"][:, 0:O], pw[:, 3, 0:O])



def steps(eng, step, T, U):
    for s in list(range(U)):
        step(s % U, lambda lag, s=s: (s - lag, (s - lag) // U) if 0 <= s - lag < T else None)
    with eng.Fori(1, T // U) as i:
        for k in range(U):
            step(k, lambda lag, k=k: (i * U + (k - lag), i + (k - lag) // U))
    for s in range(T, T + U):
        step(s % U, lambda lag, s=s: (s - lag, (s - lag) // U) if 0 <= s - lag < T else None)


def gather_windows(nc, io, scratch, layer, feats, perm, rank):
    with ExitStack() as ctx:
        def sb(name, shape, dt=F32):
            return ctx.enter_context(nc.sbuf_tensor(name + layer, shape, dt))

        used = []

        def sem(name):
            used.append(ctx.enter_context(nc.semaphore(name + "_gw" + layer)))
            return used[-1]

        H2 = EXT // 2
        ident = sb("ident_g", [32, 32])
        rep = sb("rep", [32, 128])
        place = sb("place", [128, EXT], F16)
        fb = sb("fb", [32, 2, N])
        t16 = sb("t16", [128, 2, NT * C], F16)
        l16 = sb("l16", [128, 2, NT * C], F16)
        FX = sb("FX", [128, 2, 2, M * NT * 128], F16)
        onehot = sb("onehot", [128, 2, M * NT, EXT], F16)
        ext = sb("ext", [128, 4, EXT])
        cen = sb("cen", [128, 4, PADN])
        cen16 = sb("cen16", [128, 4, PADN], F16)
        QT = sb("QT", [128, 4, GROUPS, 32, SUBS], F16)
        ptok = ctx.enter_context(nc.psum_tensor("ptok" + layer, [128, 2, 512], F32))
        pcen = ctx.enter_context(nc.psum_tensor("pcen" + layer, [128, 2, 512], F32))
        pext = ctx.enter_context(nc.psum_tensor("pext" + layer, [128, 2, 2, 512], F32))

        const_in = sem("const_in")
        zeroed = sem("zeroed")
        f_in = [sem("f_in0"), sem("f_in1")]
        f_used = sem("f_used")
        t16_ready = sem("t16_ready")
        l16_ready = sem("l16_ready")
        fx_ready = sem("fx_ready")
        hot_ready = sem("hot_ready")
        gathered = sem("gathered")
        ext_ready = sem("ext_ready")
        cen_ready = sem("cen_ready")
        q_v = sem("q_v")
        q_g = sem("q_g")
        q_out = [sem(f"q_out{k}") for k in range(4)]
        QV, QG = 8, 4
        ctx.callback(clear, nc, used)
        block = ctx.enter_context(nc.Block())

        def window_rows(eng, k, n, sem_):
            last = None
            for g0, g1, s0, s1 in ((0, 1, 2, SUBS), (1, GROUPS - 1, 0, SUBS),
                                   (GROUPS - 1, GROUPS, 0, NSUB - SUBS * (GROUPS - 1))):
                base = 44 + n + GP * g0 + PTS * s0
                at = ext[:, k, base:base + 1]
                ctr = cen[:, k, GP * g0 + PTS * s0 + n:GP * g0 + PTS * s0 + n + 1]
                G, U = g1 - g0, s1 - s0
                src = bass.AP(at.tensor, at.offset, [at.ap[0], [GP, G], [1, K], [PTS, U]])
                cbc = bass.AP(ctr.tensor, ctr.offset, [ctr.ap[0], [GP, G], [0, K], [PTS, U]])
                last = eng.tensor_tensor(QT[:, k, g0:g1, n * K:(n + 1) * K, s0:s1], src, cbc, ALU.subtract)
                last.then_inc(sem_, 1)
            U = 2 if n < LEAD - PTS else 1
            at = ext[:, k, K * n:K * n + 1]
            ctr = cen[:, k, n:n + 1]
            src = bass.AP(at.tensor, at.offset, [at.ap[0], [1, K], [K * PTS, U]])
            cbc = bass.AP(ctr.tensor, ctr.offset, [ctr.ap[0], [0, K], [PTS, U]])
            eng.tensor_tensor(QT[:, k, 0, n * K:(n + 1) * K, 0:U], src, cbc, ALU.subtract).then_inc(sem_, 1)

        @block.sync
        def _(sp):
            sp.dma_start(ident[:, :], io["ident"][0:32, 0:32]).then_inc(const_in, 16)
            sp.dma_start(rep[:, :], io["rep"]).then_inc(const_in, 16)
            sp.dma_start(place[:, :], io["place"]).then_inc(const_in, 16)

            def step(k, at):
                if at(0):
                    b, _ = at(0)
                    sp.wait_ge(f_used, b + 1)
                    sp.dma_start(fb[:, k % 2, :], feats[bass.ds(b * C, C), :]).then_inc(f_in[k % 2], 16)
                if at(2):
                    (b, _), k = at(2), (k - 2) % 4
                    sp.wait_ge(q_v, b * QV + 5 * QV)
                    sp.wait_ge(q_g, b * QG + 5 * QG)
                    sp.dma_start(scratch["q16"][bass.ds(b * GROUPS, GROUPS), :, :].rearrange("g p x -> p g x"),
                                 QT[:, k, :, :, :].rearrange("p g x s -> p g (x s)")).then_inc(q_out[k], 16)
                    sp.dma_start(scratch["c16"][bass.ds(b * GROUPS, GROUPS), :, :].rearrange("g p x -> p g x"),
                                 cen16[:, k, :].rearrange("p (g x) -> p g x", g=GROUPS)).then_inc(q_out[k], 16)

            steps(sp, step, B, 4)
            for k in range(4):
                sp.wait_ge(q_out[k], 32 * (B // 4) + 32)

        @block.gpsimd
        def _(pool):
            nc.gpsimd.memset(QT[:, :, :, :, :], 0.0).then_inc(zeroed, 1)
            nc.gpsimd.memset(cen[:, :, :], 0.0).then_inc(zeroed, 1)
            nc.gpsimd.memset(cen16[:, :, :], 0.0).then_inc(zeroed, 1)
            pool.wait_ge(zeroed, 5)
            for k in range(4):
                pool.sem_inc(q_out[k], 32)
            pool.sem_inc(q_g, 4 * QG)

            def step(k, at):
                if at(1):
                    (b, i), k = at(1), (k - 1) % 4
                    pool.wait_ge(ext_ready, b + 3)
                    pool.wait_ge(cen_ready, b + 3)
                    pool.wait_ge(q_out[k], i * 32 + 32)
                    window_rows(nc.gpsimd, k, 1, q_g)

            steps(pool, step, B, 4)

        @block.vector
        def _(dve):
            v = nc.vector
            for hl in range(2):
                v.memset(FX[:, hl, :, :].bitcast(F32), 0.0).then_inc(zeroed, 1)
            dve.wait_ge(const_in, 48)
            dve.wait_ge(zeroed, 5)
            dve.sem_inc(l16_ready, 2)
            dve.sem_inc(q_v, 4 * QV)

            def step(k, at):
                if at(0):
                    (b, _), h = at(0), k % 2
                    dve.wait_ge(f_used, b + 3)
                    dve.wait_ge(gathered, b + 1)
                    v.tensor_copy(t16[:, h, :], ptok[:, h, 0:NT * C]).then_inc(t16_ready, 1)
                    dve.wait_ge(t16_ready, b + 1)
                    v.tensor_tensor(l16[:, h, :], ptok[:, h, 0:NT * C], t16[:, h, :],
                                    ALU.subtract).then_inc(l16_ready, 1)
                    dve.wait_ge(l16_ready, b + 3)
                    for hl, src in enumerate((t16, l16)):
                        fx = FX[:, hl, h, 0:1]
                        dst = bass.AP(fx.tensor, fx.offset, [fx.ap[0], [NT * 128 + 1, M], [M, NT * C]])
                        v.tensor_copy(dst, src[:, h, :].unsqueeze(1).to_broadcast([128, M, NT * C]))\
                            .then_inc(fx_ready, 1)
                    for m in range(M):
                        for t in range(NT):
                            v.tensor_scalar(onehot[:, h, m * NT + t, :], place[:, :],
                                            rank[:, bass.ds(b + perm[m] * B, 1), t], None,
                                            ALU.is_equal).then_inc(hot_ready, 1)
                if at(1):
                    (b, i), k = at(1), (k - 1) % 4
                    dve.wait_ge(ext_ready, b + 3)
                    dve.wait_ge(cen_ready, b + 3)
                    dve.wait_ge(q_out[k], i * 32 + 32)
                    window_rows(v, k, 0, q_v)
                    window_rows(v, k, 2, q_v)

            steps(dve, step, B, 4)

        @block.tensor
        def _(pe):
            pe.wait_ge(const_in, 48)
            pe.sem_inc(f_used, 2)
            pe.sem_inc(gathered, 2)

            def step(k, at):
                if at(0):
                    (b, i), h = at(0), k % 2
                    pe.wait_ge(f_in[h], i * 32 + 16 * (k // 2 + 1))
                    pe.wait_ge(l16_ready, b + 1)
                    pe.wait_ge(cen_ready, b + 1)
                    nc.tensor.matmul(pcen[:, h, 0:N], rep[:, :], fb[:, h, :], start=True, stop=True)
                    for t in range(NT):
                        last = nc.tensor.transpose(ptok[:, h, t * C:(t + 1) * C],
                                                   fb[:, h, t * 128:(t + 1) * 128], ident[:, :])
                    last.then_inc(f_used, 1)
                if at(1):
                    (b, _), k = at(1), (k - 1) % 4
                    h = k % 2
                    pe.wait_ge(fx_ready, b * 2 + 2)
                    pe.wait_ge(hot_ready, b * M * NT + M * NT)
                    pe.wait_ge(ext_ready, b + 1)
                    for e in range(2):
                        for n in range(2 * M * NT):
                            hl, mt = n // (M * NT), n % (M * NT)
                            last = nc.tensor.matmul(pext[:, h, e, 0:H2], FX[:, hl, h, mt * 128:(mt + 1) * 128],
                                                    onehot[:, h, mt, e * H2:(e + 1) * H2],
                                                    start=n == 0, stop=n == 2 * M * NT - 1)
                    last.then_inc(gathered, 1)

            steps(pe, step, B, 4)

        @block.scalar
        def _(act):
            act.sem_inc(cen_ready, 2)
            act.sem_inc(ext_ready, 2)
            act.wait_ge(zeroed, 5)

            def step(k, at):
                if at(0):
                    b, i = at(0)
                    act.wait_ge(q_out[k], i * 32 + 32)
                    act.wait_ge(q_v, b * QV + QV)
                    act.wait_ge(q_g, b * QG + QG)
                    act.wait_ge(f_used, b + 3)
                    for s0, n0, n1 in ((0, 0, LEAD), (LEAD + 1, LEAD, N)):
                        nc.scalar.activation(cen16[:, k, s0:s0 + n1 - n0], pcen[:, k % 2, n0:n1], ACT.Copy)
                        last = nc.scalar.activation(cen[:, k, s0:s0 + n1 - n0], pcen[:, k % 2, n0:n1], ACT.Copy)
                    last.then_inc(cen_ready, 1)
                if at(1):
                    (b, _), k = at(1), (k - 1) % 4
                    act.wait_ge(gathered, b + 3)
                    act.wait_ge(q_v, b * QV + QV)
                    act.wait_ge(q_g, b * QG + QG)
                    nc.scalar.activation(ext[:, k, :].rearrange("p (e x) -> p e x", e=2), pext[:, k % 2, :, 0:H2],
                                         ACT.Copy).then_inc(ext_ready, 1)

            steps(act, step, B, 4)


def window_attention(nc, io, scratch, layer, O, W, hmax, stat):
    T = B * GROUPS
    NB = 4
    SB = 512 // O if O * SUBS > 512 else SUBS
    NVB = -(-SUBS // SB)
    with ExitStack() as ctx:
        def sb(name, shape, dt=F32):
            return ctx.enter_context(nc.sbuf_tensor(name + layer, shape, dt))

        def ps(name, shape):
            return ctx.enter_context(nc.psum_tensor(name + layer, shape, F32))

        used = []

        def sem(name):
            used.append(ctx.enter_context(nc.semaphore(name + "_wa" + layer)))
            return used[-1]

        maskL = sb("maskL", [PTS, 128], F16)
        maskR = sb("maskR", [PTS, GC], F16)
        QX = sb("QX", [128, NB, 4 * GC], F16)
        QR = sb("QR", [128, NB, GC], F16)
        CT = sb("CT", [128, NB, GP], F16)
        mx = sb("mx", [128, 2, SUBS])
        Dm = sb("Dm", [128, 2, GC])
        E = sb("E", [128, 2, GC])
        Z = sb("Z", [128, 2, SUBS])
        R = sb("R", [128, 2, SUBS])
        A = sb("Ap", [128, 2, GC])
        AT = sb("AT", [128, 2, GC])
        Vs = sb("Vs", [128, NB, SUBS * O])
        Hs = sb("Hs", [O, 2, SUBS * PTS * K])
        junk = sb("junk", [O, 2, SUBS * PTS * K])
        pS = ps("pS", [128, 2, 512])
        pV = ps("pV", [128, 2, NVB, 512])
        pH = ps("pH", [128, 2, 512])

        const_in = sem("const_in")
        zeroed = sem("zeroed")
        q_in = [sem(f"q_in{k}") for k in range(NB)]
        c_in = [sem(f"c_in{k}") for k in range(NB)]
        scored = sem("scored")
        shifted = sem("shifted")
        projected = sem("projected")
        max_ready = sem("max_ready")
        exped = sem("exped")
        summed = sem("summed")
        r_ready = sem("r_ready")
        probs = sem("probs")
        turned = sem("turned_p")
        vs_ready = sem("vs_ready")
        mixed = sem("mixed")
        hmax_done = sem("hmax_done")
        copied = sem("copied")
        squared = sem("squared")
        ctx.callback(clear, nc, used)
        block = ctx.enter_context(nc.Block())

        @block.sync
        def _(sp):
            sp.dma_start(maskL[:, :], io["maskL"]).then_inc(const_in, 16)
            sp.dma_start(maskR[:, :], io["maskR"]).then_inc(const_in, 16)
            sp.wait_ge(zeroed, 1)

            def step(k, at):
                if at(0):
                    t, _ = at(0)
                    sp.wait_ge(projected, t + 1)
                    src = scratch["q16"][bass.ds(t, 1), :, :].rearrange("g p x -> (g p) x")
                    for h in range(4):
                        sp.dma_start(QX[32 * h:32 * h + 32, k, h * GC:(h + 1) * GC],
                                     src[32 * h:32 * h + 32, :]).then_inc(q_in[k], 16)
                    sp.dma_start(QR[:, k, :], src).then_inc(q_in[k], 16)
                if at(3):
                    t, _ = at(3)
                    sp.wait_ge(mixed, t + 1)
                    sp.dma_start(CT[:, (k - 3) % NB, :], scratch["c16"][bass.ds(t, 1), :, :]
                                 .rearrange("g p x -> (g p) x")).then_inc(c_in[(k - 3) % NB], 16)

            steps(sp, step, T, NB)

        @block.tensor
        def _(pe):
            pe.sem_inc(projected, NB)
            pe.sem_inc(mixed, NB)
            pe.wait_ge(const_in, 32)

            def step(k, at):
                if at(0):
                    t, r = at(0)
                    p = k % 2
                    qx = [QX[:, k, :].rearrange("p (c s) -> p c s", s=SUBS)[:, :, u] for u in range(SUBS)]
                    qr = [QR[:, k, :].rearrange("p (c s) -> p c s", s=SUBS)[:, :, u] for u in range(SUBS)]
                    pe.wait_ge(q_in[k], r * 80 + 80)
                    pe.wait_ge(shifted, t + 1)
                    nc.tensor.matmul(pS[:, p, 0:GC], maskL[:, :], maskR[:, :], start=True, stop=False)
                    for u in range(SUBS):
                        last = nc.tensor.matmul(pS[:, p, 32 * u:32 * u + 32], qx[u], qr[u],
                                                start=False, stop=u == SUBS - 1)
                    last.then_inc(scored, 1)
                    pe.wait_ge(vs_ready, t + 1)
                    for u in range(SUBS):
                        o = (u % SB) * O
                        nc.tensor.matmul(pV[:, p, u // SB, o:o + O], qx[u], W["neigh_hi"][:, 0:O], start=True, stop=False)
                        last = nc.tensor.matmul(pV[:, p, u // SB, o:o + O], qx[u], W["neigh_lo"][:, 0:O],
                                                start=False, stop=True)
                    last.then_inc(projected, 1)
                if at(3):
                    t, r = at(3)
                    p, k3 = (k - 3) % 2, (k - 3) % NB
                    pe.wait_ge(c_in[k3], r * 16 + 16)
                    pe.wait_ge(copied, t + 1)
                    out = pH[0:O, p, 0:GC].rearrange("p (s x) -> p s x", x=32)[:, :, 0:PTS * K]\
                        .rearrange("p s (n j) -> p s n j", n=PTS)
                    ctr = CT[:, k3, :].rearrange("p (s n) -> p s n", n=PTS).unsqueeze(3)\
                        .to_broadcast([128, SUBS, PTS, K])
                    nc.tensor.matmul(out, W["center_hi"][:, 0:O], ctr, start=True, stop=False)
                    nc.tensor.matmul(out, W["center_lo"][:, 0:O], ctr, start=False, stop=False)
                    pe.wait_ge(vs_ready, t + 3)
                    pe.wait_ge(turned, t + 3)
                    for u in range(SUBS):
                        last = nc.tensor.matmul(pH[0:O, p, 32 * u:32 * u + PTS * K], Vs[:, k3, u * O:(u + 1) * O],
                                                AT[:, p, 32 * u:32 * u + PTS * K], start=False, stop=u == SUBS - 1)
                    last.then_inc(mixed, 1)

            steps(pe, step, T, NB)

        @block.vector
        def _(dve):
            v = nc.vector
            v.memset(QX[:, :, :].bitcast(F32), 0.0).then_inc(zeroed, 1)
            dve.sem_inc(shifted, 2)
            dve.sem_inc(turned, 2)
            dve.sem_inc(hmax_done, 2)

            def step(k, at):
                if at(0):
                    t, r = at(0)
                    p = k % 2
                    dve.wait_ge(scored, t + 1)
                    sc = pS[:, p, 0:GC].rearrange("p (s x) -> p s x", x=32)
                    v.tensor_reduce(mx[:, p, :], sc, X, ALU.max).then_inc(max_ready, 1)
                    dve.wait_ge(max_ready, t + 1)
                    dve.wait_ge(exped, t + 1)
                    v.tensor_tensor(Dm[:, p, :].rearrange("p (s x) -> p s x", x=32), sc,
                                    mx[:, p, :].unsqueeze(2).to_broadcast([128, SUBS, 32]),
                                    ALU.subtract).then_inc(shifted, 1)
                if at(1):
                    t, r = at(1)
                    p = (k - 1) % 2
                    dve.wait_ge(exped, t + 3)
                    v.tensor_reduce(Z[:, p, :], E[:, p, :].rearrange("p (s x) -> p s x", x=32), X,
                                    ALU.add).then_inc(summed, 1)
                    dve.wait_ge(summed, t + 1)
                    v.reciprocal(R[:, p, :], Z[:, p, :]).then_inc(r_ready, 1)
                if at(2):
                    t, r = at(2)
                    p = k % 2
                    dve.wait_ge(probs, t + 3)
                    dve.wait_ge(mixed, t + 3)
                    v.transpose(AT[:, p, :], A[:, p, :]).then_inc(turned, 1)
                if at(4):
                    t, r = at(4)
                    p = k % 2
                    dve.wait_ge(copied, t + 3)
                    dve.wait_ge(squared, t + 3)
                    v.tensor_reduce(hmax[0:O, bass.ds(t * GP, GP)],
                                    Hs[:, p, :].rearrange("p (n j) -> p n j", j=K), X, ALU.max).then_inc(hmax_done, 1)

            steps(dve, step, T, NB)

        @block.gpsimd
        def _(pool):
            pool.sem_inc(probs, 2)

            def step(k, at):
                if at(1):
                    t, r = at(1)
                    p = (k - 1) % 2
                    pool.wait_ge(r_ready, t + 1)
                    pool.wait_ge(turned, t + 1)
                    nc.gpsimd.tensor_tensor(A[:, p, :].rearrange("p (s x) -> p s x", x=32),
                                            E[:, p, :].rearrange("p (s x) -> p s x", x=32),
                                            R[:, p, :].unsqueeze(2).to_broadcast([128, SUBS, 32]),
                                            ALU.mult).then_inc(probs, 1)

            steps(pool, step, T, NB)

        @block.scalar
        def _(act):
            act.sem_inc(vs_ready, 2)
            act.sem_inc(exped, 2)
            act.sem_inc(copied, 2)
            act.sem_inc(squared, 2)

            def step(k, at):
                if at(4):
                    t, r = at(4)
                    p = k % 2
                    rows = pH[0:O, p, 0:GC].rearrange("p (s x) -> p s x", x=32)[:, :, 0:PTS * K]
                    act.wait_ge(mixed, t + 1 + NB)
                    act.wait_ge(hmax_done, t + 1)
                    nc.scalar.activation(Hs[:, p, :].rearrange("p (s x) -> p s x", x=PTS * K), rows, ACT.Copy,
                                         accum_out=stat[0:O, 0, bass.ds(t, 1)]).then_inc(copied, 1)
                    act.wait_ge(copied, t + 3)
                    act.wait_ge(squared, t + 1)
                    nc.scalar.activation(junk[:, p, :], Hs[:, p, :], ACT.Square,
                                         accum_out=stat[0:O, 1, bass.ds(t, 1)]).then_inc(squared, 1)
                if at(0):
                    t, r = at(0)
                    p = k % 2
                    act.wait_ge(shifted, t + 3)
                    act.wait_ge(probs, t + 1)
                    nc.scalar.activation(E[:, p, :], Dm[:, p, :], ACT.Exp, scale=32.0 ** -0.5).then_inc(exped, 1)
                    act.wait_ge(projected, t + 1 + NB)
                    act.wait_ge(mixed, t + 1)
                    if NVB == 1:
                        nc.scalar.activation(Vs[:, k, :], pV[:, p, 0, 0:SUBS * O], ACT.Copy).then_inc(vs_ready, 1)
                    else:
                        nc.scalar.activation(Vs[:, k, 0:SB * O], pV[:, p, 0, 0:SB * O], ACT.Copy)
                        nc.scalar.activation(Vs[:, k, SB * O:], pV[:, p, 1, 0:(SUBS - SB) * O],
                                             ACT.Copy).then_inc(vs_ready, 1)

            steps(act, step, T, NB)


def instance_norm(nc, io, scratch, layer, O, W, hmax, stat, dst):
    with ExitStack() as ctx:
        def sb(name, shape, dt=F32):
            return ctx.enter_context(nc.sbuf_tensor(name + layer, shape, dt))

        used = []

        def sem(name):
            used.append(ctx.enter_context(nc.semaphore(name + "_in" + layer)))
            return used[-1]

        tot = sb("tot", [O, 2, B])
        mean = sb("mean", [O, B])
        var = sb("var", [O, B])
        root = sb("root", [O, B])
        rstd = sb("rstd_i", [O, B])
        tmp = sb("tmp_i", [O, B])
        var_ready = sem("var_ready_i")
        root_ready = sem("root_ready_i")
        y_ready = sem("y_ready")
        stored = sem("stored_i")
        v_chain = sem("v_chain_i")
        y = hmax
        ctx.callback(clear, nc, used)
        block = ctx.enter_context(nc.Block())

        @block.scalar
        def _(act):
            act.wait_ge(var_ready, 1)
            nc.scalar.activation(root[:, :], var[:, :], ACT.Sqrt).then_inc(root_ready, 1)

        @block.vector
        def _(dve):
            v = nc.vector
            link = chain(dve, v_chain)
            amax, bias = W["amax"][0:O, :], W["bias"][0:O, :]
            link(v.tensor_reduce(tot[:, :, :], stat[0:O, :, :].rearrange("p a (b g) -> p a b g", g=GROUPS), X, ALU.add))
            link(v.tensor_scalar(tot[:, :, :], tot[:, :, :], 1.0 / (N * K), None, ALU.mult))
            link(v.tensor_tensor(tmp[:, :], tot[:, 0, :], tot[:, 0, :], ALU.mult))
            link(v.tensor_tensor(var[:, :], tot[:, 1, :], tmp[:, :], ALU.subtract))
            link(v.tensor_scalar(var[:, :], var[:, :], 0.0, amax, ALU.max, ALU.mult))
            v.tensor_scalar(var[:, :], var[:, :], amax, EPS, ALU.mult, ALU.add).then_inc(var_ready, 1)
            dve.wait_ge(root_ready, 1)
            inverse_root(v, link, rstd[:, :], var[:, :], root[:, :], tmp[:, :])
            link(v.tensor_scalar(mean[:, :], tot[:, 0, :], amax, bias, ALU.mult, ALU.add))
            flat = y[0:O, :]
            link(v.tensor_scalar(flat, flat, amax, bias, ALU.mult, ALU.add))
            for b in range(B):
                link(v.tensor_scalar(y[0:O, b * PADN:(b + 1) * PADN], y[0:O, b * PADN:(b + 1) * PADN],
                                     mean[:, b:b + 1], rstd[:, b:b + 1], ALU.subtract, ALU.mult))
            v.scalar_tensor_tensor(flat, flat, SLOPE, flat, ALU.mult, ALU.max).then_inc(y_ready, 1)

        @block.sync
        def _(sp):
            sp.wait_ge(y_ready, 1)
            yb = y[0:O, :].rearrange("p (b s) -> p b s", b=B)
            for s0, n0, n1 in ((0, 0, LEAD), (LEAD + 1, LEAD, N)):
                sp.dma_start(dst[:, :, n0:n1], yb[:, :, s0:s0 + n1 - n0]).then_inc(stored, 16)
            sp.wait_ge(stored, 32)


def join_features(nc, io, scratch):
    with ExitStack() as ctx:
        def sb(name, shape, dt=F32):
            return ctx.enter_context(nc.sbuf_tensor(name, shape, dt))

        used = []

        def sem(name):
            used.append(ctx.enter_context(nc.semaphore(name)))
            return used[-1]

        f0 = sb("f0_j", [C, B, N])
        f1 = sb("f1_j", [C, B, N])
        f2 = sb("f2_j", [2 * C, B, N])
        lat = sb("lat_j", [S, B, D])
        w0 = sb("w0_j", [C, C])
        w1 = sb("w1_j", [C, C])
        w2 = sb("w2_j", [2 * C, C])
        h = sb("h_j", [C, B, N])
        st = sb("st_j", [C, B, 6])
        mv = sb("mv_j", [C, B, 2])
        root = sb("root_j", [C, B])
        rstd = sb("rstd_j", [C, B])
        var = sb("var_j", [C, B])
        tmp = sb("tmp_j", [C, B])
        ph = ctx.enter_context(nc.psum_tensor("ph_j", [C, 4, 512], F32))
        w_in = sem("w_in_j")
        f_in = sem("f_in_j")
        lat_in = sem("lat_in_j")
        joined = sem("joined")
        copied = sem("copied_j")
        var_ready = sem("var_ready_j")
        root_ready = sem("root_ready_j")
        x_ready = sem("x_ready_j")
        stored = sem("stored_j")
        v_chain = sem("v_chain_j")
        ctx.callback(clear, nc, used)
        block = ctx.enter_context(nc.Block())

        @block.sync
        def _(sp):
            sp.dma_start(w0[:, :], io["conv3T"][0:C, :]).then_inc(w_in, 16)
            sp.dma_start(w1[:, :], io["conv3T"][C:2 * C, :]).then_inc(w_in, 16)
            sp.dma_start(w2[:, :], io["conv3T"][2 * C:4 * C, :]).then_inc(w_in, 16)
            sp.dma_start(f0[:, :, :], scratch["f0"].rearrange("(b c) n -> c b n", c=C)).then_inc(f_in, 16)
            sp.dma_start(f1[:, :, :], scratch["f1"].rearrange("(b c) n -> c b n", c=C)).then_inc(f_in, 16)
            sp.dma_start(f2[:, :, :], scratch["f2"]).then_inc(f_in, 16)
            sp.dma_start(lat[:, :, :], io["x"].rearrange("(b s) d -> s b d", s=S)).then_inc(lat_in, 16)
            sp.wait_ge(x_ready, 1)
            sp.dma_start(scratch["x1"].rearrange("(b s) d -> s b d", s=S), h[:, :, :]).then_inc(stored, 16)
            sp.wait_ge(stored, 16)

        @block.tensor
        def _(pe):
            pe.wait_ge(w_in, 48)
            pe.wait_ge(f_in, 48)
            for b in range(B):
                if b >= 4:
                    pe.wait_ge(copied, b - 3)
                nc.tensor.matmul(ph[:, b % 4, :], w0[:, :], f0[:, b, :], start=True, stop=False)
                nc.tensor.matmul(ph[:, b % 4, :], w1[:, :], f1[:, b, :], start=False, stop=False)
                nc.tensor.matmul(ph[:, b % 4, :], w2[:, :], f2[:, b, :], start=False, stop=True).then_inc(joined, 1)

        @block.scalar
        def _(act):
            for b in range(B):
                act.wait_ge(joined, b + 1)
                nc.scalar.activation(h[:, b, :], ph[:, b % 4, :], ACT.Copy).then_inc(copied, 1)
            act.wait_ge(var_ready, 1)
            nc.scalar.activation(root[:, :], var[:, :], ACT.Sqrt).then_inc(root_ready, 1)

        @block.vector
        def _(dve):
            v = nc.vector
            link = chain(dve, v_chain)
            for b in range(B):
                dve.wait_ge(copied, b + 1)
                link(v.bn_stats(st[:, b, :], h[:, b, :]))
                link(v.bn_aggr(mv[:, b, :], st[:, b, :]))
            v.tensor_scalar(var[:, :], mv[:, :, 1], EPS, None, ALU.add).then_inc(var_ready, 1)
            dve.wait_ge(root_ready, 1)
            inverse_root(v, link, rstd[:, :], var[:, :], root[:, :], tmp[:, :])
            for b in range(B):
                link(v.tensor_scalar(h[:, b, :], h[:, b, :], mv[:, b, 0:1], rstd[:, b:b + 1],
                                     ALU.subtract, ALU.mult))
            link(v.scalar_tensor_tensor(h[:, :, :], h[:, :, :], SLOPE, h[:, :, :], ALU.mult, ALU.max))
            dve.wait_ge(lat_in, 16)
            v.tensor_tensor(h[:, :, :], h[:, :, :], lat[:, :, :], ALU.add).then_inc(x_ready, 1)


def cross_attention(nc, io, scratch):
    with ExitStack() as ctx:
        def sb(name, shape, dt=F32):
            return ctx.enter_context(nc.sbuf_tensor(name, shape, dt))

        rank = sb("rank", [128, M * B, NT])
        norm_and_keys(nc, io, scratch)
        ranks(nc, io, scratch, rank)
        f1 = scratch["f1"]
        for layer, O, feats, perm, dst in (
                ("1", C, scratch["f0"], (2, 0, 3, 1), f1.rearrange("(b c) n -> c b n", c=C)),
                ("2", 2 * C, f1, (1, 3, 0, 2), scratch["f2"])):
            with ExitStack() as lctx:
                def lsb(name, shape, dt=F32):
                    return lctx.enter_context(nc.sbuf_tensor(name + layer, shape, dt))

                W = {n: lsb(n, [128, O], F16) for n in ("neigh_hi", "neigh_lo", "center_hi", "center_lo")}
                W["amax"] = lsb("amax", [O, 1])
                W["bias"] = lsb("bias", [O, 1])
                hmax = lsb("hmax", [O, B * PADN])
                stat = lsb("stat", [O, 2, B * GROUPS])
                fold_weights(nc, io, layer, O, W)
                gather_windows(nc, io, scratch, layer, feats, perm, rank)
                window_attention(nc, io, scratch, layer, O, W, hmax, stat)
                instance_norm(nc, io, scratch, layer, O, W, hmax, stat, dst)
        join_features(nc, io, scratch)


def row_norm(nc, v, link, act_sqrt, src, dst, st, mv, tmp):
    for t in range(TT):
        link(v.bn_stats(st[:, t, :], src[:, t, :]))
        link(v.bn_aggr(mv[:, t, :], st[:, t, :]))
    root, rstd, rtmp = (tmp[:, i, :] for i in range(3))
    act_sqrt(v.tensor_scalar(mv[:, :, 1], mv[:, :, 1], EPS, None, ALU.add))
    inverse_root(v, link, rstd, mv[:, :, 1], root, rtmp)
    for t in range(TT):
        link(v.tensor_scalar(dst[:, t, :], src[:, t, :], mv[:, t, 0:1], rstd[:, t:t + 1],
                             ALU.subtract, ALU.mult))


def mamba_prepare(nc, io, scratch, P):
    with ExitStack() as ctx:
        def sb(name, shape, dt=F32):
            return ctx.enter_context(nc.sbuf_tensor(name, shape, dt))

        used = []

        def sem(name):
            used.append(ctx.enter_context(nc.semaphore(name)))
            return used[-1]

        ident = sb("ident_p", [128, 128])
        later = sb("later", [128, 128])
        upto = sb("upto", [128, S])
        x1 = sb("x1_p", [128, TT, D])
        xin = sb("xin", [128, TT, D])
        hn = sb("hn", [128, TT, D])
        st = sb("st_p", [128, TT, 6])
        mv = sb("mv_p", [128, TT, 2])
        tmp = sb("tmp_p", [128, 3, TT])
        ms = sb("ms_p", [128, 3, TT])
        nw = sb("nw", [128, DT])
        wdt = sb("wdt", [128, DT, 128])
        hp = sb("hp", [128, 2])
        aneg = sb("aneg", [128, 1])
        sp_ = sb("sp", [128, 6, TOK])
        dta = sb("dta", [128, 2, TOK])
        atok = sb("atok", [128, TT, HEADS])
        R = sb("R_p", [128, 2, HEADS, S])
        pt = ctx.enter_context(nc.psum_tensor("pt_p", [128, 4, 512], F32))
        pd = ctx.enter_context(nc.psum_tensor("pd_p", [128, 512], F32))
        pz = ctx.enter_context(nc.psum_tensor("pz_p", [128, 2, 512], F32))
        x_in = sem("x_in_p")
        w_in = sem("w_in_p")
        var_ready = sem("var_ready_p")
        root_ready = sem("root_ready_p")
        xin_ready = sem("xin_ready")
        squares = sem("squares_p")
        ms_ready = sem("ms_ready")
        ms_root = sem("ms_root")
        hn_ready = sem("hn_ready")
        turned = sem("turned_h")
        hT_ready = sem("hT_ready")
        dt_raw = sem("dt_raw")
        z_ready = sem("z_ready_p")
        exp_ready = sem("exp_ready_p")
        one_ready = sem("one_ready")
        ln_ready = sem("ln_ready")
        dta_ready = sem("dta_ready")
        dta_turned = sem("dta_turned")
        r_ready = sem("r_ready_p")
        seg_ready = sem("seg_ready")
        decay_ready = sem("decay_ready")
        v_chain = sem("v_chain_p")
        ctx.callback(clear, nc, used)
        block = ctx.enter_context(nc.Block())

        @block.sync
        def _(sp):
            sp.dma_start(x1[:, :, :], scratch["x1"].rearrange("(t p) d -> p t d", p=128)).then_inc(x_in, 16)
            for dst, src in ((P["conv"][:, :], io["conv"]), (ident[:, :], io["ident"]), (later[:, :], io["later"]), (upto[:, :], io["upto"]),
                             (nw[:, :], io["norm_w"]), (wdt[:, :, :], io["in_proj"][2 * CT_ + 2 * GR]),
                             (hp[:, :], io["head_par"])):
                sp.dma_start(dst, src).then_inc(w_in, 16)

        @block.scalar
        def _(act):
            act.wait_ge(var_ready, 1)
            nc.scalar.activation(tmp[:, 0, :], mv[:, :, 1], ACT.Sqrt).then_inc(root_ready, 1)
            act.wait_ge(xin_ready, 1)
            for t in range(TT):
                last = nc.scalar.activation(hn[:, t, :], xin[:, t, :], ACT.Square, accum_out=ms[:, 0, t:t + 1])
            last.then_inc(squares, 1)
            act.wait_ge(ms_ready, 1)
            nc.scalar.activation(ms[:, 1, :], ms[:, 0, :], ACT.Sqrt).then_inc(ms_root, 1)
            act.wait_ge(w_in, 112)
            nc.scalar.activation(aneg[:, :], hp[:, 1:2], ACT.Exp)
            act.wait_ge(z_ready, 1)
            nc.scalar.activation(sp_[:, 2, :], sp_[:, 1, :], ACT.Exp, scale=-1.0).then_inc(exp_ready, 1)
            act.wait_ge(one_ready, 1)
            nc.scalar.activation(sp_[:, 4, :], sp_[:, 3, :], ACT.Ln).then_inc(ln_ready, 1)
            for n in range(TT * 8):
                q, c = n // 8, n % 8
                act.wait_ge(seg_ready, n + 1)
                nc.scalar.activation(P["decay"][:, q, 16 * c:16 * c + 16, :].rearrange("p h i -> p (h i)"),
                                     pz[:, n % 2, :], ACT.Exp).then_inc(decay_ready, 1)

        @block.vector
        def _(dve):
            v = nc.vector
            link = chain(dve, v_chain)
            dve.wait_ge(x_in, 16)

            def act_sqrt(ins):
                ins.then_inc(var_ready, 1)
                dve.wait_ge(root_ready, 1)

            row_norm(nc, v, link, act_sqrt, x1, xin, st, mv, tmp)
            v.tensor_tensor(P["acc"][:, :, :], x1[:, :, :], xin[:, :, :], ALU.add).then_inc(xin_ready, 1)
            dve.wait_ge(squares, 1)
            v.tensor_scalar(ms[:, 0, :], ms[:, 0, :], 1.0 / D, EPS, ALU.mult, ALU.add).then_inc(ms_ready, 1)
            dve.wait_ge(ms_root, 1)
            inverse_root(v, link, ms[:, 2, :], ms[:, 0, :], ms[:, 1, :], tmp[:, 2, :])
            for t in range(TT):
                last = v.tensor_scalar(hn[:, t, :], xin[:, t, :], ms[:, 2, t:t + 1], None, ALU.mult)
            last.then_inc(hn_ready, 1)
            dve.wait_ge(w_in, 112)
            for d in range(DT):
                dve.wait_ge(turned, d + 1)
                v.tensor_scalar(P["hT"][:, d, :], pt[:, d, :], nw[:, d:d + 1], None, ALU.mult).then_inc(hT_ready, 1)
            dve.wait_ge(dt_raw, 1)
            z, az, w, u, lu, d_ = (sp_[:, i, :] for i in range(6))
            link(v.tensor_scalar(z, pd[:, :], hp[:, 0:1], None, ALU.add))
            link(v.tensor_scalar(az, z, -1.0, None, ALU.mult))
            v.tensor_tensor(az, az, z, ALU.max).then_inc(z_ready, 1)
            dve.wait_ge(exp_ready, 1)
            v.tensor_scalar(u, w, 1.0, None, ALU.add).then_inc(one_ready, 1)
            dve.wait_ge(ln_ready, 1)
            link(v.tensor_scalar(d_, u, -1.0, None, ALU.add))
            link(v.tensor_scalar(az, d_, 0.0, None, ALU.is_equal))
            link(v.tensor_tensor(d_, d_, az, ALU.add))
            link(v.tensor_tensor(lu, lu, az, ALU.add))
            link(v.reciprocal(u, d_))
            link(v.tensor_tensor(lu, lu, u, ALU.mult))
            link(v.tensor_tensor(lu, lu, w, ALU.mult))
            link(v.scalar_tensor_tensor(dta[:, 0, :], z, 0.0, lu, ALU.max, ALU.add))
            v.tensor_scalar(dta[:, 1, :], dta[:, 0, :], aneg[:, 0:1], -1.0, ALU.mult, ALU.mult).then_inc(dta_ready, 1)
            dve.wait_ge(dta_turned, 1)
            link(v.tensor_copy(P["dt"][:, :, :].rearrange("p q h -> p (q h)"), pt[:, 0, :]))
            link(v.tensor_copy(atok[:, :, :].rearrange("p q h -> p (q h)"), pt[:, 1, :]))
            for q in range(TT):
                if q >= 2:
                    dve.wait_ge(seg_ready, 8 * (q - 1))
                v.tensor_tensor(R[:, q % 2, :, :], atok[:, q, :].unsqueeze(2).to_broadcast([128, HEADS, S]),
                                upto[:, :].unsqueeze(1).to_broadcast([128, HEADS, S]), ALU.mult).then_inc(r_ready, 1)

        @block.tensor
        def _(pe):
            pe.wait_ge(w_in, 112)
            pe.wait_ge(hn_ready, 1)
            for d in range(DT):
                for t in range(TT):
                    last = nc.tensor.transpose(pt[:, d, t * 128:(t + 1) * 128], hn[:, t, d * 128:(d + 1) * 128],
                                               ident[:, :])
                last.then_inc(turned, 1)
            for d in range(DT):
                pe.wait_ge(hT_ready, d + 1)
                last = nc.tensor.matmul(pd[:, :], wdt[:, d, :], P["hT"][:, d, :], start=d == 0, stop=d == DT - 1)
            last.then_inc(dt_raw, 1)
            pe.wait_ge(dta_ready, 1)
            for i in range(2):
                for t in range(TT):
                    last = nc.tensor.transpose(pt[:, i, t * 128:(t + 1) * 128], dta[:, i, t * 128:(t + 1) * 128],
                                               ident[:, :])
            last.then_inc(dta_turned, 1)
            for n in range(TT * 8):
                q, c = n // 8, n % 8
                pe.wait_ge(r_ready, q + 1)
                if n >= 2:
                    pe.wait_ge(decay_ready, n - 1)
                nc.tensor.matmul(pz[:, n % 2, :], later[:, :],
                                 R[:, q % 2, 16 * c:16 * c + 16, :].rearrange("p h i -> p (h i)"),
                                 start=True, stop=True).then_inc(seg_ready, 1)


def conv_taps(v, dve, out, padded, par, tile, c_done, count):
    cw = [par[:, bass.ds(tile * 5 + i, 1)] for i in range(5)]
    v.tensor_scalar(out, padded[:, :, 0:S], cw[0], cw[4], ALU.mult, ALU.add).then_inc(c_done, 1)
    for i in range(1, TAPS):
        dve.wait_ge(c_done, count + i)
        v.scalar_tensor_tensor(out, padded[:, :, i:i + S], cw[i], out, ALU.mult, ALU.add).then_inc(c_done, 1)


def mamba_states(nc, io, scratch, P):
    with ExitStack() as ctx:
        def sb(name, shape, dt=F32):
            return ctx.enter_context(nc.sbuf_tensor(name, shape, dt))

        used = []

        def sem(name):
            used.append(ctx.enter_context(nc.semaphore(name)))
            return used[-1]

        NB = 2 * GR
        W = sb("W_s", [128, 2, DT, 128])
        XP = sb("XP_s", [128, 2, B, S + TAPS - 1])
        cv = sb("cv_s", [128, 2, B, S])
        BC = sb("BC", [128, 2 * GR, TOK])
        causal = sb("causal", [128, 128])
        pp = ctx.enter_context(nc.psum_tensor("pp_s", [128, 2, 512], F32))
        pc = ctx.enter_context(nc.psum_tensor("pc_s", [128, 2, 512], F32))
        c_in = sem("c_in_s")
        w_in = [sem("w_in_s0"), sem("w_in_s1")]
        zeroed = sem("zeroed_s")
        projected = sem("projected_s")
        padded = sem("padded_s")
        conved = sem("conved_s")
        silued = sem("silued_s")
        cb_ready = sem("cb_ready")
        cb_masked = sem("cb_masked")
        ctx.callback(clear, nc, used)
        block = ctx.enter_context(nc.Block())

        @block.sync
        def _(sp):
            sp.dma_start(causal[:, :], io["causal"]).then_inc(c_in, 16)

            def step(k, at):
                if at(0):
                    t, r = at(0)
                    sp.wait_ge(projected, t + 1)
                    sp.dma_start(W[:, k, :, :], io["in_proj"][bass.ds(t + 2 * CT_, 1), :, :, :]
                                 .rearrange("a p d o -> (a p) d o")).then_inc(w_in[k], 16)

            steps(sp, step, NB, 2)

        @block.tensor
        def _(pe):
            pe.sem_inc(projected, 2)

            def step(k, at):
                if at(0):
                    t, r = at(0)
                    pe.wait_ge(w_in[k], r * 16 + 16)
                    pe.wait_ge(padded, t + 1)
                    for d in range(DT):
                        last = nc.tensor.matmul(pp[:, k, :], W[:, k, d, :], P["hT"][:, d, :],
                                                start=d == 0, stop=d == DT - 1)
                    last.then_inc(projected, 1)

            steps(pe, step, NB, 2)
            pe.wait_ge(silued, NB + 2)
            for g in range(GR):
                if g >= 2:
                    pe.wait_ge(cb_masked, g - 1)
                for q in range(TT):
                    last = nc.tensor.matmul(pc[:, g % 2, q * 128:(q + 1) * 128], BC[:, g, q * 128:(q + 1) * 128],
                                            BC[:, GR + g, q * 128:(q + 1) * 128], start=True, stop=True)
                last.then_inc(cb_ready, 1)

        @block.scalar
        def _(act):
            act.wait_ge(zeroed, 1)
            act.sem_inc(padded, 2)
            act.sem_inc(silued, 2)

            def step(k, at):
                if at(0):
                    t, r = at(0)
                    act.wait_ge(projected, t + 3)
                    act.wait_ge(conved, t * TAPS + TAPS)
                    nc.scalar.activation(XP[:, k, :, TAPS - 1:], pp[:, k, :].rearrange("p (b s) -> p b s", b=B),
                                         ACT.Copy).then_inc(padded, 1)
                if at(1):
                    (t, r), k = at(1), 1 - k
                    act.wait_ge(conved, t * TAPS + 3 * TAPS)
                    nc.scalar.activation(BC[:, bass.ds(t, 1), :].rearrange("p a t -> p (a t)"),
                                         cv[:, k, :, :].rearrange("p b s -> p (b s)"), ACT.Silu).then_inc(silued, 1)

            steps(act, step, NB, 2)

        @block.vector
        def _(dve):
            v = nc.vector
            v.memset(XP[:, :, :, :], 0.0).then_inc(zeroed, 1)
            dve.sem_inc(conved, 2 * TAPS)

            def step(k, at):
                if at(0):
                    t, r = at(0)
                    dve.wait_ge(padded, t + 3)
                    dve.wait_ge(silued, t + 1)
                    conv_taps(v, dve, cv[:, k, :, :], XP[:, k, :, :], P["conv"], t + CT_, conved,
                              t * TAPS + 2 * TAPS)

            steps(dve, step, NB, 2)
            dve.wait_ge(c_in, 16)
            for g in range(GR):
                dve.wait_ge(cb_ready, g + 1)
                v.tensor_tensor(P["cb"][:, g, :, :], pc[:, g % 2, :].rearrange("p (q i) -> p q i", q=TT),
                                causal[:, :].unsqueeze(1).to_broadcast([128, TT, 128]), ALU.mult)\
                    .then_inc(cb_masked, 1)


def mamba_mix(nc, io, scratch, P):
    T, U = CT_, TPG
    with ExitStack() as ctx:
        def sb(name, shape, dt=F32):
            return ctx.enter_context(nc.sbuf_tensor(name, shape, dt))

        def ps(name, shape):
            return ctx.enter_context(nc.psum_tensor(name, shape, F32))

        used = []

        def sem(name):
            used.append(ctx.enter_context(nc.semaphore(name)))
            return used[-1]

        ident = sb("ident_m", [128, 128])
        ones = sb("ones_m", [128, 1])
        zero = sb("zero_m", [128, 1])
        chan = sb("chan", [128, 2, CT_])
        Wg = sb("Wg", [128, 2, DT, 128])
        Wh = sb("Wh", [128, 2, DT, 128])
        Wo = sb("Wo", [128, 2, D])
        XP = sb("XP_m", [128, 2, B, S + TAPS - 1])
        cv = sb("cv_m", [128, 2, B, S])
        sg = sb("sg", [128, 4, TOK])
        hid = sb("hid", [128, 4, TOK])
        hc = sb("hc", [128, 2, TT, 2, HD])
        MT = sb("MT", [128, 2, 2, TT, 128])
        y = sb("y_m", [128, 2, TOK])
        yg = sb("yg", [128, 2, TOK])
        sq = sb("sq", [128, 2, TOK])
        sqsum = sb("sqsum", [128, 2, TOK])
        yw = sb("yw", [128, 2, TOK])
        rms = sb("rms", [128, 4, TT])
        pG = ps("pG", [128, 512])
        pX = ps("pX", [128, 512])
        pT = ps("pT", [128, 512])
        pY = ps("pY", [128, 512])
        pO = ps("pO", [128, 4, 512])

        const_in = sem("const_in_m")
        zeroed = sem("zeroed_m")
        g_in = [sem("g_in0"), sem("g_in1")]
        h_in = [sem("h_in0"), sem("h_in1")]
        o_in = [sem("o_in0"), sem("o_in1")]
        gate_mm = sem("gate_mm")
        hid_mm = sem("hid_mm")
        gate_silu = sem("gate_silu")
        padded = sem("padded_m")
        conved = sem("conved_m")
        hid_silu = sem("hid_silu")
        hid_turned = sem("hid_turned")
        hc_ready = sem("hc_ready")
        mt_ready = sem("mt_ready")
        mixed = sem("mixed_m")
        y_ready = sem("y_ready_m")
        yg_ready = sem("yg_ready")
        sq_ready = sem("sq_ready")
        sq_summed = sem("sq_summed")
        yw_ready = sem("yw_ready")
        out_mm = sem("out_mm")
        ssq_mm = sem("ssq_mm")
        ssq_read = sem("ssq_read")
        rms_var = sem("rms_var")
        rms_root = sem("rms_root")
        rms_link = sem("rms_link")
        rms_done = sem("rms_done")
        folded = sem("folded_m")
        ctx.callback(clear, nc, used)
        block = ctx.enter_context(nc.Block())

        @block.sync
        def _(sp):
            sp.dma_start(ident[:, :], io["ident"]).then_inc(const_in, 16)
            sp.dma_start(chan[:, :, :], io["chan"]).then_inc(const_in, 16)

            def step(k, at):
                if at(0):
                    t, r = at(0)
                    n = r * (16 * U // 2)
                    sp.wait_ge(gate_mm, t + 1)
                    sp.dma_start(Wg[:, k % 2, :, :], io["in_proj"][bass.ds(t, 1), :, :, :]
                                 .rearrange("a p d o -> (a p) d o")).then_inc(g_in[k % 2], 16)
                    sp.wait_ge(hid_mm, t + 1)
                    sp.dma_start(Wh[:, k % 2, :, :], io["in_proj"][bass.ds(t + CT_, 1), :, :, :]
                                 .rearrange("a p d o -> (a p) d o")).then_inc(h_in[k % 2], 16)
                if at(2):
                    t, r = at(2)
                    sp.wait_ge(out_mm, t + 1)
                    sp.dma_start(Wo[:, k % 2, :], io["out_proj"][bass.ds(t, 1), :, :]
                                 .rearrange("a p o -> (a p) o")).then_inc(o_in[k % 2], 16)

            steps(sp, step, T, U)

        @block.tensor
        def _(pe):
            pe.sem_inc(gate_mm, 2)
            pe.sem_inc(hid_mm, 2)
            pe.sem_inc(mixed, 2)
            pe.sem_inc(out_mm, 2)
            pe.wait_ge(const_in, 32)

            def loads(k, r):
                return r * (16 * U // 2) + 16 * (k // 2 + 1)

            def step(k, at):
                if at(0):
                    t, r = at(0)
                    pe.wait_ge(g_in[k % 2], loads(k, r))
                    pe.wait_ge(gate_silu, t + 1)
                    for d in range(DT):
                        last = nc.tensor.matmul(pG[:, :], Wg[:, k % 2, d, :], P["hT"][:, d, :],
                                                start=d == 0, stop=d == DT - 1)
                    last.then_inc(gate_mm, 1)
                if at(4):
                    (t, r), k4 = at(4), (k - 4) % U
                    pe.wait_ge(o_in[k4 % 2], loads(k4, r))
                    pe.wait_ge(yw_ready, t + 3)
                    if k4 == 0:
                        pe.wait_ge(folded, r * 4 + 4)
                    for q in range(TT):
                        last = nc.tensor.matmul(pO[:, q, :], yw[:, k4 % 2, q * 128:(q + 1) * 128], Wo[:, k4 % 2, :],
                                                start=k4 == 0, stop=k4 == U - 1)
                    last.then_inc(out_mm, 1)
                    if k4 == U - 1:
                        pe.wait_ge(hc_ready, (at(2) or (T - 1, 0))[0] + 2)
                        pe.wait_ge(sq_summed, t + 3)
                        for q in range(TT):
                            last = nc.tensor.matmul(pT[:, q:q + 1], sqsum[:, (U - 1) % 2, q * 128:(q + 1) * 128],
                                                    ones[:, :], start=True, stop=True)
                        last.then_inc(ssq_mm, 1)
                if at(1):
                    (t, r), k1 = at(1), (k - 1) % U
                    pe.wait_ge(hid_silu, t + 3)
                    pe.wait_ge(hc_ready, t + 1)
                    if k1 == 2 and not (isinstance(r, int) and r == 0):
                        pe.wait_ge(ssq_read, r + 1)
                    for q in range(TT):
                        last = nc.tensor.transpose(pT[:, q * 128:(q + 1) * 128], hid[:, k1 % 4, q * 128:(q + 1) * 128],
                                                   ident[:, :])
                    last.then_inc(hid_turned, 1)
                if at(0):
                    t, r = at(0)
                    pe.wait_ge(h_in[k % 2], loads(k, r))
                    pe.wait_ge(padded, t + 1)
                    for d in range(DT):
                        last = nc.tensor.matmul(pX[:, :], Wh[:, k % 2, d, :], P["hT"][:, d, :],
                                                start=d == 0, stop=d == DT - 1)
                    last.then_inc(hid_mm, 1)
                if at(2):
                    (t, r), k2 = at(2), (k - 2) % U
                    pe.wait_ge(hc_ready, t + 2)
                    pe.wait_ge(mt_ready, t * 2 + 6)
                    pe.wait_ge(y_ready, t + 1)
                    for h in range(2):
                        for q in range(TT):
                            last = nc.tensor.matmul(pY[HD * h:HD * h + HD, q * 128:(q + 1) * 128],
                                                    hc[:, k2 % 2, q, h, :], MT[:, k2 % 2, h, q, :],
                                                    start=True, stop=True)
                    last.then_inc(mixed, 1)

            steps(pe, step, T, U)

        @block.scalar
        def _(act):
            act.wait_ge(zeroed, 3)
            act.sem_inc(gate_silu, 1)
            act.sem_inc(padded, 1)
            act.sem_inc(hid_silu, 2)
            act.sem_inc(sq_ready, 2)
            act.sem_inc(yw_ready, 2)
            act.wait_ge(const_in, 32)

            def step(k, at):
                if at(0):
                    t, r = at(0)
                    act.wait_ge(gate_mm, t + 3)
                    act.wait_ge(yg_ready, t + 1)
                    nc.scalar.activation(sg[:, k % 4, :], pG[:, :], ACT.Silu).then_inc(gate_silu, 1)
                if at(3):
                    (t, r), k3 = at(3), (k - 3) % U
                    act.wait_ge(yg_ready, t + 5)
                    act.wait_ge(sq_summed, t + 1)
                    nc.scalar.activation(sq[:, k3 % 2, :], yg[:, k3 % 2, :], ACT.Square).then_inc(sq_ready, 1)
                    act.wait_ge(out_mm, t + 1)
                    nc.scalar.activation(yw[:, k3 % 2, :], yg[:, k3 % 2, :], ACT.Copy,
                                         scale=chan[:, 1, bass.ds(t, 1)]).then_inc(yw_ready, 1)
                if at(4) and (k - 4) % U == U - 1:
                    t, r = at(4)
                    act.wait_ge(rms_var, r + 1)
                    nc.scalar.activation(rms[:, 1, :], rms[:, 0, :], ACT.Sqrt).then_inc(rms_root, 1)
                if at(0):
                    t, r = at(0)
                    act.wait_ge(hid_mm, t + 3)
                    act.wait_ge(conved, t * TAPS + TAPS)
                    nc.scalar.activation(XP[:, k % 2, :, TAPS - 1:], pX[:, :].rearrange("p (b s) -> p b s", b=B),
                                         ACT.Copy).then_inc(padded, 1)
                    act.wait_ge(conved, t * TAPS + 3 * TAPS)
                    act.wait_ge(yg_ready, t + 1)
                    nc.scalar.activation(hid[:, k % 4, :], cv[:, k % 2, :, :].rearrange("p b s -> p (b s)"),
                                         ACT.Silu).then_inc(hid_silu, 1)

            steps(act, step, T, U)

        @block.vector
        def _(dve):
            v = nc.vector
            v.memset(XP[:, :, :, :], 0.0).then_inc(zeroed, 1)
            v.memset(ones[:, :], 1.0).then_inc(zeroed, 1)
            v.memset(zero[:, :], 0.0).then_inc(zeroed, 1)
            dve.sem_inc(conved, 2 * TAPS)
            dve.sem_inc(hc_ready, 1)
            dve.sem_inc(y_ready, 1)
            dve.sem_inc(yg_ready, 4)
            dve.sem_inc(ssq_read, 1)
            dve.sem_inc(folded, 4)
            dve.wait_ge(const_in, 32)

            def step(k, at):
                if at(3):
                    (t, r), k3 = at(3), (k - 3) % U
                    dve.wait_ge(mixed, t + 3)
                    dve.wait_ge(hid_silu, t + 3)
                    v.scalar_tensor_tensor(y[:, k3 % 2, :], hid[:, k3 % 4, :], chan[:, 0, bass.ds(t, 1)], pY[:, :],
                                           ALU.mult, ALU.add).then_inc(y_ready, 1)
                    dve.wait_ge(y_ready, t + 2)
                    dve.wait_ge(gate_silu, t + 2)
                    dve.wait_ge(sq_ready, t + 1)
                    dve.wait_ge(yw_ready, t + 1)
                    v.tensor_tensor(yg[:, k3 % 2, :], y[:, k3 % 2, :], sg[:, k3 % 4, :], ALU.mult).then_inc(yg_ready, 1)
                if at(4) and (k - 4) % U == U - 1:
                    t, r = at(4)
                    dve.wait_ge(ssq_mm, r + 1)
                    v.tensor_scalar(rms[:, 0, :], pT[:, 0:TT], 1.0 / (INNER // GR), EPS, ALU.mult, ALU.add)\
                        .then_inc(ssq_read, 1)
                    dve.wait_ge(ssq_read, r + 2)
                    v.tensor_copy(rms[:, 3, :], rms[:, 0, :]).then_inc(rms_var, 1)
                    dve.wait_ge(rms_root, r + 1)
                    base = r * 4
                    rr, tm = rms[:, 2, :], rms[:, 3, :]
                    v.reciprocal(rr, rms[:, 1, :]).then_inc(rms_link, 1)
                    dve.wait_ge(rms_link, base + 1)
                    v.tensor_tensor(tm, rr, rr, ALU.mult).then_inc(rms_link, 1)
                    dve.wait_ge(rms_link, base + 2)
                    v.tensor_tensor(tm, tm, rms[:, 0, :], ALU.mult).then_inc(rms_link, 1)
                    dve.wait_ge(rms_link, base + 3)
                    v.tensor_scalar(tm, tm, -0.5, 1.5, ALU.mult, ALU.add).then_inc(rms_link, 1)
                    dve.wait_ge(rms_link, base + 4)
                    v.tensor_tensor(rr, rr, tm, ALU.mult).then_inc(rms_done, 1)
                    dve.wait_ge(rms_done, r + 1)
                    dve.wait_ge(out_mm, t + 3)
                    for q in range(TT):
                        v.scalar_tensor_tensor(P["acc"][:, q, :], pO[:, q, :], rms[:, 2, q:q + 1], P["acc"][:, q, :],
                                               ALU.mult, ALU.add).then_inc(folded, 1)
                if at(1):
                    (t, r), k1 = at(1), (k - 1) % U
                    dve.wait_ge(hid_turned, t + 1)
                    dve.wait_ge(mixed, t + 1)
                    v.tensor_tensor(hc[:, k1 % 2, :, :, :],
                                    pT[:, :].rearrange("p (q h x) -> p q h x", q=TT, h=2),
                                    P["dt"][:, :, bass.ds(t * 2, 2)].unsqueeze(3).to_broadcast([128, TT, 2, HD]),
                                    ALU.mult).then_inc(hc_ready, 1)
                if at(0):
                    t, r = at(0)
                    dve.wait_ge(padded, t + 2)
                    dve.wait_ge(hid_silu, t + 1)
                    conv_taps(v, dve, cv[:, k % 2, :, :], XP[:, k % 2, :, :], P["conv"], t, conved,
                              t * TAPS + 2 * TAPS)

            steps(dve, step, T, U)

        @block.gpsimd
        def _(pool):
            pool.wait_ge(zeroed, 3)
            pool.sem_inc(mt_ready, 4)
            pool.sem_inc(sq_summed, 2)

            def step(k, at):
                if at(1):
                    (t, r), k1 = at(1), (k - 1) % U
                    pool.wait_ge(mixed, t + 1)
                    for h in range(2):
                        nc.gpsimd.tensor_tensor(
                            MT[:, k1 % 2, h, :, :].rearrange("p q (b i) -> p q b i", b=4),
                            P["cb"][:, bass.ds(r, 1), :, :].rearrange("p g q (b i) -> p (g q) b i", b=4),
                            P["decay"][:, :, bass.ds(t * 2 + h, 1), :].to_broadcast([128, TT, 4, S]),
                            ALU.mult).then_inc(mt_ready, 1)
                if at(3):
                    (t, r), k3 = at(3), (k - 3) % U
                    pool.wait_ge(sq_ready, t + 3)
                    if k3 == 0:
                        if not (isinstance(r, int) and r == 0):
                            pool.wait_ge(ssq_mm, r)
                        nc.gpsimd.tensor_tensor(sqsum[:, 0, :], sq[:, 0, :], zero[:, :].to_broadcast([128, TOK]),
                                                ALU.add).then_inc(sq_summed, 1)
                    else:
                        pool.wait_ge(sq_summed, t + 2)
                        nc.gpsimd.tensor_tensor(sqsum[:, k3 % 2, :], sqsum[:, 1 - k3 % 2, :], sq[:, k3 % 2, :],
                                                ALU.add).then_inc(sq_summed, 1)

            steps(pool, step, T, U)


def feed_forward(nc, io, scratch, P, out):
    with ExitStack() as ctx:
        def sb(name, shape, dt=F32):
            return ctx.enter_context(nc.sbuf_tensor(name, shape, dt))

        used = []

        def sem(name):
            used.append(ctx.enter_context(nc.semaphore(name)))
            return used[-1]

        ident = sb("ident_f", [128, 128])
        w1 = sb("w1_f", [128, FFH])
        w3 = sb("w3_f", [128, FFH])
        w2 = sb("w2_f", [FP, FR, D])
        a13 = sb("a13", [128, 2, DT, 2])
        b1 = sb("b1_f", [2, FFH])
        b3 = sb("b3_f", [2, FFH])
        a2 = sb("a2_f", [FP, 4 * FR, 2])
        b2 = sb("b2_f", [2, D])
        x2 = P["acc"]
        xn = sb("xn_f", [128, TT, D])
        st = sb("st_f", [128, TT, 6])
        mv = sb("mv_f", [128, TT, 2])
        tmp = sb("tmp_f", [128, 3, TT])
        xT = sb("xT_f", [128, DT, TOK])
        xf = sb("xf_f", [128, TOK])
        la = sb("la_f", [2, 2, TOK])
        la2 = sb("la2_f", [2, TOK])
        sg = sb("sg_f", [FP, 2, TOK])
        u = sb("u_f", [FP, 2, TOK])
        uf = sb("uf_f", [FP, FR, TOK])
        res = sb("res_f", [128, TT, D])
        pt = ctx.enter_context(nc.psum_tensor("pt_f", [128, 2, 512], F32))
        pl = ctx.enter_context(nc.psum_tensor("pl_f", [128, 512], F32))
        pg = ctx.enter_context(nc.psum_tensor("pg_f", [128, 2, 512], F32))
        pu = ctx.enter_context(nc.psum_tensor("pu_f", [128, 2, 512], F32))
        w_in = sem("w_in_f")
        var_ready = sem("var_ready_f")
        root_ready = sem("root_ready_f")
        xn_ready = sem("xn_ready_f")
        turned = sem("turned_f")
        xT_ready = sem("xT_ready_f")
        xf_ready = sem("xf_ready_f")
        la_mm = sem("la_mm")
        la_ready = sem("la_ready")
        gu_mm = sem("gu_mm")
        silued = sem("silued_f")
        u_ready = sem("u_ready_f")
        uf_ready = sem("uf_ready_f")
        la2_mm = sem("la2_mm")
        la2_ready = sem("la2_ready")
        out_mm = sem("out_mm_f")
        res_ready = sem("res_ready_f")
        stored = sem("stored_f")
        v_chain = sem("v_chain_f")
        HT = 4 * FR
        ctx.callback(clear, nc, used)
        block = ctx.enter_context(nc.Block())

        @block.sync
        def _(sp):
            loads = ((ident, "ident"), (w1, "w1"), (w3, "w3"), (w2, "w2"), (a13, "a13"), (b1, "b1"), (b3, "b3"),
                     (a2, "a2"), (b2, "b2"))
            for dst, src in loads:
                dst = dst[tuple(slice(None) for _ in dst.shape)]
                sp.dma_start(dst, io[src]).then_inc(w_in, 16)
            for q in range(TT):
                sp.wait_ge(res_ready, q + 1)
                sp.dma_start(out.rearrange("b s d -> (b s) d")[q * 128:(q + 1) * 128, :], res[:, q, :])\
                    .then_inc(stored, 16)
            sp.wait_ge(stored, 16 * TT)

        @block.scalar
        def _(act):
            act.wait_ge(var_ready, 1)
            nc.scalar.activation(tmp[:, 0, :], mv[:, :, 1], ACT.Sqrt).then_inc(root_ready, 1)
            for n in range(HT):
                act.wait_ge(gu_mm, n + 1)
                if n >= 2:
                    act.wait_ge(u_ready, n - 1)
                nc.scalar.activation(sg[:, n % 2, :], pg[0:FP, n % 2, :], ACT.Silu).then_inc(silued, 1)

        @block.vector
        def _(dve):
            v = nc.vector
            link = chain(dve, v_chain)

            def act_sqrt(ins):
                ins.then_inc(var_ready, 1)
                dve.wait_ge(root_ready, 1)

            row_norm(nc, v, link, act_sqrt, x2, xn, st, mv, tmp)
            dve.sem_inc(xn_ready, 1)
            for d in range(DT):
                dve.wait_ge(turned, d + 1)
                v.tensor_copy(xT[:, d, :], pt[:, d % 2, :]).then_inc(xT_ready, 1)
            dve.wait_ge(xT_ready, DT)
            link(v.tensor_tensor(xf[:, :], xT[:, 0, :], xT[:, 1, :], ALU.add))
            link(v.tensor_tensor(xf[:, :], xf[:, :], xT[:, 2, :], ALU.add))
            v.tensor_tensor(xf[:, :], xf[:, :], xT[:, 3, :], ALU.add).then_inc(xf_ready, 1)
            for i in range(2):
                dve.wait_ge(la_mm, i + 1)
                v.tensor_scalar(la[:, i, :], pt[0:2, i, :], 0.5, None, ALU.mult).then_inc(la_ready, 1)
            for n in range(HT):
                r, k = n // 4, n % 4
                dve.wait_ge(silued, n + 1)
                if n >= 2:
                    dve.wait_ge(la2_mm, n - 1)
                v.tensor_tensor(u[:, n % 2, :], sg[:, n % 2, :], pu[0:FP, n % 2, :], ALU.mult).then_inc(u_ready, 1)
                dve.wait_ge(u_ready, n + 1)
                if k == 0:
                    v.tensor_copy(uf[:, r, :], u[:, n % 2, :]).then_inc(uf_ready, 1)
                else:
                    dve.wait_ge(uf_ready, n)
                    v.tensor_tensor(uf[:, r, :], uf[:, r, :], u[:, n % 2, :], ALU.add).then_inc(uf_ready, 1)
            dve.wait_ge(la2_mm, HT)
            v.tensor_scalar(la2[:, :], pl[0:2, :], 0.5, None, ALU.mult).then_inc(la2_ready, 1)
            for q in range(TT):
                dve.wait_ge(out_mm, q + 1)
                v.tensor_tensor(res[:, q, :], x2[:, q, :], (pg if q < 2 else pu)[:, q % 2, :], ALU.add)\
                    .then_inc(res_ready, 1)

        @block.tensor
        def _(pe):
            pe.wait_ge(w_in, 16 * 9)
            pe.wait_ge(xn_ready, 1)
            for d in range(DT):
                if d >= 2:
                    pe.wait_ge(xT_ready, d - 1)
                for t in range(TT):
                    last = nc.tensor.transpose(pt[:, d % 2, t * 128:(t + 1) * 128], xn[:, t, d * 128:(d + 1) * 128],
                                               ident[:, :])
                last.then_inc(turned, 1)
            pe.wait_ge(xT_ready, DT)
            for i in range(2):
                for d in range(DT):
                    last = nc.tensor.matmul(pt[0:2, i, :], a13[:, i, d, :], xT[:, d, :], start=d == 0, stop=d == DT - 1)
                last.then_inc(la_mm, 1)
            pe.wait_ge(xf_ready, 1)
            pe.wait_ge(la_ready, 2)

            def low_rank(n):
                pe.wait_ge(u_ready, n + 1)
                nc.tensor.matmul(pl[0:2, :], a2[:, (n % 4) * FR + n // 4, :], u[:, n % 2, :],
                                 start=n == 0, stop=n == HT - 1).then_inc(la2_mm, 1)

            for n in range(HT):
                c = ((n % 4) * FR + n // 4) * FP
                if n >= 2:
                    pe.wait_ge(u_ready, n - 1)
                for p_, w_, b_, i in ((pg, w1, b1, 0), (pu, w3, b3, 1)):
                    nc.tensor.matmul(p_[0:FP, n % 2, :], w_[:, c:c + FP], xf[:, :], start=True, stop=False)
                    last = nc.tensor.matmul(p_[0:FP, n % 2, :], b_[:, c:c + FP], la[:, i, :], start=False, stop=True)
                last.then_inc(gu_mm, 1)
                if n >= 1:
                    low_rank(n - 1)
            low_rank(HT - 1)
            pe.wait_ge(uf_ready, HT)
            pe.wait_ge(la2_ready, 1)
            for q in range(TT):
                po = (pg if q < 2 else pu)[:, q % 2, :]
                for r in range(FR):
                    nc.tensor.matmul(po, uf[:, r, q * 128:(q + 1) * 128], w2[:, r, :], start=r == 0, stop=False)
                nc.tensor.matmul(po, la2[:, q * 128:(q + 1) * 128], b2[:, :], start=False, stop=True).then_inc(out_mm, 1)


def program(nc, io, scratch, out):
    cross_attention(nc, io, scratch)
    with ExitStack() as ctx:
        def sb(name, shape):
            return ctx.enter_context(nc.sbuf_tensor(name, shape, F32))

        P = {"acc": sb("acc", [128, TT, D])}
        with ExitStack() as mctx:
            def msb(name, shape):
                return mctx.enter_context(nc.sbuf_tensor(name, shape, F32))

            P["hT"] = msb("hT", [128, DT, TOK])
            P["dt"] = msb("dt_tok", [128, TT, HEADS])
            P["decay"] = msb("decay", [128, TT, HEADS, S])
            P["cb"] = msb("cb", [128, GR, TT, 128])
            P["conv"] = msb("conv", [128, (CT_ + 2 * GR) * 5])
            mamba_prepare(nc, io, scratch, P)
            mamba_states(nc, io, scratch, P)
            mamba_mix(nc, io, scratch, P)
        feed_forward(nc, io, scratch, P, out)


def constants():
    import numpy as np
    c = {}
    c["idx"] = ((np.arange(B * N) % N).reshape(128, -1) / 1024.0).astype(np.float32)
    c["ident"] = np.eye(128, dtype=np.float32)
    c["rep"] = np.repeat(np.eye(C, dtype=np.float32), M, axis=1)
    e = np.arange(EXT)
    lead = np.minimum(e % K, e // K + LEAD)
    place = np.where(e < LEAD * K, lead, np.minimum(e - LEAD * K, N - 1))
    c["place"] = np.tile(place.astype(np.float16), (128, 1))
    x = np.arange(32)
    batch, tok = np.arange(128) // S, np.arange(128)
    same = batch[:, None] == batch[None, :]
    c["later"] = (same & (tok[:, None] > tok[None, :])).astype(np.float32)
    c["upto"] = ((tok % S)[:, None] <= np.arange(S)[None, :]).astype(np.float32)
    c["causal"] = (same & (tok[:, None] <= tok[None, :])).astype(np.float32)
    c["maskL"] = np.array([[1024.0 * (i % 32 // K == n) for i in range(128)] for n in range(PTS)], np.float16)
    c["maskR"] = np.tile(np.array([-1024.0 * (x // K != n) for n in range(PTS)], np.float16), (1, SUBS))
    return c


def kernel(**inputs):
    import numpy as np
    import concourse.bacc as bacc
    from concourse.bass_utils import run_bass_kernel_spmd as run

    nc = bacc.Bacc("TRN2", target_bir_lowering=False, num_devices=1)
    a = {k: np.asarray(v) for k, v in inputs.items()}
    arrays = {
        "x": a["x"].reshape(B * S, D),
        "coords": a["ctx_4096"][:, :3, :].transpose(1, 0, 2).reshape(3 * B, N),
    }
    for n in "12":
        arrays["lin" + n] = a["L0_xattn_W_lin" + n]
        arrays["blin" + n] = a["L0_xattn_b_lin" + n].reshape(-1, 1)
        arrays["convT" + n] = a["L0_xattn_W_conv" + n].T
    arrays["conv3T"] = a["L0_xattn_W_conv3"].T
    w = a["L0_attn_in_proj_w"]
    arrays["in_proj"] = w.reshape(-1, 128, DT, 128).transpose(0, 3, 2, 1)
    arrays["out_proj"] = a["L0_attn_out_proj_w"].T.reshape(CT_, 128, D)
    arrays["norm_w"] = a["L0_attn_norm_w"].reshape(DT, 128).T
    arrays["head_par"] = np.stack([a["L0_attn_dt_bias"], a["L0_attn_A_log"]], 1)
    taps = np.concatenate([a["L0_attn_conv_w"], a["L0_attn_conv_b"][:, None]], 1)
    arrays["conv"] = taps.reshape(-1, 128, TAPS + 1).transpose(1, 0, 2).reshape(128, -1)
    arrays["chan"] = np.stack([np.repeat(a["L0_attn_Dp"], HD).reshape(CT_, 128).T,
                               a["L0_attn_gnorm_w"].reshape(CT_, 128).T], 1)
    arrays["w1"], arrays["w3"] = a["L0_ffn_w1q"].T, a["L0_ffn_w3q"].T
    arrays["w2"] = a["L0_ffn_w2q"].T.reshape(FR, FP, D).transpose(1, 0, 2)
    arrays["a13"] = np.stack([a["L0_ffn_a1"], a["L0_ffn_a3"]]).reshape(2, 2, DT, 128).transpose(3, 0, 2, 1)
    arrays["b1"], arrays["b3"], arrays["b2"] = a["L0_ffn_b1"].T, a["L0_ffn_b3"].T, a["L0_ffn_b2"].T
    arrays["a2"] = a["L0_ffn_a2"].reshape(2, 4 * FR, FP).transpose(2, 1, 0)
    arrays.update(constants())
    arrays = {k: np.ascontiguousarray(v) for k, v in arrays.items()}
    io = {k: nc.dram_tensor("in_" + k, v.shape, mybir.dt.from_np(v.dtype), kind="ExternalInput").ap()
          for k, v in arrays.items()}
    out = nc.dram_tensor("out_0_dram", (B, S, D), F32, kind="ExternalOutput").ap()

    def dram(name, shape, dt=F32):
        return nc.dram_tensor("scratch_" + name, shape, dt).ap()

    scratch = {"q": dram("q", (48, N), I32), "f0": dram("f0", (B * C, N)),
               "hi": dram("hi", (M, B, N)), "lo": dram("lo", (M, B, N))}
    scratch.update({"q16": dram("q16", (B * GROUPS, 128, GC), F16), "c16": dram("c16", (B * GROUPS, 128, GP), F16),
                    "f1": dram("f1", (B * C, N)), "f2": dram("f2", (2 * C, B, N)), "x1": dram("x1", (B * S, D))})
    program(nc, io, scratch, out)
    r = run(nc, [{"in_" + k: v for k, v in arrays.items()}], core_ids=[0])
    return r.results[0]["out_0_dram"]
```

```python
from contextlib import ExitStack

import concourse.bass as bass
from concourse import mybir

F32 = mybir.dt.float32
F16 = mybir.dt.float16
I32 = mybir.dt.int32
ALU = mybir.AluOpType
ACT = mybir.ActivationFunctionType
X = mybir.AxisListType.X

B, S, D = 16, 32, 512
N = D
C = S
NT = N // 128
M = 4
K = 10
HALF = K // 2
BITS = 10
LEAD = HALF
PTS = 3
SUBS = 15
GROUPS = 12
GP = PTS * SUBS
PADN = GP * GROUPS
NSUB = (N - LEAD) // PTS + 2
GC = 32 * SUBS
RUNS = (0, 0, LEAD), (LEAD + 1, LEAD, N)
EXT = LEAD * K + N + HALF - 1
EPS = 1e-5
SLOPE = 0.2
HEADS, HD, GR, NST, TAPS = 128, 64, 8, 128, 4
INNER = HEADS * HD
TOK = B * S
TT = TOK // 128
DT = D // 128
CT_ = INNER // 128
TPG = CT_ // GR
FFH = 1376
FQ = FFH // 4
FR = 4
FP = FQ // FR



def clear(nc, semaphores):
    with nc.Block() as block:
        @block.sync
        def _(sp):
            for s in semaphores:
                sp.sem_clear(s)


def chain(eng, sem):
    count = [0]

    def link(ins):
        count[0] += 1
        ins.then_inc(sem, 1)
        eng.wait_ge(sem, count[0])
        return ins

    return link


def norm_and_keys(nc, io, scratch):
    with ExitStack() as ctx:
        def sb(name, shape, dt=F32):
            return ctx.enter_context(nc.sbuf_tensor(name, shape, dt))

        used = []

        def sem(name):
            used.append(ctx.enter_context(nc.semaphore(name)))
            return used[-1]

        lat = sb("lat", [128, 4, D])
        latn = sb("latn", [128, 4, D])
        bst = sb("bst", [128, 4, 6])
        mv = sb("mv", [128, 4, 2])
        sd = sb("sd", [128, 4])
        rstd = sb("rstd", [128, 4])
        rtmp = sb("rtmp", [128, 4])
        co = sb("co", [48, N])
        cv = sb("cv", [48, N])
        ci = sb("ci", [48, N], I32)
        cf = sb("cf", [48, N])
        cg = sb("cg", [48, N])
        sc = sb("sc", [48, 24])
        sci = sb("sci", [48, 4], I32)
        P64 = B * N // 128
        A = sb("A", [128, 4, 3, P64], I32)
        A2 = sb("A2", [128, 4, 3, P64], I32)
        qin = sb("qin", [128, 3, P64], I32)
        u = sb("u", [128, 6, 2, P64], I32)
        key = sb("key", [128, 4, P64], I32)
        kp = sb("kp", [128, 4, P64], I32)
        hi = sb("hi", [128, 4, P64])
        lo = sb("lo", [128, 4, P64])
        idx = sb("idx", [128, P64])

        lat_in = sem("lat_in")
        co_in = sem("co_in")
        idx_in = sem("idx_in")
        q_out = sem("q_out")
        q_in = sem("q_in")
        q_ready = sem("q_ready")
        var_ready = sem("var_ready")
        sd_ready = sem("sd_ready")
        latn_ready = sem("latn_ready")
        keys_ready = sem("keys_ready")
        stored = sem("stored")
        v_chain = sem("v_chain_keys")
        ctx.callback(clear, nc, used)
        block = ctx.enter_context(nc.Block())

        @block.sync
        def _(sp):
            sp.dma_start(co[:, :], io["coords"]).then_inc(co_in, 16)
            sp.dma_start(idx[:, :], io["idx"]).then_inc(idx_in, 16)
            sp.dma_start(lat[:, :, :], io["x"].rearrange("(t p) d -> p t d", p=128)).then_inc(lat_in, 16)
            sp.wait_ge(q_ready, 1)
            sp.dma_start(scratch["q"], ci[:, :]).then_inc(q_out, 16)
            sp.wait_ge(q_out, 16)
            sp.dma_start(qin[:, :, :], scratch["q"].rearrange("(k b) n -> k (b n)", k=3)
                         .rearrange("k (p i) -> p k i", p=128)).then_inc(q_in, 16)
            sp.wait_ge(latn_ready, 1)
            sp.dma_start(scratch["f0"].rearrange("(t p) d -> p t d", p=128), latn[:, :, :]).then_inc(stored, 16)
            sp.wait_ge(keys_ready, 1)
            sp.dma_start(scratch["hi"].rearrange("m b n -> m (b n)").rearrange("m (p i) -> p m i", p=128),
                         hi[:, :, :]).then_inc(stored, 16)
            sp.dma_start(scratch["lo"].rearrange("m b n -> m (b n)").rearrange("m (p i) -> p m i", p=128),
                         lo[:, :, :]).then_inc(stored, 16)
            sp.wait_ge(stored, 48)

        @block.scalar
        def _(act):
            act.wait_ge(var_ready, 1)
            nc.scalar.activation(sd[:, :], mv[:, :, 1], ACT.Sqrt).then_inc(sd_ready, 1)

        @block.vector
        def _(dve):
            link = chain(dve, v_chain)
            v = nc.vector
            dve.wait_ge(co_in, 16)
            cmin, cmax, d, r, s, e = (sc[:, i:i + 1] for i in range(6))
            dh, dl, sh, sl, t0, t1 = (sc[:, i:i + 1] for i in range(6, 12))
            link(v.tensor_reduce(cmin, co[:, :], X, ALU.min))
            link(v.tensor_reduce(cmax, co[:, :], X, ALU.max))
            link(v.tensor_tensor(d, cmax, cmin, ALU.subtract))
            link(v.tensor_scalar(d, d, 1e-6, None, ALU.add))
            link(v.reciprocal(r, d))
            link(v.tensor_scalar(s, r, 1023.0, None, ALU.mult))
            for whole, high, low in ((d, dh, dl), (s, sh, sl)):
                link(v.tensor_scalar(high.bitcast(I32), whole.bitcast(I32), -4096, None, ALU.bitwise_and))
                link(v.tensor_tensor(low, whole, high, ALU.subtract))
            link(v.tensor_tensor(t0, sh, dh, ALU.mult))
            link(v.tensor_scalar(e, t0, -1.0, 1023.0, ALU.mult, ALU.add))
            for a, b in ((sh, dl), (sl, dh), (sl, dl)):
                link(v.tensor_tensor(t1, a, b, ALU.mult))
                link(v.tensor_tensor(e, e, t1, ALU.subtract))
            link(v.tensor_tensor(t1, e, r, ALU.mult))
            link(v.tensor_tensor(s, s, t1, ALU.add))
            link(v.tensor_scalar(cv[:, :], co[:, :], cmin, s, ALU.subtract, ALU.mult))
            link(v.tensor_copy(ci[:, :], cv[:, :]))
            link(v.tensor_copy(cf[:, :], ci[:, :]))
            link(v.tensor_tensor(cg[:, :], cf[:, :], cv[:, :], ALU.is_gt))
            link(v.tensor_tensor(cf[:, :], cf[:, :], cg[:, :], ALU.subtract))
            link(v.tensor_scalar(cf[:, :], cf[:, :], 0.0, float(2 ** BITS - 1), ALU.max, ALU.min))
            v.tensor_copy(ci[:, :], cf[:, :]).then_inc(q_ready, 1)

            dve.wait_ge(lat_in, 16)
            for t in range(4):
                link(v.bn_stats(bst[:, t, :], lat[:, t, :]))
            for t in range(4):
                link(v.bn_aggr(mv[:, t, :], bst[:, t, :]))
            v.tensor_scalar(mv[:, :, 1], mv[:, :, 1], EPS, None, ALU.add).then_inc(var_ready, 1)
            dve.wait_ge(sd_ready, 1)
            inverse_root(v, link, rstd[:, :], mv[:, :, 1], sd[:, :], rtmp[:, :])
            for t in range(4):
                last = v.tensor_scalar(latn[:, t, :], lat[:, t, :], mv[:, t, 0:1], rstd[:, t:t + 1],
                                       ALU.subtract, ALU.mult)
                if t < 3:
                    link(last)
            last.then_inc(latn_ready, 1)

            dve.wait_ge(q_in, 16)
            for m in range(4):
                for k in range(3):
                    link(v.tensor_copy(A[:, m, k, :], qin[:, (k if m % 2 == 0 or k == 2 else 1 - k), :]))
            ax = [A[:, 2:4, k, :] for k in range(3)]
            neg, pos, t, w = (u[:, i, :, :] for i in range(4))
            for bit in range(BITS - 1, 0, -1):
                low = 2 ** bit - 1
                link(v.tensor_scalar(pos, ax[0], 31 - bit, 31, ALU.logical_shift_left, ALU.arith_shift_right))
                link(v.scalar_tensor_tensor(ax[0], pos, low, ax[0], ALU.bitwise_and, ALU.bitwise_xor))
                for i in (1, 2):
                    link(v.tensor_scalar(pos, ax[i], 31 - bit, 31, ALU.logical_shift_left, ALU.arith_shift_right))
                    link(v.tensor_scalar(neg, pos, -1, None, ALU.bitwise_xor))
                    link(v.tensor_tensor(t, ax[0], ax[i], ALU.bitwise_xor))
                    link(v.scalar_tensor_tensor(w, t, low, neg, ALU.bitwise_and, ALU.bitwise_and))
                    link(v.tensor_tensor(ax[i], ax[i], w, ALU.bitwise_xor))
                    link(v.scalar_tensor_tensor(t, pos, low, w, ALU.bitwise_and, ALU.bitwise_xor))
                    link(v.tensor_tensor(ax[0], ax[0], t, ALU.bitwise_xor))
            link(v.tensor_tensor(ax[1], ax[1], ax[0], ALU.bitwise_xor))
            link(v.tensor_tensor(ax[2], ax[2], ax[1], ALU.bitwise_xor))
            for bit in range(BITS - 1, 0, -1):
                link(v.tensor_scalar(pos, ax[2], 31 - bit, 31, ALU.logical_shift_left, ALU.arith_shift_right))
                if bit == BITS - 1:
                    link(v.tensor_scalar(t, pos, 2 ** bit - 1, None, ALU.bitwise_and))
                else:
                    link(v.scalar_tensor_tensor(t, pos, 2 ** bit - 1, t, ALU.bitwise_and, ALU.bitwise_xor))
            for k in range(3):
                link(v.tensor_tensor(ax[k], ax[k], t, ALU.bitwise_xor))
            flat = A[:, :, :, :].rearrange("p m k i -> p (m k i)")
            flat2 = A2[:, :, :, :].rearrange("p m k i -> p (m k i)")
            for shift, mask in ((16, 0x030000FF), (8, 0x0300F00F), (4, 0x030C30C3), (2, 0x09249249)):
                link(v.scalar_tensor_tensor(flat2, flat, shift, flat, ALU.logical_shift_left, ALU.bitwise_or))
                link(v.tensor_scalar(flat, flat2, mask, None, ALU.bitwise_and))
            link(v.scalar_tensor_tensor(key[:, :, :], A[:, :, 0, :], 2, A[:, :, 2, :],
                                        ALU.logical_shift_left, ALU.bitwise_or))
            link(v.scalar_tensor_tensor(kp[:, :, :], A[:, :, 1, :], 1, key[:, :, :],
                                        ALU.logical_shift_left, ALU.bitwise_or))
            link(v.tensor_scalar(key[:, :, :], kp[:, :, :], 12, None, ALU.logical_shift_right))
            link(v.tensor_copy(hi[:, :, :], key[:, :, :]))
            link(v.tensor_scalar(hi[:, :, :], hi[:, :, :], 4096.0, None, ALU.mult))
            link(v.tensor_scalar(key[:, :, :], kp[:, :, :], 4095, None, ALU.bitwise_and))
            link(v.tensor_copy(lo[:, :, :], key[:, :, :]))
            dve.wait_ge(idx_in, 16)
            v.tensor_tensor(lo[:, :, :], lo[:, :, :], idx[:, :].unsqueeze(1).to_broadcast([128, 4, P64]),
                            ALU.add).then_inc(keys_ready, 1)


def ranks(nc, io, scratch, rank):
    with ExitStack() as ctx:
        def sb(name, shape, dt=F32):
            return ctx.enter_context(nc.sbuf_tensor(name, shape, dt))

        used = []

        def sem(name):
            used.append(ctx.enter_context(nc.semaphore(name)))
            return used[-1]

        ident = sb("ident_r", [64, 64])
        hrow = sb("hrow", [64, N])
        lrow = sb("lrow", [64, N])
        hcol = sb("hcol", [128, NT, M * B])
        lcol = sb("lcol", [128, NT, M * B])
        hall = sb("hall", [128, 2, M, N])
        lall = sb("lall", [128, 2, M, N])
        diff = sb("diff", [128, 4, N])
        sign = sb("sign", [128, NT, N], F16)
        minus = sb("minus", [128, 1], F16)
        tally = sb("tally", [128, M * B, NT])
        cols = sb("cols", [128, NT - 1, M, B])
        tp = ctx.enter_context(nc.psum_tensor("tp_r", [128, 2, 512], F32))
        pc = ctx.enter_context(nc.psum_tensor("pc_r", [128, 2, NT - 1, 512], F32))

        rows_in = sem("rows_in")
        turned = sem("turned")
        cols_ready = sem("cols_ready")
        all_in = [sem("all_in0"), sem("all_in1")]
        diff_ready = sem("diff_ready")
        tallied = sem("tallied")
        sign_used = sem("sign_used")
        cols_read = sem("cols_read")
        ctx.callback(clear, nc, used)
        block = ctx.enter_context(nc.Block())

        @block.sync
        def _(sp):
            sp.dma_start(ident[:, :], io["ident"][0:64, 0:64]).then_inc(rows_in, 16)
            sp.dma_start(hrow[:, :], scratch["hi"].rearrange("m b n -> (m b) n")).then_inc(rows_in, 16)
            sp.dma_start(lrow[:, :], scratch["lo"].rearrange("m b n -> (m b) n")).then_inc(rows_in, 16)
            with sp.Fori(0, B // 2) as i:
                for k in range(2):
                    sp.wait_ge(diff_ready, i * (2 * M * NT) + (k + 1) * M * NT)
                    for dst, src in ((hall, "hi"), (lall, "lo")):
                        sp.dma_start(dst[:, k, :, :],
                                     scratch[src][:, bass.ds(2 * i + k, 1), :].rearrange("m b n -> (m b) n")
                                     .partition_broadcast(128)).then_inc(all_in[k], 16)

        @block.tensor
        def _(pe):
            pe.wait_ge(rows_in, 48)
            for t in range(NT):
                nc.tensor.transpose(tp[:, 0, t * 64:t * 64 + 64], hrow[:, t * 128:(t + 1) * 128], ident[:, :])
                last = nc.tensor.transpose(tp[:, 1, t * 64:t * 64 + 64], lrow[:, t * 128:(t + 1) * 128], ident[:, :])
            last.then_inc(turned, 1)
            pe.sem_inc(sign_used, NT - 1)
            pe.wait_ge(cols_ready, 3)
            with pe.Fori(0, B // 2) as i:
                for k in range(2):
                    b = 2 * i + k
                    pe.wait_ge(cols_read, b + 1)
                    for m in range(M):
                        for t in range(NT - 1):
                            pe.wait_ge(tallied, b * (M * NT) + (m * NT + t + 5))
                            for c in range(t + 1, NT):
                                last = nc.tensor.matmul(pc[:, k, c - 1, m:m + 1], sign[:, t, c * 128:(c + 1) * 128],
                                                        minus[:, :], start=t == 0, stop=t == c - 1)
                            last.then_inc(sign_used, 1)

        @block.vector
        def _(dve):
            v = nc.vector
            dve.wait_ge(turned, 1)
            v.tensor_copy(hcol[:, :, :], tp[:, 0, 0:NT * 64].rearrange("p (t r) -> p t r", t=NT)).then_inc(cols_ready, 1)
            v.tensor_scalar(lcol[:, :, :], tp[:, 1, 0:NT * 64].rearrange("p (t r) -> p t r", t=NT), -1.0, None,
                            ALU.mult).then_inc(cols_ready, 1)
            v.memset(minus[:, :], -1.0).then_inc(cols_ready, 1)
            dve.wait_ge(cols_ready, 3)
            dve.sem_inc(diff_ready, 2 * M * NT)
            dve.sem_inc(cols_read, 2)

            def step(k, at):
                if at(0):
                    b, i = at(0)
                    dve.wait_ge(all_in[k], 32 * i + 32)
                    for m in range(M):
                        for t in range(NT):
                            j = m * NT + t
                            dve.wait_ge(tallied, b * (M * NT) + (j + 1))
                            ins = v.scalar_tensor_tensor(
                                diff[:, j % 4, t * 128:], hall[:, k, m, t * 128:],
                                hcol[:, t, bass.ds(b + m * B, 1)], lall[:, k, m, t * 128:], ALU.subtract, ALU.add)
                            ins.then_inc(diff_ready, 1)
                if at(1):
                    (b, _), k = at(1), (k - 1) % 2
                    dve.wait_ge(sign_used, b * (M * (NT - 1)) + (M + 1) * (NT - 1))
                    v.tensor_copy(cols[:, :, :, bass.ds(b, 1)], pc[:, k, :, 0:M].unsqueeze(3)).then_inc(cols_read, 1)

            steps(dve, step, B, 2)
            dve.wait_ge(tallied, B * M * NT + 4)
            v.tensor_scalar(rank[:, :, :], tally[:, :, :], -0.5, (N - 1) / 2.0, ALU.mult, ALU.add)\
                .then_inc(cols_ready, 1)
            dve.wait_ge(cols_ready, 4)
            dve.wait_ge(cols_read, B + 2)
            v.scalar_tensor_tensor(rank[:, :, 1:], cols[:, :, :, :].rearrange("p c m b -> p (m b) c"), -0.5,
                                   rank[:, :, 1:], ALU.mult, ALU.add).then_inc(cols_ready, 1)

        @block.scalar
        def _(act):
            act.wait_ge(cols_ready, 2)
            act.sem_inc(tallied, 4)
            act.wait_ge(sign_used, NT - 1)
            with act.Fori(0, B) as b:
                for m in range(M):
                    for t in range(NT):
                        j = m * NT + t
                        act.wait_ge(diff_ready, b * (M * NT) + (2 * M * NT + j + 1))
                        act.wait_ge(tallied, b * (M * NT) + (j + 1))
                        if t < NT - 1:
                            act.wait_ge(sign_used, b * (M * (NT - 1)) + (m * (NT - 1) + t + 1))
                        ins = nc.scalar.activation(sign[:, t, t * 128:], diff[:, j % 4, t * 128:], ACT.Sign,
                                                   bias=lcol[:, t, bass.ds(b + m * B, 1)],
                                                   accum_out=tally[:, bass.ds(b + m * B, 1), t])
                        ins.then_inc(tallied, 1)


def inverse_root(v, link, out, var, root, tmp):
    link(v.reciprocal(out, root))
    link(v.tensor_tensor(tmp, out, out, ALU.mult))
    link(v.tensor_tensor(tmp, tmp, var, ALU.mult))
    link(v.tensor_scalar(tmp, tmp, -0.5, 1.5, ALU.mult, ALU.add))
    return link(v.tensor_tensor(out, out, tmp, ALU.mult))


def split16(v, link, high, low, whole):
    link(v.tensor_copy(high, whole))
    return link(v.tensor_tensor(low, whole, high, ALU.subtract))


def fold_weights(nc, io, layer, O, W):
    with ExitStack() as ctx:
        def sb(name, shape, dt=F32):
            return ctx.enter_context(nc.sbuf_tensor(name + layer, shape, dt))

        used = []

        def sem(name):
            used.append(ctx.enter_context(nc.semaphore(name + "_fw" + layer)))
            return used[-1]

        ident = sb("ident_w", [128, 128])
        lin = sb("lin", [64, 256])
        convT = sb("convT", [64, 128])
        blin = sb("blin", [64, 1])
        eff = sb("eff", [128, 256])
        inv = sb("inv", [128, 1])
        pw = ctx.enter_context(nc.psum_tensor("pw" + layer, [128, 4, 512], F32))
        w_in = sem("w_in")
        folded = sem("folded")
        scaled = sem("scaled")
        turned = sem("w_turned")
        v_chain = sem("v_chain_w")
        ctx.callback(clear, nc, used)
        block = ctx.enter_context(nc.Block())

        @block.sync
        def _(sp):
            sp.dma_start(ident[:, :], io["ident"]).then_inc(w_in, 16)
            sp.dma_start(lin[:, :], io["lin" + layer]).then_inc(w_in, 16)
            sp.dma_start(convT[:, :], io["convT" + layer]).then_inc(w_in, 16)
            sp.dma_start(blin[:, :], io["blin" + layer]).then_inc(w_in, 16)

        @block.tensor
        def _(pe):
            pe.wait_ge(w_in, 64)
            nc.tensor.matmul(pw[:, 0, 0:256], convT[:, :], lin[:, :], start=True, stop=True)
            nc.tensor.matmul(pw[:, 1, 0:1], convT[:, :], blin[:, :], start=True, stop=True).then_inc(folded, 1)
            pe.wait_ge(scaled, 1)
            nc.tensor.transpose(pw[:, 2, 0:O], eff[0:O, 0:128], ident[0:O, 0:O])
            nc.tensor.transpose(pw[:, 3, 0:O], eff[0:O, 128:256], ident[0:O, 0:O]).then_inc(turned, 1)

        @block.vector
        def _(dve):
            v = nc.vector
            link = chain(dve, v_chain)
            dve.wait_ge(folded, 1)
            link(v.tensor_copy(W["bias"][:, :], pw[:, 1, 0:1]))
            link(v.tensor_reduce(W["amax"][:, :], pw[:, 0, 0:256], X, ALU.max, apply_absolute_value=True))
            link(v.tensor_scalar(W["amax"][:, :], W["amax"][:, :], 1e-30, None, ALU.max))
            link(v.reciprocal(inv[:, :], W["amax"][:, :]))
            v.tensor_scalar(eff[:, :], pw[:, 0, 0:256], inv[:, :], None, ALU.mult).then_inc(scaled, 1)
            dve.wait_ge(turned, 1)
            split16(v, link, W["center_hi"][:, 0:O], W["center_lo"][:, 0:O], pw[:, 2, 0:O])
            split16(v, link, W["neigh_hi"][:, 0:O], W["neigh_lo"][:, 0:O], pw[:, 3, 0:O])



def steps(eng, step, T, U):
    for s in list(range(U)):
        step(s % U, lambda lag, s=s: (s - lag, (s - lag) // U) if 0 <= s - lag < T else None)
    with eng.Fori(1, T // U) as i:
        for k in range(U):
            step(k, lambda lag, k=k: (i * U + (k - lag), i + (k - lag) // U))
    for s in range(T, T + U):
        step(s % U, lambda lag, s=s: (s - lag, (s - lag) // U) if 0 <= s - lag < T else None)


def gather_windows(nc, io, scratch, layer, feats, runs, perm, rank):
    with ExitStack() as ctx:
        def sb(name, shape, dt=F32):
            return ctx.enter_context(nc.sbuf_tensor(name + layer, shape, dt))

        used = []

        def sem(name):
            used.append(ctx.enter_context(nc.semaphore(name + "_gw" + layer)))
            return used[-1]

        H2 = EXT // 2
        ident = sb("ident_g", [32, 32])
        rep = sb("rep", [32, 128])
        place = sb("place", [128, EXT], F16)
        fb = sb("fb", [32, 2, N])
        t16 = sb("t16", [128, 2, NT * C], F16)
        l16 = sb("l16", [128, 2, NT * C], F16)
        FX = sb("FX", [128, 2, 2, M * NT * 128], F16)
        onehot = sb("onehot", [128, 2, M * NT, EXT], F16)
        ext = sb("ext", [128, 4, EXT])
        cen = sb("cen", [128, 4, PADN])
        cen16 = sb("cen16", [128, 4, PADN], F16)
        qt = sb("QT", [128, 4, GROUPS * GC], F16)
        QT = qt[:, :, :].rearrange("p b (g x s) -> p b g x s", g=GROUPS, x=32)
        ptok = ctx.enter_context(nc.psum_tensor("ptok" + layer, [128, 2, 512], F32))
        pcen = ctx.enter_context(nc.psum_tensor("pcen" + layer, [128, 2, 512], F32))
        pext = ctx.enter_context(nc.psum_tensor("pext" + layer, [128, 2, 2, 512], F32))

        const_in = sem("const_in")
        zeroed = sem("zeroed")
        fx_zeroed = sem("fx_zeroed")
        f_in = [sem("f_in0"), sem("f_in1")]
        f_used = sem("f_used")
        t16_ready = sem("t16_ready")
        l16_ready = sem("l16_ready")
        fx_ready = sem("fx_ready")
        hot_ready = sem("hot_ready")
        gathered = sem("gathered")
        ext_ready = sem("ext_ready")
        cen_ready = sem("cen_ready")
        q_v = sem("q_v")
        q_g = sem("q_g")
        q_out = [sem(f"q_out{k}") for k in range(4)]
        QV, QG = 8, 4
        ctx.callback(clear, nc, used)
        block = ctx.enter_context(nc.Block())

        def window_rows(eng, k, n, sem_):
            last = None
            for g0, g1, s0, s1 in ((0, 1, 2, SUBS), (1, GROUPS - 1, 0, SUBS),
                                   (GROUPS - 1, GROUPS, 0, NSUB - SUBS * (GROUPS - 1))):
                base = 44 + n + GP * g0 + PTS * s0
                at = ext[:, k, base:base + 1]
                ctr = cen[:, k, GP * g0 + PTS * s0 + n:GP * g0 + PTS * s0 + n + 1]
                G, U = g1 - g0, s1 - s0
                src = bass.AP(at.tensor, at.offset, [at.ap[0], [GP, G], [1, K], [PTS, U]])
                cbc = bass.AP(ctr.tensor, ctr.offset, [ctr.ap[0], [GP, G], [0, K], [PTS, U]])
                last = eng.tensor_tensor(QT[:, k, g0:g1, n * K:(n + 1) * K, s0:s1], src, cbc, ALU.subtract)
                last.then_inc(sem_, 1)
            U = 2 if n < LEAD - PTS else 1
            at = ext[:, k, K * n:K * n + 1]
            ctr = cen[:, k, n:n + 1]
            src = bass.AP(at.tensor, at.offset, [at.ap[0], [1, K], [K * PTS, U]])
            cbc = bass.AP(ctr.tensor, ctr.offset, [ctr.ap[0], [0, K], [PTS, U]])
            eng.tensor_tensor(QT[:, k, 0, n * K:(n + 1) * K, 0:U], src, cbc, ALU.subtract).then_inc(sem_, 1)

        @block.sync
        def _(sp):
            sp.dma_start(ident[:, :], io["ident"][0:32, 0:32]).then_inc(const_in, 16)
            sp.dma_start(rep[:, :], io["rep"]).then_inc(const_in, 16)
            sp.dma_start(place[:, :], io["place"]).then_inc(const_in, 16)

            def step(k, at):
                if at(0):
                    b, _ = at(0)
                    sp.wait_ge(f_used, b + 1)
                    for s0, n0, n1 in runs:
                        sp.dma_start(fb[:, k % 2, n0:n1], feats[:, bass.ds(b, 1), s0:s0 + n1 - n0]
                                     .rearrange("c b n -> c (b n)")).then_inc(f_in[k % 2], 16)
                if at(3):
                    (b, _), k = at(3), (k - 3) % 4
                    sp.wait_ge(q_v, b * QV + 5 * QV)
                    sp.wait_ge(q_g, b * QG + 5 * QG)
                    sp.dma_start(scratch["q16"][bass.ds(b * GROUPS, GROUPS), :, :].rearrange("g p x -> p g x"),
                                 QT[:, k, :, :, :].rearrange("p g x s -> p g (x s)")).then_inc(q_out[k], 16)
                    sp.dma_start(scratch["c16"][bass.ds(b * GROUPS, GROUPS), :, :].rearrange("g p x -> p g x"),
                                 cen16[:, k, :].rearrange("p (g x) -> p g x", g=GROUPS)).then_inc(q_out[k], 16)

            steps(sp, step, B, 4)
            for k in range(4):
                sp.wait_ge(q_out[k], 32 * (B // 4) + 32)

        @block.gpsimd
        def _(pool):
            nc.gpsimd.memset(cen[:, :, :], 0.0).then_inc(zeroed, 1)
            nc.gpsimd.memset(cen16[:, :, :], 0.0).then_inc(zeroed, 1)
            nc.gpsimd.memset(qt[:, :, :].bitcast(F32), 0.0).then_inc(zeroed, 1)
            pool.wait_ge(zeroed, 3)
            for k in range(4):
                pool.sem_inc(q_out[k], 32)
            pool.sem_inc(q_g, 4 * QG)

            def step(k, at):
                if at(2):
                    (b, i), k = at(2), (k - 2) % 4
                    pool.wait_ge(ext_ready, b + 3)
                    pool.wait_ge(cen_ready, b + 3)
                    pool.wait_ge(q_out[k], i * 32 + 32)
                    window_rows(nc.gpsimd, k, 1, q_g)

            steps(pool, step, B, 4)

        @block.vector
        def _(dve):
            v = nc.vector
            for hl in range(2):
                v.memset(FX[:, hl, :, :].bitcast(F32), 0.0).then_inc(fx_zeroed, 1)
            dve.wait_ge(const_in, 48)
            dve.wait_ge(fx_zeroed, 2)
            dve.sem_inc(l16_ready, 2)
            dve.sem_inc(q_v, 4 * QV)

            def step(k, at):
                if at(0):
                    (b, _), h = at(0), k % 2
                    dve.wait_ge(f_used, b + 3)
                    dve.wait_ge(gathered, b + 1)
                    v.tensor_copy(t16[:, h, :], ptok[:, h, 0:NT * C]).then_inc(t16_ready, 1)
                    dve.wait_ge(t16_ready, b + 1)
                    v.tensor_tensor(l16[:, h, :], ptok[:, h, 0:NT * C], t16[:, h, :],
                                    ALU.subtract).then_inc(l16_ready, 1)
                    dve.wait_ge(l16_ready, b + 3)
                    for hl, src in enumerate((t16, l16)):
                        fx = FX[:, hl, h, 0:1]
                        dst = bass.AP(fx.tensor, fx.offset, [fx.ap[0], [NT * 128 + 1, M], [M, NT * C]])
                        v.tensor_copy(dst, src[:, h, :].unsqueeze(1).to_broadcast([128, M, NT * C]))\
                            .then_inc(fx_ready, 1)
                    for m in range(M):
                        for t in range(NT):
                            v.tensor_scalar(onehot[:, h, m * NT + t, :], place[:, :],
                                            rank[:, bass.ds(b + perm[m] * B, 1), t], None,
                                            ALU.is_equal).then_inc(hot_ready, 1)
                if at(2):
                    (b, i), k = at(2), (k - 2) % 4
                    dve.wait_ge(zeroed, 3)
                    dve.wait_ge(ext_ready, b + 3)
                    dve.wait_ge(cen_ready, b + 3)
                    dve.wait_ge(q_out[k], i * 32 + 32)
                    window_rows(v, k, 0, q_v)
                    window_rows(v, k, 2, q_v)

            steps(dve, step, B, 4)

        @block.tensor
        def _(pe):
            pe.wait_ge(const_in, 48)
            pe.sem_inc(f_used, 2)
            pe.sem_inc(gathered, 2)

            def step(k, at):
                if at(0):
                    (b, i), h = at(0), k % 2
                    pe.wait_ge(f_in[h], (i * 32 + 16 * (k // 2 + 1)) * len(runs))
                    pe.wait_ge(l16_ready, b + 1)
                    pe.wait_ge(cen_ready, b + 1)
                    nc.tensor.matmul(pcen[:, h, 0:N], rep[:, :], fb[:, h, :], start=True, stop=True)
                    for t in range(NT):
                        last = nc.tensor.transpose(ptok[:, h, t * C:(t + 1) * C],
                                                   fb[:, h, t * 128:(t + 1) * 128], ident[:, :])
                    last.then_inc(f_used, 1)
                if at(1):
                    (b, _), k = at(1), (k - 1) % 4
                    h = k % 2
                    pe.wait_ge(fx_ready, b * 2 + 2)
                    pe.wait_ge(hot_ready, b * M * NT + M * NT)
                    pe.wait_ge(ext_ready, b + 1)
                    for e in range(2):
                        for n in range(2 * M * NT):
                            hl, mt = n // (M * NT), n % (M * NT)
                            last = nc.tensor.matmul(pext[:, h, e, 0:H2], FX[:, hl, h, mt * 128:(mt + 1) * 128],
                                                    onehot[:, h, mt, e * H2:(e + 1) * H2],
                                                    start=n == 0, stop=n == 2 * M * NT - 1)
                    last.then_inc(gathered, 1)

            steps(pe, step, B, 4)

        @block.scalar
        def _(act):
            act.sem_inc(cen_ready, 2)
            act.sem_inc(ext_ready, 2)
            act.wait_ge(zeroed, 2)

            def step(k, at):
                if at(0):
                    b, i = at(0)
                    act.wait_ge(q_out[k], i * 32 + 32)
                    act.wait_ge(q_v, b * QV + QV)
                    act.wait_ge(q_g, b * QG + QG)
                    act.wait_ge(f_used, b + 3)
                    for s0, n0, n1 in RUNS:
                        nc.scalar.activation(cen16[:, k, s0:s0 + n1 - n0], pcen[:, k % 2, n0:n1], ACT.Copy)
                        last = nc.scalar.activation(cen[:, k, s0:s0 + n1 - n0], pcen[:, k % 2, n0:n1], ACT.Copy)
                    last.then_inc(cen_ready, 1)
                if at(1):
                    (b, _), k = at(1), (k - 1) % 4
                    act.wait_ge(gathered, b + 3)
                    act.wait_ge(q_v, b * QV + QV)
                    act.wait_ge(q_g, b * QG + QG)
                    nc.scalar.activation(ext[:, k, :].rearrange("p (e x) -> p e x", e=2), pext[:, k % 2, :, 0:H2],
                                         ACT.Copy).then_inc(ext_ready, 1)

            steps(act, step, B, 4)


def window_attention(nc, io, scratch, layer, O, W, hmax, stat):
    T = B * GROUPS
    NB = 8
    ND = 4
    SB = 512 // O if O * SUBS > 512 else SUBS
    NVB = -(-SUBS // SB)
    SL = 128 // O
    with ExitStack() as ctx:
        def sb(name, shape, dt=F32):
            return ctx.enter_context(nc.sbuf_tensor(name + layer, shape, dt))

        def ps(name, shape):
            return ctx.enter_context(nc.psum_tensor(name + layer, shape, F32))

        used = []

        def sem(name):
            used.append(ctx.enter_context(nc.semaphore(name + "_wa" + layer)))
            return used[-1]

        maskL = sb("maskL", [PTS, 128], F16)
        maskR = sb("maskR", [PTS, GC], F16)
        QX = sb("QX", [128, NB, 4 * GC], F16)
        QR = sb("QR", [128, NB, GC], F16)
        CT = sb("CT", [128, NB, GP], F16)
        Sc = sb("Sc", [128, ND, GC])
        mx = sb("mx", [128, ND, SUBS])
        Dm = sb("Dm", [128, ND, GC])
        E = sb("E", [128, ND, GC])
        Z = sb("Z", [128, ND, SUBS])
        R = sb("R", [128, ND, SUBS])
        A = sb("Ap", [128, ND, GC])
        AT = sb("AT", [128, ND, GC])
        Vs = sb("Vs", [128, NB, SUBS * O])
        Hs = sb("Hs", [128, 2, SUBS * PTS * K])
        junk = sb("junk", [128, 2, SUBS * PTS * K])
        pS = ps("pS", [128, 2, 512])
        pV = ps("pV", [128, 2, NVB, 512])
        pH = ps("pH", [128, 2, 512])

        const_in = sem("const_in")
        zeroed = sem("zeroed")
        q_in = [sem(f"q_in{k}") for k in range(NB // 2)]
        c_in = [sem(f"c_in{k}") for k in range(NB // 2)]
        scored = sem("scored")
        scores_out = sem("scores_out")
        shifted = sem("shifted")
        projected = sem("projected")
        max_ready = sem("max_ready")
        exped = sem("exped")
        summed = sem("summed")
        r_ready = sem("r_ready")
        probs = sem("probs")
        turned = sem("turned_p")
        vs_ready = sem("vs_ready")
        mixed = sem("mixed")
        hmax_done = sem("hmax_done")
        copied = sem("copied")
        squared = sem("squared")
        ctx.callback(clear, nc, used)
        block = ctx.enter_context(nc.Block())

        def pack(r, k):
            return r * (NB // SL) + k // SL

        @block.sync
        def _(sp):
            sp.dma_start(maskL[:, :], io["maskL"]).then_inc(const_in, 16)
            sp.dma_start(maskR[:, :], io["maskR"]).then_inc(const_in, 16)

            def step(k, at):
                if at(0) and k % 2 == 0:
                    t, _ = at(0)
                    sp.wait_ge(zeroed, k // 2 + 1)
                    sp.wait_ge(projected, t + 2)
                    src = scratch["q16"][bass.ds(t, 2), :, :].rearrange("g p x -> p g x")
                    for h in range(4):
                        sp.dma_start(QX[32 * h:32 * h + 32, k:k + 2, h * GC:(h + 1) * GC],
                                     src[32 * h:32 * h + 32, :, :]).then_inc(q_in[k // 2], 16)
                    sp.dma_start(QR[:, k:k + 2, :], src).then_inc(q_in[k // 2], 16)
                if at(2) and k % 2 == 0:
                    (t, _), k = at(2), (k - 2) % NB
                    sp.wait_ge(mixed, t + 2)
                    sp.dma_start(CT[:, k:k + 2, :], scratch["c16"][bass.ds(t, 2), :, :]
                                 .rearrange("g p x -> p g x")).then_inc(c_in[k // 2], 16)

            steps(sp, step, T, NB)

        @block.tensor
        def _(pe):
            pe.sem_inc(projected, NB)
            pe.sem_inc(mixed, NB)
            pe.wait_ge(const_in, 32)

            def step(k, at):
                if at(0):
                    t, r = at(0)
                    p = k % 2
                    qx = [QX[:, k, :].rearrange("p (c s) -> p c s", s=SUBS)[:, :, u] for u in range(SUBS)]
                    qr = [QR[:, k, :].rearrange("p (c s) -> p c s", s=SUBS)[:, :, u] for u in range(SUBS)]
                    pe.wait_ge(q_in[k // 2], r * 80 + 80)
                    pe.wait_ge(scores_out, t + 1)
                    nc.tensor.matmul(pS[:, p, 0:GC], maskL[:, :], maskR[:, :], start=True, stop=False)
                    for u in range(SUBS):
                        last = nc.tensor.matmul(pS[:, p, 32 * u:32 * u + 32], qx[u], qr[u],
                                                start=False, stop=u == SUBS - 1)
                    last.then_inc(scored, 1)
                    pe.wait_ge(vs_ready, t + 1)
                    for u in range(SUBS):
                        o = (u % SB) * O
                        nc.tensor.matmul(pV[:, p, u // SB, o:o + O], qx[u], W["neigh_hi"][:, 0:O], start=True, stop=False)
                        last = nc.tensor.matmul(pV[:, p, u // SB, o:o + O], qx[u], W["neigh_lo"][:, 0:O],
                                                start=False, stop=True)
                    last.then_inc(projected, 1)
                if at(6):
                    t, r = at(6)
                    k3 = (k - 6) % NB
                    p, slot = k3 // SL % 2, k3 % SL
                    pe.wait_ge(c_in[k3 // 2], r * 16 + 16)
                    if slot == 0:
                        pe.wait_ge(copied, pack(r, k3) + 1)
                    out = pH[slot * O:(slot + 1) * O, p, 0:GC].rearrange("p (s x) -> p s x", x=32)[:, :, 0:PTS * K]\
                        .rearrange("p s (n j) -> p s n j", n=PTS)
                    ctr = CT[:, k3, :].rearrange("p (s n) -> p s n", n=PTS).unsqueeze(3)\
                        .to_broadcast([128, SUBS, PTS, K])
                    nc.tensor.matmul(out, W["center_hi"][:, 0:O], ctr, start=True, stop=False)
                    nc.tensor.matmul(out, W["center_lo"][:, 0:O], ctr, start=False, stop=False)
                    pe.wait_ge(vs_ready, t + 3)
                    pe.wait_ge(turned, t + 1 + ND)
                    for u in range(SUBS):
                        last = nc.tensor.matmul(pH[slot * O:(slot + 1) * O, p, 32 * u:32 * u + PTS * K], Vs[:, k3, u * O:(u + 1) * O],
                                                AT[:, k3 % ND, 32 * u:32 * u + PTS * K], start=False, stop=u == SUBS - 1)
                    last.then_inc(mixed, 1)

            steps(pe, step, T, NB)

        @block.vector
        def _(dve):
            v = nc.vector
            for k in range(0, NB, 2):
                v.memset(QX[:, k:k + 2, :].bitcast(F32), 0.0).then_inc(zeroed, 1)
            dve.sem_inc(turned, ND)
            dve.sem_inc(hmax_done, 2)

            def step(k, at):
                if at(1):
                    (t, _), p = at(1), (k - 1) % ND
                    dve.wait_ge(scores_out, t + 3)
                    dve.wait_ge(shifted, t + 1)
                    v.tensor_reduce(mx[:, p, :], Sc[:, p, :].rearrange("p (s x) -> p s x", x=32), X,
                                    ALU.max).then_inc(max_ready, 1)
                if at(4):
                    (t, _), p = at(4), (k - 4) % ND
                    dve.wait_ge(exped, t + 1 + ND)
                    v.tensor_reduce(Z[:, p, :], E[:, p, :].rearrange("p (s x) -> p s x", x=32), X,
                                    ALU.add).then_inc(summed, 1)
                if at(5):
                    (t, _), p = at(5), (k - 5) % ND
                    dve.wait_ge(probs, t + 1 + ND)
                    dve.wait_ge(mixed, t + 1 + NB - ND)
                    v.transpose(AT[:, p, :], A[:, p, :]).then_inc(turned, 1)
                if at(4):
                    (t, _), p = at(4), (k - 4) % ND
                    dve.wait_ge(summed, t + 1)
                    v.reciprocal(R[:, p, :], Z[:, p, :]).then_inc(r_ready, 1)
                if at(7) and (k - 7) % SL == SL - 1:
                    (_, r), k6 = at(7), (k - 7) % NB
                    q, p = pack(r, k6), k6 // SL % 2
                    dve.wait_ge(copied, q + 3)
                    dve.wait_ge(squared, q + 3)
                    v.tensor_reduce(hmax[:, bass.ds(q * GP, GP)],
                                    Hs[:, p, :].rearrange("p (n j) -> p n j", j=K), X, ALU.max).then_inc(hmax_done, 1)

            steps(dve, step, T, NB)

        @block.gpsimd
        def _(pool):
            pool.sem_inc(probs, ND)
            pool.sem_inc(shifted, ND)

            def step(k, at):
                if at(1):
                    (t, _), p = at(1), (k - 1) % ND
                    pool.wait_ge(max_ready, t + 1)
                    pool.wait_ge(exped, t + 1)
                    nc.gpsimd.tensor_tensor(Dm[:, p, :].rearrange("p (s x) -> p s x", x=32),
                                            Sc[:, p, :].rearrange("p (s x) -> p s x", x=32),
                                            mx[:, p, :].unsqueeze(2).to_broadcast([128, SUBS, 32]),
                                            ALU.subtract).then_inc(shifted, 1)
                if at(4):
                    (t, _), p = at(4), (k - 4) % ND
                    pool.wait_ge(r_ready, t + 1)
                    pool.wait_ge(turned, t + 1)
                    nc.gpsimd.tensor_tensor(A[:, p, :].rearrange("p (s x) -> p s x", x=32),
                                            E[:, p, :].rearrange("p (s x) -> p s x", x=32),
                                            R[:, p, :].unsqueeze(2).to_broadcast([128, SUBS, 32]),
                                            ALU.mult).then_inc(probs, 1)

            steps(pool, step, T, NB)

        @block.scalar
        def _(act):
            act.sem_inc(vs_ready, 2)
            act.sem_inc(scores_out, 2)
            act.sem_inc(exped, ND)
            act.sem_inc(copied, 2)
            act.sem_inc(squared, 2)

            def step(k, at):
                if at(1):
                    (t, _), p = at(1), (k - 1) % 2
                    act.wait_ge(scored, t + 1)
                    act.wait_ge(shifted, t + 1)
                    nc.scalar.activation(Sc[:, (k - 1) % ND, :], pS[:, p, 0:GC], ACT.Copy).then_inc(scores_out, 1)
                if at(1):
                    (t, _), p, kv = at(1), (k - 1) % 2, (k - 1) % NB
                    act.wait_ge(projected, t + 1 + NB)
                    act.wait_ge(mixed, t + 1)
                    for c in range(NVB):
                        n = min(SB, SUBS - c * SB) * O
                        last = nc.scalar.activation(Vs[:, kv, c * SB * O:c * SB * O + n], pV[:, p, c, 0:n], ACT.Copy)
                    last.then_inc(vs_ready, 1)
                if at(7) and (k - 7) % SL == SL - 1:
                    (t, r), k6 = at(7), (k - 7) % NB
                    q, p = pack(r, k6), k6 // SL % 2
                    rows = pH[:, p, 0:GC].rearrange("p (s x) -> p s x", x=32)[:, :, 0:PTS * K]
                    act.wait_ge(mixed, t + 1 + NB)
                    act.wait_ge(hmax_done, q + 1)
                    nc.scalar.activation(Hs[:, p, :].rearrange("p (s x) -> p s x", x=PTS * K), rows, ACT.Copy,
                                         accum_out=stat[:, 0, bass.ds(q, 1)]).then_inc(copied, 1)
                if at(3):
                    (t, _), p = at(3), (k - 3) % ND
                    act.wait_ge(shifted, t + 1 + ND)
                    act.wait_ge(probs, t + 1)
                    nc.scalar.activation(E[:, p, :], Dm[:, p, :], ACT.Exp, scale=32.0 ** -0.5).then_inc(exped, 1)
                if at(7) and (k - 7) % SL == SL - 1:
                    (_, r), k6 = at(7), (k - 7) % NB
                    q, p = pack(r, k6), k6 // SL % 2
                    act.wait_ge(copied, q + 3)
                    act.wait_ge(squared, q + 1)
                    nc.scalar.activation(junk[:, p, :], Hs[:, p, :], ACT.Square,
                                         accum_out=stat[:, 1, bass.ds(q, 1)]).then_inc(squared, 1)

            steps(act, step, T, NB)


def instance_norm(nc, io, scratch, layer, O, W, hmax, stat, dst):
    SL = 128 // O
    PK = GROUPS // SL
    with ExitStack() as ctx:
        def sb(name, shape, dt=F32):
            return ctx.enter_context(nc.sbuf_tensor(name + layer, shape, dt))

        used = []

        def sem(name):
            used.append(ctx.enter_context(nc.semaphore(name + "_in" + layer)))
            return used[-1]

        merge = sb("merge", [128, 128])
        part = sb("part", [128, 2, B])
        tot = sb("tot", [128, 2, B])
        mean = sb("mean", [128, B])
        var = sb("var", [128, B])
        root = sb("root", [128, B])
        rstd = sb("rstd_i", [128, B])
        tmp = sb("tmp_i", [128, B])
        pm = ctx.enter_context(nc.psum_tensor("pm" + layer, [128, 512], F32))
        merge_in = sem("merge_in")
        part_ready = sem("part_ready")
        merged = sem("merged")
        var_ready = sem("var_ready_i")
        root_ready = sem("root_ready_i")
        y_ready = sem("y_ready")
        stored = sem("stored_i")
        v_chain = sem("v_chain_i")
        ctx.callback(clear, nc, used)
        block = ctx.enter_context(nc.Block())

        @block.tensor
        def _(pe):
            pe.wait_ge(merge_in, 16)
            pe.wait_ge(part_ready, 1)
            nc.tensor.matmul(pm[:, 0:2 * B], merge[:, :], part[:, :, :].rearrange("p a b -> p (a b)"),
                             start=True, stop=True).then_inc(merged, 1)

        @block.scalar
        def _(act):
            act.wait_ge(var_ready, 1)
            nc.scalar.activation(root[:, :], var[:, :], ACT.Sqrt).then_inc(root_ready, 1)

        @block.vector
        def _(dve):
            v = nc.vector
            link = chain(dve, v_chain)
            amax, bias = W["amax"][:, :], W["bias"][:, :]
            v.tensor_reduce(part[:, :, :], stat[:, :, :].rearrange("p a (b g) -> p a b g", g=PK), X, ALU.add)\
                .then_inc(part_ready, 1)
            link(v.tensor_scalar(hmax[:, :], hmax[:, :], amax, bias, ALU.mult, ALU.add))
            dve.wait_ge(merged, 1)
            link(v.tensor_scalar(tot[:, :, :], pm[:, 0:2 * B].rearrange("p (a b) -> p a b", a=2), 1.0 / (N * K), None,
                                 ALU.mult))
            link(v.tensor_tensor(tmp[:, :], tot[:, 0, :], tot[:, 0, :], ALU.mult))
            link(v.tensor_tensor(var[:, :], tot[:, 1, :], tmp[:, :], ALU.subtract))
            link(v.tensor_scalar(var[:, :], var[:, :], 0.0, amax, ALU.max, ALU.mult))
            v.tensor_scalar(var[:, :], var[:, :], amax, EPS, ALU.mult, ALU.add).then_inc(var_ready, 1)
            dve.wait_ge(root_ready, 1)
            inverse_root(v, link, rstd[:, :], var[:, :], root[:, :], tmp[:, :])
            link(v.tensor_scalar(mean[:, :], tot[:, 0, :], amax, bias, ALU.mult, ALU.add))
            for b in range(B):
                y = hmax[:, b * PK * GP:(b + 1) * PK * GP]
                link(v.tensor_scalar(y, y, mean[:, b:b + 1], rstd[:, b:b + 1], ALU.subtract, ALU.mult))
            v.scalar_tensor_tensor(hmax[:, :], hmax[:, :], SLOPE, hmax[:, :], ALU.mult, ALU.max).then_inc(y_ready, 1)

        @block.sync
        def _(sp):
            sp.dma_start(merge[:, :], io["merge" + layer]).then_inc(merge_in, 16)
            sp.wait_ge(y_ready, 1)
            for sl in range(SL):
                sp.dma_start(dst.rearrange("c b (q l x) -> c (b q) l x", l=SL, x=GP)[:, :, sl, :],
                             hmax[sl * O:(sl + 1) * O, :].rearrange("p (q x) -> p q x", x=GP)).then_inc(stored, 16)
            sp.wait_ge(stored, 16 * SL)


def join_features(nc, io, scratch):
    with ExitStack() as ctx:
        def sb(name, shape, dt=F32):
            return ctx.enter_context(nc.sbuf_tensor(name, shape, dt))

        used = []

        def sem(name):
            used.append(ctx.enter_context(nc.semaphore(name)))
            return used[-1]

        f = sb("f_j", [4 * C, B, N])
        lat = sb("lat_j", [128, TT, D])
        w = sb("w_j", [4 * C, C])
        h = sb("h_j", [128, TT, N])
        st = sb("st_j", [128, TT, 6])
        mv = sb("mv_j", [128, TT, 2])
        root = sb("root_j", [128, TT])
        rstd = sb("rstd_j", [128, TT])
        var = sb("var_j", [128, TT])
        tmp = sb("tmp_j", [128, TT])
        ph = ctx.enter_context(nc.psum_tensor("ph_j", [128, TT, 512], F32))
        w_in = sem("w_in_j")
        f_in = [sem(f"f_in_j{q}") for q in range(TT)]
        lat_in = sem("lat_in_j")
        joined = sem("joined")
        var_ready = sem("var_ready_j")
        root_ready = sem("root_ready_j")
        x_ready = sem("x_ready_j")
        stored = sem("stored_j")
        v_chain = sem("v_chain_j")
        ctx.callback(clear, nc, used)
        block = ctx.enter_context(nc.Block())

        @block.sync
        def _(sp):
            sp.dma_start(w[:, :], io["conv3T"]).then_inc(w_in, 16)
            for q in range(TT):
                bs = slice(4 * q, 4 * q + 4)
                sp.dma_start(f[0:C, bs, :], scratch["f0"].rearrange("(b c) n -> c b n", c=C)[:, bs, :])\
                    .then_inc(f_in[q], 16)
                for s0, n0, n1 in RUNS:
                    sp.dma_start(f[C:2 * C, bs, n0:n1], scratch["f1"][:, bs, s0:s0 + n1 - n0]).then_inc(f_in[q], 16)
                    sp.dma_start(f[2 * C:4 * C, bs, n0:n1], scratch["f2"][:, bs, s0:s0 + n1 - n0])\
                        .then_inc(f_in[q], 16)
            sp.dma_start(lat[:, :, :], io["x"].rearrange("(t p) d -> p t d", p=128)).then_inc(lat_in, 16)
            for q in range(TT):
                sp.wait_ge(x_ready, q + 1)
                sp.dma_start(scratch["x1"][q * 128:(q + 1) * 128, :], h[:, q, :]).then_inc(stored, 16)
            sp.wait_ge(stored, 16 * TT)

        @block.tensor
        def _(pe):
            pe.wait_ge(w_in, 16)
            for q in range(TT):
                pe.wait_ge(f_in[q], 16 * (1 + 2 * len(RUNS)))
                for b in range(4):
                    last = nc.tensor.matmul(ph[b * C:(b + 1) * C, q, :], w[:, :], f[:, 4 * q + b, :],
                                            start=True, stop=True)
                last.then_inc(joined, 1)

        @block.scalar
        def _(act):
            act.wait_ge(var_ready, 1)
            nc.scalar.activation(root[:, :], var[:, :], ACT.Sqrt).then_inc(root_ready, 1)

        @block.vector
        def _(dve):
            v = nc.vector
            link = chain(dve, v_chain)
            for q in range(TT):
                dve.wait_ge(joined, q + 1)
                link(v.bn_stats(st[:, q, :], ph[:, q, :]))
                link(v.bn_aggr(mv[:, q, :], st[:, q, :]))
            v.tensor_scalar(var[:, :], mv[:, :, 1], EPS, None, ALU.add).then_inc(var_ready, 1)
            dve.wait_ge(root_ready, 1)
            inverse_root(v, link, rstd[:, :], var[:, :], root[:, :], tmp[:, :])
            dve.wait_ge(lat_in, 16)
            for q in range(TT):
                link(v.tensor_scalar(h[:, q, :], ph[:, q, :], mv[:, q, 0:1], rstd[:, q:q + 1], ALU.subtract, ALU.mult))
                link(v.scalar_tensor_tensor(h[:, q, :], h[:, q, :], SLOPE, h[:, q, :], ALU.mult, ALU.max))
                v.tensor_tensor(h[:, q, :], h[:, q, :], lat[:, q, :], ALU.add).then_inc(x_ready, 1)


def cross_attention(nc, io, scratch):
    with ExitStack() as ctx:
        def sb(name, shape, dt=F32):
            return ctx.enter_context(nc.sbuf_tensor(name, shape, dt))

        rank = sb("rank", [128, M * B, NT])
        norm_and_keys(nc, io, scratch)
        ranks(nc, io, scratch, rank)
        f0 = scratch["f0"].rearrange("(b c) n -> c b n", c=C)
        for layer, O, feats, runs, perm, dst in (
                ("1", C, f0, ((0, 0, N),), (2, 0, 3, 1), scratch["f1"]),
                ("2", 2 * C, scratch["f1"], RUNS, (1, 3, 0, 2), scratch["f2"])):
            with ExitStack() as lctx:
                def lsb(name, shape, dt=F32):
                    return lctx.enter_context(nc.sbuf_tensor(name + layer, shape, dt))

                W = {n: lsb(n, [128, O], F16) for n in ("neigh_hi", "neigh_lo", "center_hi", "center_lo")}
                W["amax"] = lsb("amax", [128, 1])
                W["bias"] = lsb("bias", [128, 1])
                hmax = lsb("hmax", [128, B * PADN * O // 128])
                stat = lsb("stat", [128, 2, B * GROUPS * O // 128])
                fold_weights(nc, io, layer, O, W)
                gather_windows(nc, io, scratch, layer, feats, runs, perm, rank)
                window_attention(nc, io, scratch, layer, O, W, hmax, stat)
                instance_norm(nc, io, scratch, layer, O, W, hmax, stat, dst)
        join_features(nc, io, scratch)


def row_norm(nc, v, link, act_sqrt, src, dst, st, mv, tmp):
    for t in range(TT):
        link(v.bn_stats(st[:, t, :], src[:, t, :]))
        link(v.bn_aggr(mv[:, t, :], st[:, t, :]))
    root, rstd, rtmp = (tmp[:, i, :] for i in range(3))
    act_sqrt(v.tensor_scalar(mv[:, :, 1], mv[:, :, 1], EPS, None, ALU.add))
    inverse_root(v, link, rstd, mv[:, :, 1], root, rtmp)
    for t in range(TT):
        link(v.tensor_scalar(dst[:, t, :], src[:, t, :], mv[:, t, 0:1], rstd[:, t:t + 1],
                             ALU.subtract, ALU.mult))


def mamba_prepare(nc, io, scratch, P):
    with ExitStack() as ctx:
        def sb(name, shape, dt=F32):
            return ctx.enter_context(nc.sbuf_tensor(name, shape, dt))

        used = []

        def sem(name):
            used.append(ctx.enter_context(nc.semaphore(name)))
            return used[-1]

        ident = sb("ident_p", [128, 128])
        later = sb("later", [128, 128])
        upto = sb("upto", [128, S])
        x1 = sb("x1_p", [128, TT, D])
        xin = sb("xin", [128, TT, D])
        hn = sb("hn", [128, TT, D])
        st = sb("st_p", [128, TT, 6])
        mv = sb("mv_p", [128, TT, 2])
        tmp = sb("tmp_p", [128, 3, TT])
        ms = sb("ms_p", [128, 3, TT])
        nw = sb("nw", [128, DT])
        wdt = sb("wdt", [128, DT, 128])
        hp = sb("hp", [128, 2])
        aneg = sb("aneg", [128, 1])
        sp_ = sb("sp", [128, 6, TOK])
        dta = sb("dta", [128, 2, TOK])
        atok = sb("atok", [128, TT, HEADS])
        R = sb("R_p", [128, 2, HEADS, S])
        pt = ctx.enter_context(nc.psum_tensor("pt_p", [128, 4, 512], F32))
        pd = ctx.enter_context(nc.psum_tensor("pd_p", [128, 512], F32))
        pz = ctx.enter_context(nc.psum_tensor("pz_p", [128, 2, 512], F32))
        x_in = sem("x_in_p")
        w_in = sem("w_in_p")
        var_ready = sem("var_ready_p")
        root_ready = sem("root_ready_p")
        xin_ready = sem("xin_ready")
        squares = sem("squares_p")
        ms_ready = sem("ms_ready")
        ms_root = sem("ms_root")
        hn_ready = sem("hn_ready")
        turned = sem("turned_h")
        hT_ready = sem("hT_ready")
        dt_raw = sem("dt_raw")
        z_ready = sem("z_ready_p")
        exp_ready = sem("exp_ready_p")
        one_ready = sem("one_ready")
        ln_ready = sem("ln_ready")
        dta_ready = sem("dta_ready")
        dta_turned = sem("dta_turned")
        r_ready = sem("r_ready_p")
        seg_ready = sem("seg_ready")
        decay_ready = sem("decay_ready")
        v_chain = sem("v_chain_p")
        ctx.callback(clear, nc, used)
        block = ctx.enter_context(nc.Block())

        @block.sync
        def _(sp):
            sp.dma_start(x1[:, :, :], scratch["x1"].rearrange("(t p) d -> p t d", p=128)).then_inc(x_in, 16)
            for dst, src in ((P["conv"][:, :], io["conv"]), (ident[:, :], io["ident"]), (later[:, :], io["later"]), (upto[:, :], io["upto"]),
                             (nw[:, :], io["norm_w"]), (wdt[:, :, :], io["in_proj"][2 * CT_ + 2 * GR]),
                             (hp[:, :], io["head_par"])):
                sp.dma_start(dst, src).then_inc(w_in, 16)

        @block.scalar
        def _(act):
            act.wait_ge(var_ready, 1)
            nc.scalar.activation(tmp[:, 0, :], mv[:, :, 1], ACT.Sqrt).then_inc(root_ready, 1)
            act.wait_ge(xin_ready, 1)
            for t in range(TT):
                last = nc.scalar.activation(hn[:, t, :], xin[:, t, :], ACT.Square, accum_out=ms[:, 0, t:t + 1])
            last.then_inc(squares, 1)
            act.wait_ge(ms_ready, 1)
            nc.scalar.activation(ms[:, 1, :], ms[:, 0, :], ACT.Sqrt).then_inc(ms_root, 1)
            act.wait_ge(w_in, 112)
            nc.scalar.activation(aneg[:, :], hp[:, 1:2], ACT.Exp)
            act.wait_ge(z_ready, 1)
            nc.scalar.activation(sp_[:, 2, :], sp_[:, 1, :], ACT.Exp, scale=-1.0).then_inc(exp_ready, 1)
            act.wait_ge(one_ready, 1)
            nc.scalar.activation(sp_[:, 4, :], sp_[:, 3, :], ACT.Ln).then_inc(ln_ready, 1)
            for n in range(TT * 8):
                q, c = n // 8, n % 8
                act.wait_ge(seg_ready, n + 1)
                nc.scalar.activation(P["decay"][:, q, 16 * c:16 * c + 16, :].rearrange("p h i -> p (h i)"),
                                     pz[:, n % 2, :], ACT.Exp).then_inc(decay_ready, 1)

        @block.vector
        def _(dve):
            v = nc.vector
            link = chain(dve, v_chain)
            dve.wait_ge(x_in, 16)

            def act_sqrt(ins):
                ins.then_inc(var_ready, 1)
                dve.wait_ge(root_ready, 1)

            row_norm(nc, v, link, act_sqrt, x1, xin, st, mv, tmp)
            v.tensor_tensor(P["acc"][:, :, :], x1[:, :, :], xin[:, :, :], ALU.add).then_inc(xin_ready, 1)
            dve.wait_ge(squares, 1)
            v.tensor_scalar(ms[:, 0, :], ms[:, 0, :], 1.0 / D, EPS, ALU.mult, ALU.add).then_inc(ms_ready, 1)
            dve.wait_ge(ms_root, 1)
            inverse_root(v, link, ms[:, 2, :], ms[:, 0, :], ms[:, 1, :], tmp[:, 2, :])
            for t in range(TT):
                last = v.tensor_scalar(hn[:, t, :], xin[:, t, :], ms[:, 2, t:t + 1], None, ALU.mult)
            last.then_inc(hn_ready, 1)
            dve.wait_ge(w_in, 112)
            for d in range(DT):
                dve.wait_ge(turned, d + 1)
                v.tensor_scalar(P["hT"][:, d, :], pt[:, d, :], nw[:, d:d + 1], None, ALU.mult).then_inc(hT_ready, 1)
            dve.wait_ge(dt_raw, 1)
            z, az, w, u, lu, d_ = (sp_[:, i, :] for i in range(6))
            link(v.tensor_scalar(z, pd[:, :], hp[:, 0:1], None, ALU.add))
            link(v.tensor_scalar(az, z, -1.0, None, ALU.mult))
            v.tensor_tensor(az, az, z, ALU.max).then_inc(z_ready, 1)
            dve.wait_ge(exp_ready, 1)
            v.tensor_scalar(u, w, 1.0, None, ALU.add).then_inc(one_ready, 1)
            dve.wait_ge(ln_ready, 1)
            link(v.tensor_scalar(d_, u, -1.0, None, ALU.add))
            link(v.tensor_scalar(az, d_, 0.0, None, ALU.is_equal))
            link(v.tensor_tensor(d_, d_, az, ALU.add))
            link(v.tensor_tensor(lu, lu, az, ALU.add))
            link(v.reciprocal(u, d_))
            link(v.tensor_tensor(lu, lu, u, ALU.mult))
            link(v.tensor_tensor(lu, lu, w, ALU.mult))
            link(v.scalar_tensor_tensor(dta[:, 0, :], z, 0.0, lu, ALU.max, ALU.add))
            v.tensor_scalar(dta[:, 1, :], dta[:, 0, :], aneg[:, 0:1], -1.0, ALU.mult, ALU.mult).then_inc(dta_ready, 1)
            dve.wait_ge(dta_turned, 1)
            link(v.tensor_copy(P["dt"][:, :, :].rearrange("p q h -> p (q h)"), pt[:, 0, :]))
            link(v.tensor_copy(atok[:, :, :].rearrange("p q h -> p (q h)"), pt[:, 1, :]))
            for q in range(TT):
                if q >= 2:
                    dve.wait_ge(seg_ready, 8 * (q - 1))
                v.tensor_tensor(R[:, q % 2, :, :], atok[:, q, :].unsqueeze(2).to_broadcast([128, HEADS, S]),
                                upto[:, :].unsqueeze(1).to_broadcast([128, HEADS, S]), ALU.mult).then_inc(r_ready, 1)

        @block.tensor
        def _(pe):
            pe.wait_ge(w_in, 112)
            pe.wait_ge(hn_ready, 1)
            for d in range(DT):
                for t in range(TT):
                    last = nc.tensor.transpose(pt[:, d, t * 128:(t + 1) * 128], hn[:, t, d * 128:(d + 1) * 128],
                                               ident[:, :])
                last.then_inc(turned, 1)
            for d in range(DT):
                pe.wait_ge(hT_ready, d + 1)
                last = nc.tensor.matmul(pd[:, :], wdt[:, d, :], P["hT"][:, d, :], start=d == 0, stop=d == DT - 1)
            last.then_inc(dt_raw, 1)
            pe.wait_ge(dta_ready, 1)
            for i in range(2):
                for t in range(TT):
                    last = nc.tensor.transpose(pt[:, i, t * 128:(t + 1) * 128], dta[:, i, t * 128:(t + 1) * 128],
                                               ident[:, :])
            last.then_inc(dta_turned, 1)
            for n in range(TT * 8):
                q, c = n // 8, n % 8
                pe.wait_ge(r_ready, q + 1)
                if n >= 2:
                    pe.wait_ge(decay_ready, n - 1)
                nc.tensor.matmul(pz[:, n % 2, :], later[:, :],
                                 R[:, q % 2, 16 * c:16 * c + 16, :].rearrange("p h i -> p (h i)"),
                                 start=True, stop=True).then_inc(seg_ready, 1)


def conv_taps(v, dve, out, padded, par, tile, c_done, count):
    cw = [par[:, bass.ds(tile * 5 + i, 1)] for i in range(5)]
    v.tensor_scalar(out, padded[:, :, 0:S], cw[0], cw[4], ALU.mult, ALU.add).then_inc(c_done, 1)
    for i in range(1, TAPS):
        dve.wait_ge(c_done, count + i)
        v.scalar_tensor_tensor(out, padded[:, :, i:i + S], cw[i], out, ALU.mult, ALU.add).then_inc(c_done, 1)


def mamba_states(nc, io, scratch, P):
    with ExitStack() as ctx:
        def sb(name, shape, dt=F32):
            return ctx.enter_context(nc.sbuf_tensor(name, shape, dt))

        used = []

        def sem(name):
            used.append(ctx.enter_context(nc.semaphore(name)))
            return used[-1]

        NB = 2 * GR
        W = sb("W_s", [128, 2, DT, 128])
        XP = sb("XP_s", [128, 2, B, S + TAPS - 1])
        cv = sb("cv_s", [128, 2, B, S])
        BC = sb("BC", [128, 2 * GR, TOK])
        causal = sb("causal", [128, 128])
        pp = ctx.enter_context(nc.psum_tensor("pp_s", [128, 2, 512], F32))
        pc = ctx.enter_context(nc.psum_tensor("pc_s", [128, 2, 512], F32))
        c_in = sem("c_in_s")
        w_in = [sem("w_in_s0"), sem("w_in_s1")]
        zeroed = sem("zeroed_s")
        projected = sem("projected_s")
        padded = sem("padded_s")
        conved = sem("conved_s")
        silued = sem("silued_s")
        cb_ready = sem("cb_ready")
        cb_masked = sem("cb_masked")
        ctx.callback(clear, nc, used)
        block = ctx.enter_context(nc.Block())

        @block.sync
        def _(sp):
            sp.dma_start(causal[:, :], io["causal"]).then_inc(c_in, 16)

            def step(k, at):
                if at(0):
                    t, r = at(0)
                    sp.wait_ge(projected, t + 1)
                    sp.dma_start(W[:, k, :, :], io["in_proj"][bass.ds(t + 2 * CT_, 1), :, :, :]
                                 .rearrange("a p d o -> (a p) d o")).then_inc(w_in[k], 16)

            steps(sp, step, NB, 2)

        @block.tensor
        def _(pe):
            pe.sem_inc(projected, 2)

            def step(k, at):
                if at(0):
                    t, r = at(0)
                    pe.wait_ge(w_in[k], r * 16 + 16)
                    pe.wait_ge(padded, t + 1)
                    for d in range(DT):
                        last = nc.tensor.matmul(pp[:, k, :], W[:, k, d, :], P["hT"][:, d, :],
                                                start=d == 0, stop=d == DT - 1)
                    last.then_inc(projected, 1)

            steps(pe, step, NB, 2)
            pe.wait_ge(silued, NB + 2)
            for g in range(GR):
                if g >= 2:
                    pe.wait_ge(cb_masked, g - 1)
                for q in range(TT):
                    last = nc.tensor.matmul(pc[:, g % 2, q * 128:(q + 1) * 128], BC[:, g, q * 128:(q + 1) * 128],
                                            BC[:, GR + g, q * 128:(q + 1) * 128], start=True, stop=True)
                last.then_inc(cb_ready, 1)

        @block.scalar
        def _(act):
            act.wait_ge(zeroed, 1)
            act.sem_inc(padded, 2)
            act.sem_inc(silued, 2)

            def step(k, at):
                if at(0):
                    t, r = at(0)
                    act.wait_ge(projected, t + 3)
                    act.wait_ge(conved, t * TAPS + TAPS)
                    nc.scalar.activation(XP[:, k, :, TAPS - 1:], pp[:, k, :].rearrange("p (b s) -> p b s", b=B),
                                         ACT.Copy).then_inc(padded, 1)
                if at(1):
                    (t, r), k = at(1), 1 - k
                    act.wait_ge(conved, t * TAPS + 3 * TAPS)
                    nc.scalar.activation(BC[:, bass.ds(t, 1), :].rearrange("p a t -> p (a t)"),
                                         cv[:, k, :, :].rearrange("p b s -> p (b s)"), ACT.Silu).then_inc(silued, 1)

            steps(act, step, NB, 2)

        @block.vector
        def _(dve):
            v = nc.vector
            v.memset(XP[:, :, :, :], 0.0).then_inc(zeroed, 1)
            dve.sem_inc(conved, 2 * TAPS)

            def step(k, at):
                if at(0):
                    t, r = at(0)
                    dve.wait_ge(padded, t + 3)
                    dve.wait_ge(silued, t + 1)
                    conv_taps(v, dve, cv[:, k, :, :], XP[:, k, :, :], P["conv"], t + CT_, conved,
                              t * TAPS + 2 * TAPS)

            steps(dve, step, NB, 2)
            dve.wait_ge(c_in, 16)
            for g in range(GR):
                dve.wait_ge(cb_ready, g + 1)
                v.tensor_tensor(P["cb"][:, g, :, :], pc[:, g % 2, :].rearrange("p (q i) -> p q i", q=TT),
                                causal[:, :].unsqueeze(1).to_broadcast([128, TT, 128]), ALU.mult)\
                    .then_inc(cb_masked, 1)


def mamba_mix(nc, io, scratch, P):
    T, U = CT_, TPG
    with ExitStack() as ctx:
        def sb(name, shape, dt=F32):
            return ctx.enter_context(nc.sbuf_tensor(name, shape, dt))

        def ps(name, shape):
            return ctx.enter_context(nc.psum_tensor(name, shape, F32))

        used = []

        def sem(name):
            used.append(ctx.enter_context(nc.semaphore(name)))
            return used[-1]

        ident = sb("ident_m", [128, 128])
        ones = sb("ones_m", [128, 1])
        zero = sb("zero_m", [128, 1])
        chan = sb("chan", [128, 2, CT_])
        Wg = sb("Wg", [128, 2, DT, 128])
        Wh = sb("Wh", [128, 2, DT, 128])
        W16 = sb("W16", [128, 2, 4, 2, DT, 128], F16)
        h16 = sb("h16", [128, 2, DT, TOK], F16)
        Wo = sb("Wo", [128, 2, D])
        XP = sb("XP_m", [128, 2, B, S + TAPS - 1])
        cv = sb("cv_m", [128, 2, B, S])
        sg = sb("sg", [128, 4, TOK])
        hid = sb("hid", [128, 4, TOK])
        hc = sb("hc", [128, 2, TT, 2, HD])
        MT = sb("MT", [128, 2, 2, TT, 128])
        y = sb("y_m", [128, 2, TOK])
        yg = sb("yg", [128, 2, TOK])
        sq = sb("sq", [128, 2, TOK])
        sqsum = sb("sqsum", [128, 2, TOK])
        yw = sb("yw", [128, 2, 2, TOK], F16)
        Wo16 = sb("Wo16", [128, 2, 2, D], F16)
        rms = sb("rms", [128, 4, TT])
        pG = ps("pG", [128, 512])
        pX = ps("pX", [128, 512])
        pT = ps("pT", [128, 512])
        pY = ps("pY", [128, 512])
        pO = ps("pO", [128, 4, 512])

        const_in = sem("const_in_m")
        zeroed = sem("zeroed_m")
        g_in = [sem("g_in0"), sem("g_in1")]
        h_in = [sem("h_in0"), sem("h_in1")]
        o_in = [sem("o_in0"), sem("o_in1")]
        h_high = sem("h_high")
        h_split = sem("h_split")
        w_high = sem("w_high")
        w_split = sem("w_split")
        gate_mm = sem("gate_mm")
        hid_mm = sem("hid_mm")
        gate_silu = sem("gate_silu")
        padded = sem("padded_m")
        conved = sem("conved_m")
        hid_silu = sem("hid_silu")
        hid_turned = sem("hid_turned")
        hc_ready = sem("hc_ready")
        mt_ready = sem("mt_ready")
        mixed = sem("mixed_m")
        y_ready = sem("y_ready_m")
        yg_ready = sem("yg_ready")
        sq_ready = sem("sq_ready")
        sq_summed = sem("sq_summed")
        yw_high = sem("yw_high")
        yw_ready = sem("yw_ready")
        wo_high = sem("wo_high")
        wo_split = sem("wo_split")
        out_mm = sem("out_mm")
        ssq_mm = sem("ssq_mm")
        ssq_read = sem("ssq_read")
        rms_var = sem("rms_var")
        rms_root = sem("rms_root")
        rms_link = sem("rms_link")
        rms_done = sem("rms_done")
        folded = sem("folded_m")
        ctx.callback(clear, nc, used)
        block = ctx.enter_context(nc.Block())

        def after_split(inner):
            return lambda k, at: inner((k - 2) % U, lambda lag: at(lag + 2))

        def loads(k, r):
            return r * (16 * U // 2) + 16 * (k // 2 + 1)

        @block.sync
        def _(sp):
            sp.dma_start(ident[:, :], io["ident"]).then_inc(const_in, 16)
            sp.dma_start(chan[:, :, :], io["chan"]).then_inc(const_in, 16)

            def step(k, at):
                if at(0):
                    t, r = at(0)
                    sp.wait_ge(w_split, t * 2 + 2)
                    sp.dma_start(Wg[:, k % 2, :, :], io["in_proj"][bass.ds(t, 1), :, :, :]
                                 .rearrange("a p d o -> (a p) d o")).then_inc(g_in[k % 2], 16)
                    sp.dma_start(Wh[:, k % 2, :, :], io["in_proj"][bass.ds(t + CT_, 1), :, :, :]
                                 .rearrange("a p d o -> (a p) d o")).then_inc(h_in[k % 2], 16)
                if at(4):
                    (t, _), k3 = at(4), (k - 4) % U
                    sp.wait_ge(wo_split, t + 1)
                    sp.dma_start(Wo[:, k3 % 2, :], io["out_proj"][bass.ds(t, 1), :, :]
                                 .rearrange("a p o -> (a p) o")).then_inc(o_in[k3 % 2], 16)

            steps(sp, step, T, U)

        @block.tensor
        def _(pe):
            pe.sem_inc(gate_mm, 4)
            pe.sem_inc(hid_mm, 4)
            pe.sem_inc(mixed, 2)
            pe.sem_inc(out_mm, 2)
            pe.wait_ge(const_in, 32)
            pe.wait_ge(h_split, DT)

            def project(out, i, quarter):
                for d in range(DT):
                    for a, b in ((0, 0), (0, 1), (1, 0)):
                        last = nc.tensor.matmul(out, W16[:, i, quarter, a, d, :], h16[:, b, d, :],
                                                start=d + a + b == 0, stop=d == DT - 1 and a == 1)
                return last

            def step(k, at):
                if at(0):
                    t, r = at(0)
                    pe.wait_ge(w_split, t * 2 + 5)
                    pe.wait_ge(gate_silu, t + 1)
                    project(pG[:, :], 0, k % 4).then_inc(gate_mm, 1)
                if at(4):
                    (t, r), k4 = at(4), (k - 4) % U
                    pe.wait_ge(wo_split, t + 3)
                    pe.wait_ge(yw_ready, t + 3)
                    if k4 == 0:
                        pe.wait_ge(folded, r * 4 + 4)
                    for q in range(TT):
                        for a, b in ((0, 0), (0, 1), (1, 0)):
                            last = nc.tensor.matmul(pO[:, q, :], yw[:, k4 % 2, a, q * 128:(q + 1) * 128],
                                                    Wo16[:, k4 % 2, b, :], start=k4 + a + b == 0,
                                                    stop=k4 == U - 1 and a == 1)
                    last.then_inc(out_mm, 1)
                    if k4 == U - 1:
                        pe.wait_ge(hc_ready, (at(2) or (T - 1, 0))[0] + 2)
                        pe.wait_ge(sq_summed, t + 3)
                        for q in range(TT):
                            last = nc.tensor.matmul(pT[:, q:q + 1], sqsum[:, (U - 1) % 2, q * 128:(q + 1) * 128],
                                                    ones[:, :], start=True, stop=True)
                        last.then_inc(ssq_mm, 1)
                if at(1):
                    (t, r), k1 = at(1), (k - 1) % U
                    pe.wait_ge(hid_silu, t + 3)
                    pe.wait_ge(hc_ready, t + 1)
                    if k1 == 2 and not (isinstance(r, int) and r == 0):
                        pe.wait_ge(ssq_read, r + 1)
                    for q in range(TT):
                        last = nc.tensor.transpose(pT[:, q * 128:(q + 1) * 128], hid[:, k1 % 4, q * 128:(q + 1) * 128],
                                                   ident[:, :])
                    last.then_inc(hid_turned, 1)
                if at(0):
                    t, r = at(0)
                    pe.wait_ge(w_split, t * 2 + 6)
                    pe.wait_ge(padded, t + 1)
                    project(pX[:, :], 1, k % 4).then_inc(hid_mm, 1)
                if at(2):
                    (t, r), k2 = at(2), (k - 2) % U
                    pe.wait_ge(hc_ready, t + 2)
                    pe.wait_ge(mt_ready, t * 2 + 6)
                    pe.wait_ge(y_ready, t + 1)
                    for h in range(2):
                        for q in range(TT):
                            last = nc.tensor.matmul(pY[HD * h:HD * h + HD, q * 128:(q + 1) * 128],
                                                    hc[:, k2 % 2, q, h, :], MT[:, k2 % 2, h, q, :],
                                                    start=True, stop=True)
                    last.then_inc(mixed, 1)

            steps(pe, after_split(step), T, U)

        @block.scalar
        def _(act):
            act.wait_ge(zeroed, 4)
            act.sem_inc(gate_silu, 1)
            act.sem_inc(padded, 1)
            act.sem_inc(hid_silu, 2)
            act.sem_inc(sq_ready, 2)
            act.sem_inc(yw_high, 2)
            act.wait_ge(const_in, 32)
            for d in range(DT):
                nc.scalar.activation(h16[:, 0, d, :], P["hT"][:, d, :], ACT.Copy).then_inc(h_high, 1)

            def step(k, at):
                if at(0):
                    t, r = at(0)
                    act.wait_ge(gate_mm, t + 5)
                    act.wait_ge(yg_ready, t + 1)
                    nc.scalar.activation(sg[:, k % 4, :], pG[:, :], ACT.Silu, scale=2.0 ** -10).then_inc(gate_silu, 1)
                if at(3):
                    (t, r), k3 = at(3), (k - 3) % U
                    act.wait_ge(out_mm, t + 1)
                    act.wait_ge(o_in[k3 % 2], loads(k3, r))
                    nc.scalar.activation(Wo16[:, k3 % 2, 0, :], Wo[:, k3 % 2, :], ACT.Copy,
                                         scale=2.0 ** 10).then_inc(wo_high, 1)
                    act.wait_ge(yg_ready, t + 5)
                    nc.scalar.activation(yw[:, k3 % 2, 0, :], yg[:, k3 % 2, :], ACT.Copy,
                                         scale=chan[:, 1, bass.ds(t, 1)]).then_inc(yw_high, 1)
                    act.wait_ge(sq_summed, t + 1)
                    nc.scalar.activation(sq[:, k3 % 2, :], yg[:, k3 % 2, :], ACT.Square).then_inc(sq_ready, 1)
                if at(4) and (k - 4) % U == U - 1:
                    t, r = at(4)
                    act.wait_ge(rms_var, r + 1)
                    nc.scalar.activation(rms[:, 1, :], rms[:, 0, :], ACT.Sqrt).then_inc(rms_root, 1)
                if at(0):
                    t, r = at(0)
                    act.wait_ge(hid_mm, t + 5)
                    act.wait_ge(conved, t * TAPS + TAPS)
                    nc.scalar.activation(XP[:, k % 2, :, TAPS - 1:], pX[:, :].rearrange("p (b s) -> p b s", b=B),
                                         ACT.Copy, scale=2.0 ** -10).then_inc(padded, 1)
                    act.wait_ge(conved, t * TAPS + 3 * TAPS)
                    act.wait_ge(yg_ready, t + 1)
                    nc.scalar.activation(hid[:, k % 4, :], cv[:, k % 2, :, :].rearrange("p b s -> p (b s)"),
                                         ACT.Silu).then_inc(hid_silu, 1)

            def split_step(k, at):
                if at(0):
                    t, r = at(0)
                    for i, raw, raw_in, used_mm in ((0, Wg, g_in, gate_mm), (1, Wh, h_in, hid_mm)):
                        act.wait_ge(raw_in[k % 2], loads(k, r))
                        act.wait_ge(used_mm, t + 1)
                        nc.scalar.activation(W16[:, i, k % 4, 0, :, :], raw[:, k % 2, :, :], ACT.Copy,
                                             scale=2.0 ** 10).then_inc(w_high, 1)
                after_split(step)(k, at)

            steps(act, split_step, T, U)

        @block.vector
        def _(dve):
            v = nc.vector
            v.memset(XP[:, :, :, :], 0.0).then_inc(zeroed, 1)
            v.memset(ones[:, :], 1.0).then_inc(zeroed, 1)
            v.memset(zero[:, :], 0.0).then_inc(zeroed, 1)
            dve.sem_inc(conved, 2 * TAPS)
            dve.sem_inc(hc_ready, 1)
            dve.sem_inc(y_ready, 1)
            dve.sem_inc(yg_ready, 4)
            dve.sem_inc(ssq_read, 1)
            dve.sem_inc(folded, 4)
            dve.sem_inc(w_split, 4)
            dve.sem_inc(wo_split, 2)
            dve.sem_inc(yw_ready, 2)
            dve.wait_ge(const_in, 32)
            v.tensor_scalar(chan[:, 1, :], chan[:, 1, :], 4.0, None, ALU.mult).then_inc(zeroed, 1)
            dve.wait_ge(zeroed, 4)
            for d in range(DT):
                dve.wait_ge(h_high, d + 1)
                v.tensor_tensor(h16[:, 1, d, :], P["hT"][:, d, :], h16[:, 0, d, :], ALU.subtract).then_inc(h_split, 1)

            def step(k, at):
                if at(3):
                    (t, r), k3 = at(3), (k - 3) % U
                    dve.wait_ge(mixed, t + 3)
                    dve.wait_ge(hid_silu, t + 3)
                    v.scalar_tensor_tensor(y[:, k3 % 2, :], hid[:, k3 % 4, :], chan[:, 0, bass.ds(t, 1)], pY[:, :],
                                           ALU.mult, ALU.add).then_inc(y_ready, 1)
                    dve.wait_ge(y_ready, t + 2)
                    dve.wait_ge(gate_silu, t + 2)
                    dve.wait_ge(sq_ready, t + 1)
                    dve.wait_ge(yw_ready, t + 1)
                    v.tensor_tensor(yg[:, k3 % 2, :], y[:, k3 % 2, :], sg[:, k3 % 4, :], ALU.mult).then_inc(yg_ready, 1)
                if at(4) and (k - 4) % U == U - 1:
                    t, r = at(4)
                    dve.wait_ge(ssq_mm, r + 1)
                    v.tensor_scalar(rms[:, 0, :], pT[:, 0:TT], 1.0 / (INNER // GR), EPS, ALU.mult, ALU.add)\
                        .then_inc(ssq_read, 1)
                    dve.wait_ge(ssq_read, r + 2)
                    v.tensor_copy(rms[:, 3, :], rms[:, 0, :]).then_inc(rms_var, 1)
                    dve.wait_ge(rms_root, r + 1)
                    base = r * 4
                    rr, tm = rms[:, 2, :], rms[:, 3, :]
                    v.reciprocal(rr, rms[:, 1, :]).then_inc(rms_link, 1)
                    dve.wait_ge(rms_link, base + 1)
                    v.tensor_tensor(tm, rr, rr, ALU.mult).then_inc(rms_link, 1)
                    dve.wait_ge(rms_link, base + 2)
                    v.tensor_tensor(tm, tm, rms[:, 0, :], ALU.mult).then_inc(rms_link, 1)
                    dve.wait_ge(rms_link, base + 3)
                    v.tensor_scalar(tm, tm, -0.5, 1.5, ALU.mult, ALU.add).then_inc(rms_link, 1)
                    dve.wait_ge(rms_link, base + 4)
                    v.scalar_tensor_tensor(rr, rr, 2.0 ** -12, tm, ALU.mult, ALU.mult).then_inc(rms_done, 1)
                    dve.wait_ge(rms_done, r + 1)
                    dve.wait_ge(out_mm, t + 3)
                    for q in range(TT):
                        v.scalar_tensor_tensor(P["acc"][:, q, :], pO[:, q, :], rms[:, 2, q:q + 1], P["acc"][:, q, :],
                                               ALU.mult, ALU.add).then_inc(folded, 1)
                if at(1):
                    (t, r), k1 = at(1), (k - 1) % U
                    dve.wait_ge(hid_turned, t + 1)
                    dve.wait_ge(mixed, t + 1)
                    v.tensor_tensor(hc[:, k1 % 2, :, :, :],
                                    pT[:, :].rearrange("p (q h x) -> p q h x", q=TT, h=2),
                                    P["dt"][:, :, bass.ds(t * 2, 2)].unsqueeze(3).to_broadcast([128, TT, 2, HD]),
                                    ALU.mult).then_inc(hc_ready, 1)
                if at(3):
                    (t, r), k3 = at(3), (k - 3) % U
                    dve.wait_ge(yw_high, t + 3)
                    v.scalar_tensor_tensor(yw[:, k3 % 2, 1, :], yg[:, k3 % 2, :], chan[:, 1, bass.ds(t, 1)],
                                           yw[:, k3 % 2, 0, :], ALU.mult, ALU.subtract).then_inc(yw_ready, 1)
                    dve.wait_ge(wo_high, t + 1)
                    v.scalar_tensor_tensor(Wo16[:, k3 % 2, 1, :], Wo[:, k3 % 2, :], 2.0 ** 10,
                                           Wo16[:, k3 % 2, 0, :], ALU.mult, ALU.subtract).then_inc(wo_split, 1)
                if at(0):
                    t, r = at(0)
                    dve.wait_ge(padded, t + 2)
                    dve.wait_ge(hid_silu, t + 1)
                    conv_taps(v, dve, cv[:, k % 2, :, :], XP[:, k % 2, :, :], P["conv"], t, conved,
                              t * TAPS + 2 * TAPS)

            def split_step(k, at):
                if at(1):
                    (t, _), k1 = at(1), (k - 1) % U
                    for i, raw in ((0, Wg), (1, Wh)):
                        dve.wait_ge(w_high, t * 2 + i + 1)
                        v.scalar_tensor_tensor(W16[:, i, k1 % 4, 1, :, :], raw[:, k1 % 2, :, :], 2.0 ** 10,
                                               W16[:, i, k1 % 4, 0, :, :], ALU.mult, ALU.subtract).then_inc(w_split, 1)
                after_split(step)(k, at)

            steps(dve, split_step, T, U)

        @block.gpsimd
        def _(pool):
            pool.wait_ge(zeroed, 3)
            pool.sem_inc(mt_ready, 4)
            pool.sem_inc(sq_summed, 2)

            def step(k, at):
                if at(1):
                    (t, r), k1 = at(1), (k - 1) % U
                    pool.wait_ge(mixed, t + 1)
                    for h in range(2):
                        nc.gpsimd.tensor_tensor(
                            MT[:, k1 % 2, h, :, :].rearrange("p q (b i) -> p q b i", b=4),
                            P["cb"][:, bass.ds(r, 1), :, :].rearrange("p g q (b i) -> p (g q) b i", b=4),
                            P["decay"][:, :, bass.ds(t * 2 + h, 1), :].to_broadcast([128, TT, 4, S]),
                            ALU.mult).then_inc(mt_ready, 1)
                if at(3):
                    (t, r), k3 = at(3), (k - 3) % U
                    pool.wait_ge(sq_ready, t + 3)
                    if k3 == 0:
                        if not (isinstance(r, int) and r == 0):
                            pool.wait_ge(ssq_mm, r)
                        nc.gpsimd.tensor_tensor(sqsum[:, 0, :], sq[:, 0, :], zero[:, :].to_broadcast([128, TOK]),
                                                ALU.add).then_inc(sq_summed, 1)
                    else:
                        pool.wait_ge(sq_summed, t + 2)
                        nc.gpsimd.tensor_tensor(sqsum[:, k3 % 2, :], sqsum[:, 1 - k3 % 2, :], sq[:, k3 % 2, :],
                                                ALU.add).then_inc(sq_summed, 1)

            steps(pool, after_split(step), T, U)


def feed_forward(nc, io, scratch, P, out):
    with ExitStack() as ctx:
        def sb(name, shape, dt=F32):
            return ctx.enter_context(nc.sbuf_tensor(name, shape, dt))

        used = []

        def sem(name):
            used.append(ctx.enter_context(nc.semaphore(name)))
            return used[-1]

        ident = sb("ident_f", [128, 128])
        w1 = sb("w1_f", [128, FFH])
        w3 = sb("w3_f", [128, FFH])
        w2 = sb("w2_f", [FP, FR, D])
        a13 = sb("a13", [128, 2, DT, 2])
        b1 = sb("b1_f", [2, FFH])
        b3 = sb("b3_f", [2, FFH])
        a2 = sb("a2_f", [FP, 4 * FR, 2])
        b2 = sb("b2_f", [2, D])
        x2 = P["acc"]
        xn = sb("xn_f", [128, TT, D])
        st = sb("st_f", [128, TT, 6])
        mv = sb("mv_f", [128, TT, 2])
        tmp = sb("tmp_f", [128, 3, TT])
        xT = sb("xT_f", [128, DT, TOK])
        xf = sb("xf_f", [128, TOK])
        la = sb("la_f", [2, 2, TOK])
        la2 = sb("la2_f", [2, TOK])
        sg = sb("sg_f", [FP, 2, TOK])
        u = sb("u_f", [FP, 2, TOK])
        uf = sb("uf_f", [FP, FR, TOK])
        res = sb("res_f", [128, TT, D])
        pt = ctx.enter_context(nc.psum_tensor("pt_f", [128, 2, 512], F32))
        pl = ctx.enter_context(nc.psum_tensor("pl_f", [128, 512], F32))
        pg = ctx.enter_context(nc.psum_tensor("pg_f", [128, 2, 512], F32))
        pu = ctx.enter_context(nc.psum_tensor("pu_f", [128, 2, 512], F32))
        w_in = sem("w_in_f")
        var_ready = sem("var_ready_f")
        root_ready = sem("root_ready_f")
        xn_ready = sem("xn_ready_f")
        turned = sem("turned_f")
        xT_ready = sem("xT_ready_f")
        xf_ready = sem("xf_ready_f")
        la_mm = sem("la_mm")
        la_ready = sem("la_ready")
        gu_mm = sem("gu_mm")
        silued = sem("silued_f")
        u_ready = sem("u_ready_f")
        uf_ready = sem("uf_ready_f")
        la2_mm = sem("la2_mm")
        la2_ready = sem("la2_ready")
        out_mm = sem("out_mm_f")
        res_ready = sem("res_ready_f")
        stored = sem("stored_f")
        v_chain = sem("v_chain_f")
        HT = 4 * FR
        ctx.callback(clear, nc, used)
        block = ctx.enter_context(nc.Block())

        @block.sync
        def _(sp):
            loads = ((ident, "ident"), (w1, "w1"), (w3, "w3"), (w2, "w2"), (a13, "a13"), (b1, "b1"), (b3, "b3"),
                     (a2, "a2"), (b2, "b2"))
            for dst, src in loads:
                dst = dst[tuple(slice(None) for _ in dst.shape)]
                sp.dma_start(dst, io[src]).then_inc(w_in, 16)
            for q in range(TT):
                sp.wait_ge(res_ready, q + 1)
                sp.dma_start(out.rearrange("b s d -> (b s) d")[q * 128:(q + 1) * 128, :], res[:, q, :])\
                    .then_inc(stored, 16)
            sp.wait_ge(stored, 16 * TT)

        @block.scalar
        def _(act):
            act.wait_ge(var_ready, 1)
            nc.scalar.activation(tmp[:, 0, :], mv[:, :, 1], ACT.Sqrt).then_inc(root_ready, 1)
            for n in range(HT):
                act.wait_ge(gu_mm, n + 1)
                if n >= 2:
                    act.wait_ge(u_ready, n - 1)
                nc.scalar.activation(sg[:, n % 2, :], pg[0:FP, n % 2, :], ACT.Silu).then_inc(silued, 1)

        @block.vector
        def _(dve):
            v = nc.vector
            link = chain(dve, v_chain)

            def act_sqrt(ins):
                ins.then_inc(var_ready, 1)
                dve.wait_ge(root_ready, 1)

            row_norm(nc, v, link, act_sqrt, x2, xn, st, mv, tmp)
            dve.sem_inc(xn_ready, 1)
            for d in range(DT):
                dve.wait_ge(turned, d + 1)
                v.tensor_copy(xT[:, d, :], pt[:, d % 2, :]).then_inc(xT_ready, 1)
            dve.wait_ge(xT_ready, DT)
            link(v.tensor_tensor(xf[:, :], xT[:, 0, :], xT[:, 1, :], ALU.add))
            link(v.tensor_tensor(xf[:, :], xf[:, :], xT[:, 2, :], ALU.add))
            v.tensor_tensor(xf[:, :], xf[:, :], xT[:, 3, :], ALU.add).then_inc(xf_ready, 1)
            for i in range(2):
                dve.wait_ge(la_mm, i + 1)
                v.tensor_scalar(la[:, i, :], pt[0:2, i, :], 0.5, None, ALU.mult).then_inc(la_ready, 1)
            for n in range(HT):
                r, k = n // 4, n % 4
                dve.wait_ge(silued, n + 1)
                if n >= 2:
                    dve.wait_ge(la2_mm, n - 1)
                v.tensor_tensor(u[:, n % 2, :], sg[:, n % 2, :], pu[0:FP, n % 2, :], ALU.mult).then_inc(u_ready, 1)
                dve.wait_ge(u_ready, n + 1)
                if k == 0:
                    v.tensor_copy(uf[:, r, :], u[:, n % 2, :]).then_inc(uf_ready, 1)
                else:
                    dve.wait_ge(uf_ready, n)
                    v.tensor_tensor(uf[:, r, :], uf[:, r, :], u[:, n % 2, :], ALU.add).then_inc(uf_ready, 1)
            dve.wait_ge(la2_mm, HT)
            v.tensor_scalar(la2[:, :], pl[0:2, :], 0.5, None, ALU.mult).then_inc(la2_ready, 1)
            for q in range(TT):
                dve.wait_ge(out_mm, q + 1)
                v.tensor_tensor(res[:, q, :], x2[:, q, :], (pg if q < 2 else pu)[:, q % 2, :], ALU.add)\
                    .then_inc(res_ready, 1)

        @block.tensor
        def _(pe):
            pe.wait_ge(w_in, 16 * 9)
            pe.wait_ge(xn_ready, 1)
            for d in range(DT):
                if d >= 2:
                    pe.wait_ge(xT_ready, d - 1)
                for t in range(TT):
                    last = nc.tensor.transpose(pt[:, d % 2, t * 128:(t + 1) * 128], xn[:, t, d * 128:(d + 1) * 128],
                                               ident[:, :])
                last.then_inc(turned, 1)
            pe.wait_ge(xT_ready, DT)
            for i in range(2):
                for d in range(DT):
                    last = nc.tensor.matmul(pt[0:2, i, :], a13[:, i, d, :], xT[:, d, :], start=d == 0, stop=d == DT - 1)
                last.then_inc(la_mm, 1)
            pe.wait_ge(xf_ready, 1)
            pe.wait_ge(la_ready, 2)

            def low_rank(n):
                pe.wait_ge(u_ready, n + 1)
                nc.tensor.matmul(pl[0:2, :], a2[:, (n % 4) * FR + n // 4, :], u[:, n % 2, :],
                                 start=n == 0, stop=n == HT - 1).then_inc(la2_mm, 1)

            for n in range(HT):
                c = ((n % 4) * FR + n // 4) * FP
                if n >= 2:
                    pe.wait_ge(u_ready, n - 1)
                for p_, w_, b_, i in ((pg, w1, b1, 0), (pu, w3, b3, 1)):
                    nc.tensor.matmul(p_[0:FP, n % 2, :], w_[:, c:c + FP], xf[:, :], start=True, stop=False)
                    last = nc.tensor.matmul(p_[0:FP, n % 2, :], b_[:, c:c + FP], la[:, i, :], start=False, stop=True)
                last.then_inc(gu_mm, 1)
                if n >= 1:
                    low_rank(n - 1)
            low_rank(HT - 1)
            pe.wait_ge(uf_ready, HT)
            pe.wait_ge(la2_ready, 1)
            for q in range(TT):
                po = (pg if q < 2 else pu)[:, q % 2, :]
                for r in range(FR):
                    nc.tensor.matmul(po, uf[:, r, q * 128:(q + 1) * 128], w2[:, r, :], start=r == 0, stop=False)
                nc.tensor.matmul(po, la2[:, q * 128:(q + 1) * 128], b2[:, :], start=False, stop=True).then_inc(out_mm, 1)


def program(nc, io, scratch, out):
    cross_attention(nc, io, scratch)
    with ExitStack() as ctx:
        def sb(name, shape):
            return ctx.enter_context(nc.sbuf_tensor(name, shape, F32))

        P = {"acc": sb("acc", [128, TT, D])}
        with ExitStack() as mctx:
            def msb(name, shape):
                return mctx.enter_context(nc.sbuf_tensor(name, shape, F32))

            P["hT"] = msb("hT", [128, DT, TOK])
            P["dt"] = msb("dt_tok", [128, TT, HEADS])
            P["decay"] = msb("decay", [128, TT, HEADS, S])
            P["cb"] = msb("cb", [128, GR, TT, 128])
            P["conv"] = msb("conv", [128, (CT_ + 2 * GR) * 5])
            mamba_prepare(nc, io, scratch, P)
            mamba_states(nc, io, scratch, P)
            mamba_mix(nc, io, scratch, P)
        feed_forward(nc, io, scratch, P, out)


def constants():
    import numpy as np
    c = {}
    c["idx"] = ((np.arange(B * N) % N).reshape(128, -1) / 1024.0).astype(np.float32)
    c["ident"] = np.eye(128, dtype=np.float32)
    c["rep"] = np.repeat(np.eye(C, dtype=np.float32), M, axis=1)
    e = np.arange(EXT)
    lead = np.minimum(e % K, e // K + LEAD)
    place = np.where(e < LEAD * K, lead, np.minimum(e - LEAD * K, N - 1))
    c["place"] = np.tile(place.astype(np.float16), (128, 1))
    x = np.arange(32)
    batch, tok = np.arange(128) // S, np.arange(128)
    same = batch[:, None] == batch[None, :]
    c["later"] = (same & (tok[:, None] > tok[None, :])).astype(np.float32)
    c["upto"] = ((tok % S)[:, None] <= np.arange(S)[None, :]).astype(np.float32)
    c["causal"] = (same & (tok[:, None] <= tok[None, :])).astype(np.float32)
    for layer, O in (("1", C), ("2", 2 * C)):
        c["merge" + layer] = (tok[:, None] % O == tok[None, :] % O).astype(np.float32)
    c["maskL"] = np.array([[1024.0 * (i % 32 // K == n) for i in range(128)] for n in range(PTS)], np.float16)
    c["maskR"] = np.tile(np.array([-1024.0 * (x // K != n) for n in range(PTS)], np.float16), (1, SUBS))
    return c


def kernel(**inputs):
    import numpy as np
    import concourse.bacc as bacc
    from concourse.bass_utils import run_bass_kernel_spmd as run

    nc = bacc.Bacc("TRN2", target_bir_lowering=False, num_devices=1)
    a = {k: np.asarray(v) for k, v in inputs.items()}
    arrays = {
        "x": a["x"].reshape(B * S, D),
        "coords": a["ctx_4096"][:, :3, :].transpose(1, 0, 2).reshape(3 * B, N),
    }
    for n in "12":
        arrays["lin" + n] = a["L0_xattn_W_lin" + n]
        arrays["blin" + n] = a["L0_xattn_b_lin" + n].reshape(-1, 1)
        convT = a["L0_xattn_W_conv" + n].T
        arrays["convT" + n] = np.tile(convT, (1, 128 // convT.shape[1]))
    arrays["conv3T"] = a["L0_xattn_W_conv3"].T
    w = a["L0_attn_in_proj_w"]
    arrays["in_proj"] = w.reshape(-1, 128, DT, 128).transpose(0, 3, 2, 1)
    arrays["out_proj"] = a["L0_attn_out_proj_w"].T.reshape(CT_, 128, D)
    arrays["norm_w"] = a["L0_attn_norm_w"].reshape(DT, 128).T
    arrays["head_par"] = np.stack([a["L0_attn_dt_bias"], a["L0_attn_A_log"]], 1)
    taps = np.concatenate([a["L0_attn_conv_w"], a["L0_attn_conv_b"][:, None]], 1)
    arrays["conv"] = taps.reshape(-1, 128, TAPS + 1).transpose(1, 0, 2).reshape(128, -1)
    arrays["chan"] = np.stack([np.repeat(a["L0_attn_Dp"], HD).reshape(CT_, 128).T,
                               a["L0_attn_gnorm_w"].reshape(CT_, 128).T], 1)
    arrays["w1"], arrays["w3"] = a["L0_ffn_w1q"].T, a["L0_ffn_w3q"].T
    arrays["w2"] = a["L0_ffn_w2q"].T.reshape(FR, FP, D).transpose(1, 0, 2)
    arrays["a13"] = np.stack([a["L0_ffn_a1"], a["L0_ffn_a3"]]).reshape(2, 2, DT, 128).transpose(3, 0, 2, 1)
    arrays["b1"], arrays["b3"], arrays["b2"] = a["L0_ffn_b1"].T, a["L0_ffn_b3"].T, a["L0_ffn_b2"].T
    arrays["a2"] = a["L0_ffn_a2"].reshape(2, 4 * FR, FP).transpose(2, 1, 0)
    arrays.update(constants())
    arrays = {k: np.ascontiguousarray(v) for k, v in arrays.items()}
    io = {k: nc.dram_tensor("in_" + k, v.shape, mybir.dt.from_np(v.dtype), kind="ExternalInput").ap()
          for k, v in arrays.items()}
    out = nc.dram_tensor("out_0_dram", (B, S, D), F32, kind="ExternalOutput").ap()

    def dram(name, shape, dt=F32):
        return nc.dram_tensor("scratch_" + name, shape, dt).ap()

    scratch = {"q": dram("q", (48, N), I32), "f0": dram("f0", (B * C, N)),
               "hi": dram("hi", (M, B, N)), "lo": dram("lo", (M, B, N))}
    scratch.update({"q16": dram("q16", (B * GROUPS, 128, GC), F16), "c16": dram("c16", (B * GROUPS, 128, GP), F16),
                    "f1": dram("f1", (C, B, PADN)), "f2": dram("f2", (2 * C, B, PADN)), "x1": dram("x1", (B * S, D))})
    program(nc, io, scratch, out)
    r = run(nc, [{"in_" + k: v for k, v in arrays.items()}], core_ids=[0])
    return r.results[0]["out_0_dram"]
```
